# Optimizing a Trainium2 kernel written in Bass

```python
import numpy as np
import jax
import jax.numpy as jnp

def _softmax(x, axis=-1):
    return jax.nn.softmax(x, axis=axis)

def _gelu(x):
    return jax.nn.gelu(x, approximate=True)

def _silu(x):
    return jax.nn.silu(x)

def _sigmoid(x):
    return jax.nn.sigmoid(x)

def _layernorm(x, axis=-1, eps=1e-05):
    m = jnp.mean(x, axis=axis, keepdims=True)
    v = jnp.var(x, axis=axis, keepdims=True)
    return (x - m) / jnp.sqrt(v + eps)

def _scatter_add(tgt, idx, src, axis=0):
    return tgt.at[idx].add(src)

def _segment_sum(src, seg, n):
    return jax.ops.segment_sum(src, seg, n)
kernel_name = 'mk_xattn_ffn_d2_seqx_r4_963825'

def setup_inputs(seed: int=0):
    np.random.seed(seed)
    _w = jnp.asarray

    def _rec_inputs():
        import jax
        import jax.numpy as jnp
        _rk = jax.random.key(seed)
        x = -0.0002928 + 1 * jax.random.normal(jax.random.fold_in(_rk, 1), (4, 512, 256), jnp.float32)
        _lenS = 512 - jax.random.randint(jax.random.fold_in(_rk, 7), (4,), 0, max(1, 512 // 4) + 1, jnp.int32)
        _lenS2 = 512 - jax.random.randint(jax.random.fold_in(_rk, 8), (4,), 0, max(1, 512 // 4) + 1, jnp.int32)
        _ctx_1024P = jax.random.normal(jax.random.fold_in(_rk, 11), (4, 16, 256), jnp.float32)
        _ctx_1024c = jax.random.dirichlet(jax.random.fold_in(_rk, 511), 0.3 * jnp.ones((16,), jnp.float32), (4, 512))
        _ctx_1024t = jnp.einsum('bsk,bkd->bsd', _ctx_1024c, _ctx_1024P)
        _ctx_1024t = _ctx_1024t * jax.lax.rsqrt(jnp.mean(jnp.square(_ctx_1024t)) + 1e-12) * 0.953939
        ctx_1024 = -1.39393e-06 + 0.999914 * (_ctx_1024t + 0.3 * jax.random.normal(jax.random.fold_in(_rk, 611), (4, 512, 256), jnp.float32))
        _validS = jnp.arange(512)[None, :] < _lenS[:, None]
        _validS2 = jnp.arange(512)[None, :] < _lenS2[:, None]
        _causal = jnp.tril(jnp.ones((512, 512), dtype=bool))
        mask_Bx1x1xS2_ff0 = jnp.where(jnp.ones((4, 1, 1, 512), dtype=bool), 0.0, -1000000000.0).astype(jnp.float32)
        mask_1x1xSxS2_fk0 = jnp.where(jnp.broadcast_to(_validS2[0:1, None, None, :], (1, 1, 512, 512)), -1000000000.0, 0.0).astype(jnp.float32)
        return (x, ctx_1024, mask_Bx1x1xS2_ff0, mask_1x1xSxS2_fk0)
    x, ctx_1024, mask_Bx1x1xS2_ff0, mask_1x1xSxS2_fk0 = _rec_inputs()

    def _L0_xattn_setup():
        import jax, jax.numpy as jnp
        import numpy as np
        D_MODEL = 256
        key = jax.random.key(seed)
        ks = jax.random.split(key, 8)
        B, S, D = (2, 512, D_MODEL)
        s = 1.0 / np.sqrt(D)
        causal = jnp.where(jnp.tril(jnp.ones((S, S), dtype=bool)), 0.0, -1000000000.0)[None, None]
        return {'query': jax.random.normal(ks[0], (B, S, D), jnp.float32), 'key': jax.random.normal(ks[1], (B, S, D), jnp.float32), 'value': jax.random.normal(ks[2], (B, S, D), jnp.float32), 'padding_mask': jnp.zeros((B, 1, 1, S), jnp.float32), 'lookahead_mask': causal.astype(jnp.float32), 'w_q': jax.random.normal(ks[3], (D, D), jnp.float32) * s, 'w_k': jax.random.normal(ks[4], (D, D), jnp.float32) * s, 'w_v': jax.random.normal(ks[5], (D, D), jnp.float32) * s, 'w_out': jax.random.normal(ks[6], (D, D), jnp.float32) * s, 'b_q': jnp.zeros((D,), jnp.float32), 'b_k': jnp.zeros((D,), jnp.float32), 'b_v': jnp.zeros((D,), jnp.float32), 'b_out': jnp.zeros((D,), jnp.float32), 'n_heads': 16}
    _L0_xattn_all = _L0_xattn_setup()
    _L0_xattn_in = {k: v for k, v in _L0_xattn_all.items() if k in ('w_q', 'w_k', 'w_v', 'w_out', 'b_q', 'b_k', 'b_v', 'b_out')}
    del _L0_xattn_all

    def _L0_ffn_setup():
        import jax, jax.numpy as jnp
        import numpy as np
        S, B, H = (512, 4, 256)
        E = 64
        K = 4
        I = 128
        CAP = 256
        key = jax.random.key(seed)
        k1, k2, k3, k4 = jax.random.split(key, 4)
        return {'hidden_states': jax.random.normal(k1, (S, B, H), dtype=jnp.float32), 'router_w': jax.random.normal(k2, (H, E), dtype=jnp.float32) * 0.02, 'w1': jax.random.normal(k3, (E, H, 2 * I), dtype=jnp.float32) * 0.02, 'w2': jax.random.normal(k4, (E, I, H), dtype=jnp.float32) * 0.02}
    _L0_ffn_all = _L0_ffn_setup()
    _L0_ffn_in = {k: v for k, v in _L0_ffn_all.items() if k in ('router_w', 'w1', 'w2')}
    del _L0_ffn_all

    def _L1_xattn_setup():
        import jax, jax.numpy as jnp
        import numpy as np
        HIDDEN = 256
        HEADS = 16
        HEAD_DIM = 64
        key = jax.random.key(seed)
        ks = jax.random.split(key, 7)
        B, Q, K = (2, 512, 1024)
        s = 1.0 / np.sqrt(HIDDEN)
        return {'query': jax.random.normal(ks[0], (B, Q, HIDDEN), dtype=jnp.float32), 'key': jax.random.normal(ks[1], (B, K, HIDDEN), dtype=jnp.float32), 'value': jax.random.normal(ks[2], (B, K, HIDDEN), dtype=jnp.float32), 'w_q': jax.random.normal(ks[3], (HIDDEN, HEADS * HEAD_DIM), dtype=jnp.float32) * s, 'w_k': jax.random.normal(ks[4], (HIDDEN, HEADS * HEAD_DIM), dtype=jnp.float32) * s, 'w_v': jax.random.normal(ks[5], (HIDDEN, HEADS * HEAD_DIM), dtype=jnp.float32) * s, 'w_o': jax.random.normal(ks[6], (HEADS * HEAD_DIM, HIDDEN), dtype=jnp.float32) * s}
    _L1_xattn_all = _L1_xattn_setup()
    _L1_xattn_in = {k: v for k, v in _L1_xattn_all.items() if k in ('w_q', 'w_k', 'w_v', 'w_o')}
    del _L1_xattn_all

    def _L1_ffn_setup():
        import math
        import jax, jax.numpy as jnp
        import numpy as np
        HIDDEN = 256
        INTER = 1024
        EXPERTS = 8
        B, T = (4, 512)
        EPS = 1e-12
        CAP_FACTOR = 1.0
        MIN_CAP = 4

        def layer_norm(x, g, b, eps=EPS):
            m = jnp.mean(x, axis=-1, keepdims=True)
            v = jnp.var(x, axis=-1, keepdims=True)
            return (x - m) * jax.lax.rsqrt(v + eps) * g + b

        def top1_gate(x, wg, capacity):
            logits = x @ wg
            gates = jax.nn.softmax(logits, axis=-1)
            E = wg.shape[-1]
            idx = jnp.argmax(gates, axis=-1)
            mask1 = jax.nn.one_hot(idx, E, dtype=gates.dtype)
            locations = jnp.cumsum(mask1, axis=0) - mask1
            mask1 = mask1 * (locations < capacity).astype(gates.dtype)
            gates1_s = jnp.sum(gates * mask1, axis=-1)
            loc_s = jnp.sum(locations * mask1, axis=-1).astype(jnp.int32)
            loc_oh = jax.nn.one_hot(loc_s, capacity, dtype=gates.dtype)
            combine = gates1_s[:, None, None] * mask1[:, :, None] * loc_oh[:, None, :]
            dispatch = jax.lax.stop_gradient((combine > 0).astype(x.dtype))
            return (combine, dispatch)
        key = jax.random.key(seed)
        ks = jax.random.split(key, 8)
        s = 0.02
        return {'x': jax.random.normal(ks[0], (B, T, HIDDEN), jnp.float32), 'attn_nw': jnp.ones((HIDDEN,), jnp.float32), 'attn_nb': jnp.zeros((HIDDEN,), jnp.float32), 'wg': jax.random.normal(ks[1], (HIDDEN, EXPERTS), jnp.float32) * s, 'inter_w': jax.random.normal(ks[2], (EXPERTS, HIDDEN, INTER), jnp.float32) * s, 'inter_b': jnp.zeros((EXPERTS, INTER), jnp.float32), 'output_w': jax.random.normal(ks[3], (EXPERTS, INTER, HIDDEN), jnp.float32) * s, 'output_b': jnp.zeros((EXPERTS, HIDDEN), jnp.float32), 'res_inter_w': jax.random.normal(ks[4], (HIDDEN, INTER), jnp.float32) * s, 'res_inter_b': jnp.zeros((INTER,), jnp.float32), 'res_output_w': jax.random.normal(ks[5], (INTER, HIDDEN), jnp.float32) * s, 'res_output_b': jnp.zeros((HIDDEN,), jnp.float32), 'res_coef': jax.random.normal(ks[6], (HIDDEN, 2), jnp.float32) * s}
    _L1_ffn_all = _L1_ffn_setup()
    _L1_ffn_in = {k: v for k, v in _L1_ffn_all.items() if k in ('attn_nw', 'attn_nb', 'wg', 'inter_w', 'inter_b', 'output_w', 'output_b', 'res_inter_w', 'res_inter_b', 'res_output_w', 'res_output_b', 'res_coef')}
    del _L1_ffn_all
    return {'x': x, 'ctx_1024': ctx_1024, 'mask_Bx1x1xS2_ff0': mask_Bx1x1xS2_ff0, 'mask_1x1xSxS2_fk0': mask_1x1xSxS2_fk0, 'L0_xattn_w_q': _L0_xattn_in['w_q'], 'L0_xattn_w_k': _L0_xattn_in['w_k'], 'L0_xattn_w_v': _L0_xattn_in['w_v'], 'L0_xattn_w_out': _L0_xattn_in['w_out'], 'L0_xattn_b_q': _L0_xattn_in['b_q'], 'L0_xattn_b_k': _L0_xattn_in['b_k'], 'L0_xattn_b_v': _L0_xattn_in['b_v'], 'L0_xattn_b_out': _L0_xattn_in['b_out'], 'L0_ffn_router_w': _L0_ffn_in['router_w'], 'L0_ffn_w1': _L0_ffn_in['w1'], 'L0_ffn_w2': _L0_ffn_in['w2'], 'L1_xattn_w_q': _L1_xattn_in['w_q'], 'L1_xattn_w_k': _L1_xattn_in['w_k'], 'L1_xattn_w_v': _L1_xattn_in['w_v'], 'L1_xattn_w_o': _L1_xattn_in['w_o'], 'L1_ffn_attn_nw': _L1_ffn_in['attn_nw'], 'L1_ffn_attn_nb': _L1_ffn_in['attn_nb'], 'L1_ffn_wg': _L1_ffn_in['wg'], 'L1_ffn_inter_w': _L1_ffn_in['inter_w'], 'L1_ffn_inter_b': _L1_ffn_in['inter_b'], 'L1_ffn_output_w': _L1_ffn_in['output_w'], 'L1_ffn_output_b': _L1_ffn_in['output_b'], 'L1_ffn_res_inter_w': _L1_ffn_in['res_inter_w'], 'L1_ffn_res_inter_b': _L1_ffn_in['res_inter_b'], 'L1_ffn_res_output_w': _L1_ffn_in['res_output_w'], 'L1_ffn_res_output_b': _L1_ffn_in['res_output_b'], 'L1_ffn_res_coef': _L1_ffn_in['res_coef']}

def reference(x, ctx_1024, mask_Bx1x1xS2_ff0, mask_1x1xSxS2_fk0, L0_xattn_w_q, L0_xattn_w_k, L0_xattn_w_v, L0_xattn_w_out, L0_xattn_b_q, L0_xattn_b_k, L0_xattn_b_v, L0_xattn_b_out, L0_ffn_router_w, L0_ffn_w1, L0_ffn_w2, L1_xattn_w_q, L1_xattn_w_k, L1_xattn_w_v, L1_xattn_w_o, L1_ffn_attn_nw, L1_ffn_attn_nb, L1_ffn_wg, L1_ffn_inter_w, L1_ffn_inter_b, L1_ffn_output_w, L1_ffn_output_b, L1_ffn_res_inter_w, L1_ffn_res_inter_b, L1_ffn_res_output_w, L1_ffn_res_output_b, L1_ffn_res_coef):
    import jax
    import jax.numpy as jnp

    def _L0_xattn_ref(query, key, value, padding_mask, lookahead_mask, w_q, w_k, w_v, w_out, b_q, b_k, b_v, b_out, n_heads):
        import jax, jax.numpy as jnp
        import numpy as np
        D_MODEL = 256
        B, S, D = query.shape
        d_k = D // n_heads
        q = (query @ w_q + b_q).reshape(B, S, n_heads, d_k).transpose(0, 2, 1, 3)
        k = (key @ w_k + b_k).reshape(B, S, n_heads, d_k).transpose(0, 2, 1, 3)
        v = (value @ w_v + b_v).reshape(B, S, n_heads, d_k).transpose(0, 2, 1, 3)
        scores = jnp.einsum('bhqd,bhkd->bhqk', q, k) / jnp.sqrt(jnp.float32(d_k))
        scores = scores + padding_mask + lookahead_mask
        attn = jax.nn.softmax(scores, axis=-1)
        out = jnp.einsum('bhqk,bhkd->bhqd', attn, v)
        out = out.transpose(0, 2, 1, 3).reshape(B, S, D)
        return out @ w_out + b_out

    def _L0_ffn_ref(hidden_states, router_w, w1, w2):
        import jax, jax.numpy as jnp
        import numpy as np
        S, B, H = (512, 4, 256)
        E = 64
        K = 4
        I = 128
        CAP = 256
        s, b, h = hidden_states.shape
        x = hidden_states.reshape(-1, h)
        T = x.shape[0]
        P = T * K
        logits = x @ router_w
        probs_all = jax.nn.softmax(logits, axis=-1)
        top_p, top_i = jax.lax.top_k(probs_all, K)
        rows = jnp.arange(T)[:, None]
        routing_map = jnp.zeros((T, E), dtype=bool).at[rows, top_i].set(True)
        probs = jnp.zeros((T, E), dtype=x.dtype).at[rows, top_i].set(top_p)
        flat = routing_map.T.reshape(-1)
        order = jnp.argsort((~flat).astype(jnp.int32), stable=True)[:P]
        expert_id = order // T
        token_idx = order % T
        group_sizes = routing_map.sum(axis=0)
        starts = jnp.cumsum(group_sizes) - group_sizes
        pos = jnp.arange(P) - starts[expert_id]
        perm_x = x[token_idx]
        buf = jnp.zeros((E, CAP, h), dtype=x.dtype).at[expert_id, pos].set(perm_x)
        h1 = jnp.einsum('ech,ehf->ecf', buf, w1)
        g = jax.nn.silu(h1[..., :I]) * h1[..., I:]
        y = jnp.einsum('eci,eih->ech', g, w2)
        perm_y = y[expert_id, pos]
        perm_probs = probs.T.reshape(-1)[order]
        out = jnp.zeros((T, h), dtype=x.dtype).at[token_idx].add(perm_y * perm_probs[:, None])
        return out.reshape(s, b, h)

    def _L1_xattn_ref(query, key, value, w_q, w_k, w_v, w_o):
        import jax, jax.numpy as jnp
        import numpy as np
        HIDDEN = 256
        HEADS = 16
        HEAD_DIM = 64
        B, Q, _ = query.shape
        Kl = key.shape[1]
        scale = HEAD_DIM ** (-0.5)
        q = (query @ w_q).reshape(B, Q, HEADS, HEAD_DIM).transpose(0, 2, 1, 3)
        k = (key @ w_k).reshape(B, Kl, HEADS, HEAD_DIM).transpose(0, 2, 1, 3)
        v = (value @ w_v).reshape(B, Kl, HEADS, HEAD_DIM).transpose(0, 2, 1, 3)
        scores = jnp.einsum('bhqd,bhkd->bhqk', q, k) * scale
        attn = jax.nn.softmax(scores, axis=-1)
        out = jnp.einsum('bhqk,bhkd->bhqd', attn, v)
        out = out.transpose(0, 2, 1, 3).reshape(B, Q, HEADS * HEAD_DIM)
        return out @ w_o

    def _L1_ffn_ref(x, attn_nw, attn_nb, wg, inter_w, inter_b, output_w, output_b, res_inter_w, res_inter_b, res_output_w, res_output_b, res_coef):
        import math
        import jax, jax.numpy as jnp
        import numpy as np
        HIDDEN = 256
        INTER = 1024
        EXPERTS = 8
        B, T = (4, 512)
        EPS = 1e-12
        CAP_FACTOR = 1.0
        MIN_CAP = 4

        def layer_norm(x, g, b, eps=EPS):
            m = jnp.mean(x, axis=-1, keepdims=True)
            v = jnp.var(x, axis=-1, keepdims=True)
            return (x - m) * jax.lax.rsqrt(v + eps) * g + b

        def top1_gate(x, wg, capacity):
            logits = x @ wg
            gates = jax.nn.softmax(logits, axis=-1)
            E = wg.shape[-1]
            idx = jnp.argmax(gates, axis=-1)
            mask1 = jax.nn.one_hot(idx, E, dtype=gates.dtype)
            locations = jnp.cumsum(mask1, axis=0) - mask1
            mask1 = mask1 * (locations < capacity).astype(gates.dtype)
            gates1_s = jnp.sum(gates * mask1, axis=-1)
            loc_s = jnp.sum(locations * mask1, axis=-1).astype(jnp.int32)
            loc_oh = jax.nn.one_hot(loc_s, capacity, dtype=gates.dtype)
            combine = gates1_s[:, None, None] * mask1[:, :, None] * loc_oh[:, None, :]
            dispatch = jax.lax.stop_gradient((combine > 0).astype(x.dtype))
            return (combine, dispatch)
        Bx, Tx, M = x.shape
        S = Bx * Tx
        E = wg.shape[-1]
        capacity = max(MIN_CAP, math.ceil(S / E * CAP_FACTOR))
        residual = x.reshape(S, M)
        attn_out = layer_norm(residual, attn_nw, attn_nb)
        combine, dispatch = top1_gate(attn_out, wg, capacity)
        dispatched = jnp.einsum('sec,sm->ecm', dispatch, attn_out)
        h = jax.nn.gelu(jnp.einsum('ecm,emi->eci', dispatched, inter_w) + inter_b[:, None, :], approximate=True)
        expert_out = jnp.einsum('eci,eim->ecm', h, output_w) + output_b[:, None, :]
        moe_out = jnp.einsum('sec,ecm->sm', combine, expert_out)
        rh = jax.nn.gelu(attn_out @ res_inter_w + res_inter_b, approximate=True)
        res_mlp_out = rh @ res_output_w + res_output_b
        coef = jax.nn.softmax(attn_out @ res_coef, axis=-1)
        out = res_mlp_out * coef[:, :1] + moe_out * coef[:, 1:]
        out = out + residual
        return out.reshape(Bx, Tx, M)
    x = x + _L0_xattn_ref(_layernorm(x, axis=-1), ctx_1024, ctx_1024, mask_Bx1x1xS2_ff0, mask_1x1xSxS2_fk0, L0_xattn_w_q, L0_xattn_w_k, L0_xattn_w_v, L0_xattn_w_out, L0_xattn_b_q, L0_xattn_b_k, L0_xattn_b_v, L0_xattn_b_out, 16)
    x = x + _L0_ffn_ref(_layernorm(x, axis=-1), L0_ffn_router_w, L0_ffn_w1, L0_ffn_w2)
    x = x + _L1_xattn_ref(_layernorm(x, axis=-1), ctx_1024, ctx_1024, L1_xattn_w_q, L1_xattn_w_k, L1_xattn_w_v, L1_xattn_w_o)
    x = x + _L1_ffn_ref(_layernorm(x, axis=-1), L1_ffn_attn_nw, L1_ffn_attn_nb, L1_ffn_wg, L1_ffn_inter_w, L1_ffn_inter_b, L1_ffn_output_w, L1_ffn_output_b, L1_ffn_res_inter_w, L1_ffn_res_inter_b, L1_ffn_res_output_w, L1_ffn_res_output_b, L1_ffn_res_coef)
    return x

_drawn_inputs = setup_inputs


def setup_inputs(seed=0):
    import zlib

    import numpy as np

    out = dict(_drawn_inputs(seed))
    spreads = {'L0_xattn_b_q': (0.0, 0.495),
     'L0_xattn_b_k': (0.0, 2.0),
     'L0_xattn_b_v': (0.0, 0.1),
     'L0_xattn_b_out': (0.0, 0.1),
     'L1_ffn_attn_nw': (1.0, 0.6),
     'L1_ffn_attn_nb': (0.0, 0.8),
     'L1_ffn_inter_b': (0.0, 0.8),
     'L1_ffn_output_b': (0.0, 0.8),
     'L1_ffn_res_inter_b': (0.0, 2.0),
     'L1_ffn_res_output_b': (0.0, 1.16)}
    factors = {'L0_ffn_router_w': 8.0,
     'L0_ffn_w1': 8.0,
     'L0_ffn_w2': 8.0,
     'L1_ffn_wg': 8.0,
     'L1_ffn_inter_w': 8.0,
     'L1_ffn_output_w': 8.0,
     'L1_ffn_res_coef': 8.0,
     'L1_ffn_res_inter_w': 3.785}
    for name, (base, spread) in spreads.items():
        noise = np.random.default_rng([zlib.crc32(name.encode()), seed]).standard_normal(out[name].shape)
        drawn = base * np.exp(spread * noise) if base else spread * noise
        out[name] = jnp.asarray(drawn.astype(out[name].dtype))
    for name, factor in factors.items():
        out[name] = (out[name] * factor).astype(out[name].dtype)
    return out
```

```python
from contextlib import ExitStack

import concourse.bass as bass
from concourse import mybir

P = 128
B, S, D = 4, 512, 256
N = B * S
NT = S // P
KD = D // P
HEADS = 16
DH0, PAD0 = 16, 32
DH1 = 64
QUADS = HEADS // 4
ITEMS = B * QUADS
E0, TOP0, I0, CAP0 = 64, 4, 128, 256
E1, TOP1, I1, CAP1 = 8, 1, 1024, 256
KI = I1 // P
SKIP = 1.0e6

F32 = mybir.dt.float32
BF16 = mybir.dt.bfloat16
U32 = mybir.dt.uint32
I32 = mybir.dt.int32
ALU = mybir.AluOpType
ACT = mybir.ActivationFunctionType
AX = mybir.AxisListType.X

Q_PARTS = (0, 0, 1, 0, 1, 2)
K_PARTS = (0, 1, 0, 2, 1, 0)
STACK = len(Q_PARTS) * DH0


class Store:

    def __init__(self, nc, ctx, prefix):
        self.nc, self.ctx, self.prefix = nc, ctx, prefix

    def sb(self, name, shape, dt=F32):
        return self.ctx.enter_context(self.nc.sbuf_tensor(f"{self.prefix}_{name}", shape, dt))

    def ps(self, name, shape=(P, 512), dt=F32):
        return self.ctx.enter_context(self.nc.psum_tensor(f"{self.prefix}_ps_{name}", list(shape), dt))

    def sems(self, names):
        return {n: self.nc.alloc_semaphore(f"{self.prefix}_{n}") for n in names.split()}


def build_constants(nc, c):
    filled, made = nc.alloc_semaphore("constants_filled"), nc.alloc_semaphore("constants_made")
    ones16_made = nc.alloc_semaphore("constants_ones16")
    with nc.Block() as block:
        @block.vector
        def _(dve):
            nc.vector.memset(c["ones"][:, :], 1.0)
            nc.vector.memset(c["zeros"][:, :], 0.0).then_inc(filled, 1)
            nc.vector.memset(c["ones16"][:, :], 1.0).then_inc(ones16_made, 1)
            dve.wait_ge(ones16_made, 1)

        @block.gpsimd
        def _(pool):
            pool.wait_ge(filled, 1)
            nc.gpsimd.affine_select(out=c["ident"][:, :], in_=c["ones"][:, :], compare_op=ALU.is_equal, fill=0.0, base=0,
                                    pattern=[[-1, P]], channel_multiplier=1).then_inc(made, 1)
            nc.gpsimd.affine_select(out=c["before"][:, :], in_=c["ones"][:, :], compare_op=ALU.is_gt, fill=0.0, base=0,
                                    pattern=[[1, P]], channel_multiplier=-1).then_inc(made, 1)
            nc.gpsimd.iota(c["expert_no"][:, :], pattern=[[1, E0]], base=0, channel_multiplier=0,
                           allow_small_or_imprecise_dtypes=True).then_inc(made, 1)
            nc.gpsimd.iota(c["token_no"][:, :], pattern=[[P, NT]], base=0, channel_multiplier=1,
                           allow_small_or_imprecise_dtypes=True).then_inc(made, 1)
            pool.wait_ge(made, 4)


def layer_norm(nc, x, stats, mv, var, half, rstd, out, eps):
    for t in range(NT):
        nc.vector.bn_stats(stats[:, t, :], x[:, t, :])
    nc.vector.drain()
    for t in range(NT):
        nc.vector.bn_aggr(mv[:, t, :], stats[:, t, :])
    nc.vector.drain()
    nc.vector.tensor_scalar(var[:, :], mv[:, :, 1], eps, None, ALU.add)
    nc.vector.drain()
    nc.vector.tensor_scalar(rstd[:, :].bitcast(I32), var[:, :].bitcast(I32), -0.5, float(0x5F3759DF), ALU.mult, ALU.add)
    nc.vector.drain()
    for _ in range(3):
        nc.vector.tensor_tensor(half[:, :], rstd[:, :], rstd[:, :], ALU.mult)
        nc.vector.drain()
        nc.vector.tensor_tensor(half[:, :], half[:, :], var[:, :], ALU.mult)
        nc.vector.drain()
        nc.vector.tensor_scalar(half[:, :], half[:, :], -0.5, 1.5, ALU.mult, ALU.add)
        nc.vector.drain()
        nc.vector.tensor_tensor(rstd[:, :], rstd[:, :], half[:, :], ALU.mult)
        nc.vector.drain()
    for t in range(NT):
        last = nc.vector.tensor_scalar(out[:, t, :], x[:, t, :], mv[:, t, 0:1], rstd[:, t:t + 1],
                                       ALU.subtract, ALU.mult)
    return last


def norm_buffers(st, prefix=""):
    return (st.sb(prefix + "stats", [P, NT, 6]), st.sb(prefix + "mv", [P, NT, 2]),
            st.sb(prefix + "var", [P, NT]), st.sb(prefix + "half", [P, NT]), st.sb(prefix + "rstd", [P, NT]))


def at(ap, i):
    v = ap[bass.ds(i, 1)]
    names = " ".join("abcdefg"[:len(ap.shape) - 1])
    first = names.split(" ", 1)
    rest = " " + first[1] if len(first) > 1 else ""
    return v.rearrange(f"z {names} -> (z {first[0]}){rest}")


def project_stage(nc, c, io, d):
    with ExitStack() as ctx:
        st = Store(nc, ctx, "pj")
        s = st.sems("w_in x_in c_in bias normed turned_x turned_c xT_out cT_out q_mm k_mm v_mm q_out k_out q_split "
                    "k_split v_out cT_saved parts_saved v_saved")
        w = {n: st.sb(n, [P, KD, D]) for n in "qkv"}
        bcol = {n: st.sb("bcol" + n, [P, KD]) for n in "qk"}
        bq4 = st.sb("bq4", [P, KD])
        bv = st.sb("bv", [P, D])
        x4, c4, xn4 = st.sb("x4", [P, NT, D]), st.sb("c4", [P, NT, D]), st.sb("xn4", [P, NT, D])
        xT, cT = st.sb("xT", [P, KD, S]), st.sb("cT", [P, KD, S])
        q1, k1, rest = st.sb("q1", [P, KD, S]), st.sb("k1", [P, KD, S]), st.sb("rest", [P, KD, S])
        qp, kp = st.sb("qp", [P, 3, KD, S], BF16), st.sb("kp", [P, 3, KD, S], BF16)
        vp = st.sb("vp", [P, NT, HEADS, PAD0])
        nb = norm_buffers(st)
        tx = [st.ps(f"tx{k}") for k in range(KD)]
        tc = [st.ps(f"tc{k}") for k in range(KD)]
        pq = [st.ps(f"pq{k}") for k in range(KD)]
        pk = [st.ps(f"pk{k}") for k in range(KD)]

        with nc.Block() as block:
            @block.sync
            def _(sp):
                for n, src in (("q", io["L0_xattn_w_q"]), ("k", io["L0_xattn_w_k"]), ("v", io["L0_xattn_w_v"])):
                    sp.dma_start(w[n][:, :, :], src.rearrange("(k p) f -> p k f", p=P)).then_inc(s["w_in"], 16)
                with nc.allow_non_contiguous_dma(reason="256 biases as columns"):
                    sp.dma_start(bcol["q"][:, :], io["L0_xattn_b_q"].rearrange("(k p) -> p k", p=P)).then_inc(s["bias"], 16)
                    sp.dma_start(bcol["k"][:, :], io["L0_xattn_b_k"].rearrange("(k p) -> p k", p=P)).then_inc(s["bias"], 16)
                sp.dma_start(bv[:, :], io["L0_xattn_b_v"].rearrange("(a f) -> a f", a=1).to_broadcast([P, D])).then_inc(s["bias"], 16)
                with sp.Fori(0, B) as b:
                    sp.wait_ge(s["normed"], b)
                    sp.dma_start(x4[:, :, :], at(io["x"], b).rearrange("(t p) f -> p t f", p=P)).then_inc(s["x_in"], 16)
                    sp.wait_ge(s["turned_c"], b)
                    sp.dma_start(c4[:, :, :], at(io["ctx_1024"], b).rearrange("(t p) f -> p t f", p=P)).then_inc(s["c_in"], 16)
                    sp.wait_ge(s["cT_out"], KD * (b + 1))
                    sp.dma_start(at(d["ctxT"], b).rearrange("(k p) s -> p k s", p=P), cT[:, :, :]).then_inc(s["cT_saved"], 16)
                    sp.wait_ge(s["k_split"], b + 1)
                    sp.dma_start(at(d["kp"], b).rearrange("j (k p) s -> p (j k) s", p=P),
                                 kp[:, :, :, :].rearrange("p j k s -> p (j k) s")).then_inc(s["parts_saved"], 16)
                    sp.wait_ge(s["q_split"], b + 1)
                    sp.dma_start(at(d["qp"], b).rearrange("j (k p) s -> p (j k) s", p=P),
                                 qp[:, :, :, :].rearrange("p j k s -> p (j k) s")).then_inc(s["parts_saved"], 16)
                    sp.wait_ge(s["v_out"], NT * (b + 1))
                    for q in range(QUADS):
                        sp.dma_start(at(d["v0"], b)[q].rearrange("(t p) f -> p t f", p=P),
                                     vp[:, :, 4 * q:4 * q + 4, :].rearrange("p t h f -> p t (h f)")).then_inc(s["v_saved"], 16)
                sp.wait_ge(s["cT_saved"], 16 * B)
                sp.wait_ge(s["parts_saved"], 16 * 2 * B)
                sp.wait_ge(s["v_saved"], 16 * QUADS * B)

            @block.tensor
            def _(pe):
                pe.wait_ge(s["w_in"], 48)
                with pe.Fori(0, B) as b:
                    pe.wait_ge(s["c_in"], 16 * b + 16)
                    for k in range(KD):
                        for t in range(NT):
                            last = nc.tensor.transpose(tc[k][:, t * P:(t + 1) * P], c4[:, t, k * P:(k + 1) * P], c["ident"][:, :])
                    last.then_inc(s["turned_c"], 1)
                    pe.wait_ge(s["normed"], b + 1)
                    pe.wait_ge(s["v_out"], NT * b)
                    for k in range(KD):
                        for t in range(NT):
                            last = nc.tensor.transpose(tx[k][:, t * P:(t + 1) * P], xn4[:, t, k * P:(k + 1) * P], c["ident"][:, :])
                    last.then_inc(s["turned_x"], 1)
                    pe.wait_ge(s["cT_out"], KD * (b + 1))
                    for m in range(KD):
                        for k in range(KD):
                            last = nc.tensor.matmul(pk[m][:, :], w["k"][:, k, m * P:(m + 1) * P], cT[:, k, :],
                                                    start=k == 0, stop=k == KD - 1)
                        last.then_inc(s["k_mm"], 1)
                    pe.wait_ge(s["xT_out"], KD * (b + 1))
                    for m in range(KD):
                        for k in range(KD):
                            last = nc.tensor.matmul(pq[m][:, :], w["q"][:, k, m * P:(m + 1) * P], xT[:, k, :],
                                                    start=k == 0, stop=k == KD - 1)
                        last.then_inc(s["q_mm"], 1)
                    for t in range(NT):
                        for k in range(KD):
                            last = nc.tensor.matmul(tx[t // 2][:, (t % 2) * D:(t % 2 + 1) * D], cT[:, k, t * P:(t + 1) * P],
                                                    w["v"][:, k, :], start=k == 0, stop=k == KD - 1)
                        if t % 2:
                            last.then_inc(s["v_mm"], 1)

            @block.scalar
            def _(act):
                act.wait_ge(s["bias"], 48 + 1)
                with act.Fori(0, B) as b:
                    act.wait_ge(s["turned_c"], b + 1)
                    act.wait_ge(s["cT_saved"], 16 * b)
                    for k in range(KD):
                        nc.scalar.copy(cT[:, k, :], tc[k][:, :]).then_inc(s["cT_out"], 1)
                    act.wait_ge(s["turned_x"], b + 1)
                    for k in range(KD):
                        nc.scalar.copy(xT[:, k, :], tx[k][:, :]).then_inc(s["xT_out"], 1)
                    for m in range(KD):
                        act.wait_ge(s["k_mm"], KD * b + m + 1)
                        act.wait_ge(s["k_split"], b)
                        nc.scalar.activation(k1[:, m, :], pk[m][:, :], ACT.Identity, bias=bcol["k"][:, m:m + 1]).then_inc(s["k_out"], 1)
                    for m in range(KD):
                        act.wait_ge(s["q_mm"], KD * b + m + 1)
                        act.wait_ge(s["q_split"], b)
                        nc.scalar.activation(q1[:, m, :], pq[m][:, :], ACT.Identity, bias=bq4[:, m:m + 1],
                                             scale=DH0 ** -0.5).then_inc(s["q_out"], 1)

            @block.vector
            def _(dve):
                nc.vector.memset(vp[:, :, :, :].rearrange("p t h f -> p (t h f)"), 0.0)
                dve.wait_ge(s["bias"], 48)
                nc.vector.tensor_scalar(bq4[:, :], bcol["q"][:, :], DH0 ** -0.5, None, ALU.mult).then_inc(s["bias"], 1)

                def split(src, parts):
                    nc.vector.tensor_copy(parts[:, 0], src[:, :, :])
                    nc.vector.drain()
                    nc.vector.tensor_tensor(rest[:, :, :], src[:, :, :], parts[:, 0], ALU.subtract)
                    nc.vector.drain()
                    nc.vector.tensor_copy(parts[:, 1], rest[:, :, :])
                    nc.vector.drain()
                    return nc.vector.tensor_tensor(parts[:, 2], rest[:, :, :], parts[:, 1], ALU.subtract)

                with dve.Fori(0, B) as b:
                    dve.wait_ge(s["x_in"], 16 * b + 16)
                    dve.wait_ge(s["turned_x"], b)
                    layer_norm(nc, x4, *nb, xn4, 1e-5).then_inc(s["normed"], 1)
                    dve.wait_ge(s["k_out"], KD * (b + 1))
                    dve.wait_ge(s["parts_saved"], 32 * b)
                    split(k1, kp).then_inc(s["k_split"], 1)
                    dve.wait_ge(s["v_saved"], 16 * QUADS * b)
                    for t in range(NT):
                        if t % 2 == 0:
                            dve.wait_ge(s["v_mm"], NT // 2 * b + t // 2 + 1)
                        nc.vector.tensor_tensor(vp[:, t, :, 0:DH0],
                                                tx[t // 2][:, (t % 2) * D:(t % 2 + 1) * D].rearrange("p (h f) -> p h f", h=HEADS),
                                                bv[:, :].rearrange("p (h f) -> p h f", h=HEADS), ALU.add).then_inc(s["v_out"], 1)
                    dve.wait_ge(s["q_out"], KD * (b + 1))
                    split(q1, qp).then_inc(s["q_split"], 1)



NU = 4 * NT
BODY = 2 * NU
DEEP = 4
LAG_T = 3
LAG_V = 5
LAG_N = 6
STEPS = BODY + LAG_N + 2


def masked_attention_stage(nc, c, io, d):
    with ExitStack() as ctx:
        st = Store(nc, ctx, "a0")
        s = st.sems("in0 in1 mask_in mask_made scores lifted exped turned evac_d evac_a pv o_copied spread recip_mm normed saved0 saved1")
        qs = [st.sb(f"qs{i}", [STACK, 4, S], BF16) for i in range(2)]
        ks = [st.sb(f"ks{i}", [STACK, 4, S], BF16) for i in range(2)]
        v = [st.sb(f"v{i}", [P, NT, 4 * PAD0]) for i in range(2)]
        mask, maskb, pad = st.sb("mask", [P, NT, S]), st.sb("maskb", [P, NT, S]), st.sb("pad", [P, B, S])
        low = [st.sb(f"low{i}", [P, S]) for i in range(DEEP)]
        prob = [st.sb(f"prob{i}", [P, S]) for i in range(DEEP)]
        nmax, total = st.sb("nmax", [P, BODY]), st.sb("total", [P, BODY])
        recip, spread = st.sb("recip", [P, NU]), st.sb("spread", [P, NT, 4, PAD0])
        pT = [st.sb(f"pT{i}", [P, NT, S]) for i in range(2)]
        o_sb = st.sb("o_sb", [P, S])
        o_n = [st.sb(f"o_n{i}", [P, S]) for i in range(2)]
        cells = st.sb("cells", [P, BODY])
        ps_s = [st.ps(f"s{i}") for i in range(2)]
        ps_t = [st.ps(f"t{i}") for i in range(2)]
        ps_o = [st.ps(f"o{i}") for i in range(2)]
        ps_r = st.ps("r")
        s_in, s_saved = (s["in0"], s["in1"]), (s["saved0"], s["saved1"])
        LOADS = 2 * len(Q_PARTS) + 1

        with nc.Block() as block:
            @block.sync
            def _(sp):
                def load(b, quad, par):
                    for t, (a, b_) in enumerate(zip(Q_PARTS, K_PARTS)):
                        for dst, src in ((qs[par], at(d["qp"], b)[a]), (ks[par], at(d["kp"], b)[b_])):
                            sp.dma_start(dst[t * DH0:(t + 1) * DH0, :, :],
                                         src[quad * 64:quad * 64 + 64, :].rearrange("(h f) s -> f h s", h=4)).then_inc(s_in[par], 16)
                    sp.dma_start(v[par][:, :, :], at(d["v0"], b)[quad].rearrange("(t p) f -> p t f", p=P)).then_inc(s_in[par], 16)

                def save(n, par):
                    sp.wait_ge(s["normed"], n + 2)
                    sp.dma_start(at(d["o0"], n), o_n[par][:, :]).then_inc(s_saved[par], 16)

                sp.sem_inc(s["saved0"], 16)
                sp.sem_inc(s["saved1"], 16)
                sp.dma_start(mask[:, :, :], io["mask_1x1xSxS2_fk0"].rearrange("x y (t p) s -> p (x y t) s", p=P)).then_inc(s["mask_in"], 16)
                for b in range(B):
                    sp.dma_start(pad[:, b, :], io["mask_Bx1x1xS2_ff0"][b, 0].to_broadcast([P, S])).then_inc(s["mask_in"], 16)
                for par in range(2):
                    load(0, par, par)
                for par in range(2):
                    sp.wait_ge(s["pv"], 4 * par + 4 + 2)
                    load(0, 2 + par, par)
                    save(par, par)
                with sp.Fori(1, B) as b:
                    for quad in range(QUADS):
                        sp.wait_ge(s["pv"], b * 16 + 4 * quad - 2)
                        load(b, quad, quad % 2)
                        save(b * QUADS + quad - 2, quad % 2)
                save(ITEMS - 2, 0)
                save(ITEMS - 1, 1)
                for par in range(2):
                    sp.wait_ge(s_saved[par], 16 * (ITEMS // 2) + 16)

            @block.tensor
            def _(pe):
                pe.sem_inc(s["turned"], DEEP)
                pe.sem_inc(s["pv"], 2)
                with pe.Fori(0, ITEMS // 2) as body:
                    u0 = body * BODY
                    for step in range(STEPS):
                        w = step
                        if w < BODY:
                            par, h, t = w // NU, w % NU // NT, w % NT
                            if w % NU == 0:
                                pe.wait_ge(s_in[par], body * (LOADS * 16) + LOADS * 16)
                            pe.wait_ge(s["lifted"], u0 + w + 1)
                            nc.tensor.matmul(ps_s[w % 2][:, :], qs[par][:, h, t * P:(t + 1) * P], ks[par][:, h, :],
                                             start=True, stop=True).then_inc(s["scores"], 1)
                        w = step - LAG_T
                        if 0 <= w < BODY:
                            pe.wait_ge(s["exped"], u0 + w + 1 + DEEP)
                            pe.wait_ge((s["evac_d"], s["evac_a"])[w % 2], body * NU + w // 2 + 1)
                            for k in range(NT):
                                last = nc.tensor.transpose(ps_t[w % 2][:, k * P:(k + 1) * P],
                                                           prob[w % DEEP][:, k * P:(k + 1) * P], c["ident"][:, :])
                            last.then_inc(s["turned"], 1)
                        w = step - LAG_V
                        if 0 <= w < BODY and w % NT == NT - 1:
                            par, h, g = w // NU, w % NU // NT, w // NT
                            pe.wait_ge(s["evac_d"], body * NU + w // 2 + 1 + 1)
                            pe.wait_ge(s["evac_a"], body * NU + w // 2 + 1 + 1)
                            if h == 0:
                                pe.wait_ge(s["o_copied"], body * 2 + par + 1)
                            for k in range(NT):
                                last = nc.tensor.matmul(ps_o[par][h * PAD0:(h + 1) * PAD0, :],
                                                        v[par][:, k, h * PAD0:(h + 1) * PAD0], pT[g % 2][:, k, :],
                                                        start=k == 0, stop=k == NT - 1)
                            last.then_inc(s["pv"], 1)
                        w = step - LAG_N
                        if 0 <= w < BODY and w % NU == NU - 1:
                            par = w // NU
                            pe.wait_ge(s["spread"], body * 2 + par + 1)
                            pe.wait_ge(s["normed"], body * 2 + par + 1)
                            for t in range(NT):
                                last = nc.tensor.matmul(ps_r[:, t * P:(t + 1) * P],
                                                        spread[:, t, :, :].rearrange("p h f -> p (h f)"), c["ident"][:, :],
                                                        start=True, stop=True)
                            last.then_inc(s["recip_mm"], 1)

            @block.vector
            def _(dve):
                dve.sem_inc(s["lifted"], 2)
                dve.sem_inc(s["evac_d"], 1)
                dve.sem_inc(s["normed"], 1)
                dve.wait_ge(s["mask_in"], 16 * (B + 1))
                with dve.Fori(0, B) as b:
                    nc.vector.drain()
                    for t in range(NT):
                        nc.vector.tensor_tensor(maskb[:, t, :], mask[:, t, :],
                                                pad[:, bass.ds(b, 1), :].rearrange("p a s -> p (a s)"), ALU.add)
                    nc.vector.drain()
                    with dve.Fori(0, 2) as half:
                        body = b * 2 + half
                        u0 = body * BODY
                        for step in range(STEPS):
                            w = step
                            if w < BODY:
                                dve.wait_ge(s["scores"], u0 + w + 1)
                                dve.wait_ge(s["exped"], u0 + w + 1)
                                if w < LAG_T or w % 2 == 0:
                                    nc.vector.memset(cells[:, w:w + 1], 0.0)
                            w = step - LAG_T
                            if 0 <= w < BODY and w % 2 == 0:
                                dve.wait_ge(s["turned"], u0 + w + 1 + DEEP)
                                if w % NT == 0:
                                    dve.wait_ge(s["pv"], body * 8 + w // NT + 1)
                                nc.vector.tensor_copy(pT[w // NT % 2][:, :, w % NT * P:(w % NT + 1) * P],
                                                      ps_t[0][:, :].rearrange("p (k s) -> p k s", k=NT)).then_inc(s["evac_d"], 1)
                            w = step
                            if w < BODY:
                                nc.vector.tensor_tensor_reduce(out=low[w % DEEP][:, :], in0=ps_s[w % 2][:, :],
                                                               in1=maskb[:, w % NT, :], scale=-1.0, scalar=3.0e38,
                                                               op0=ALU.add, op1=ALU.min,
                                                               accum_out=nmax[:, w:w + 1]).then_inc(s["lifted"], 1)
                            if 0 <= step - LAG_T < BODY and (step - LAG_T) % NU == NU - 1:
                                par = (step - LAG_T) // NU
                                dve.wait_ge(s["exped"], u0 + (par + 1) * NU + DEEP)
                                dve.wait_ge(s["recip_mm"], body * 2 + par)
                                nc.vector.reciprocal(recip[:, :], total[:, par * NU:(par + 1) * NU])
                                nc.vector.drain()
                                nc.vector.tensor_copy(spread[:, :, :, :],
                                                      recip[:, :].rearrange("p (h t o) -> p t h o", h=4, o=1)
                                                      .to_broadcast([P, NT, 4, PAD0])).then_inc(s["spread"], 1)
                            w = step - LAG_N - 1
                            if 0 <= w < BODY and w % NU == NU - 1:
                                par = w // NU
                                dve.wait_ge(s["recip_mm"], body * 2 + par + 1)
                                dve.wait_ge(s["o_copied"], body * 2 + par + 1 + 2)
                                dve.wait_ge(s_saved[par], body * 16 + 16)
                                nc.vector.tensor_tensor(o_n[par][:, :], o_sb[:, :], ps_r[:, :], ALU.mult).then_inc(s["normed"], 1)

            @block.scalar
            def _(act):
                act.sem_inc(s["exped"], DEEP)
                act.sem_inc(s["evac_a"], 1)
                act.sem_inc(s["o_copied"], 2)
                with act.Fori(0, ITEMS // 2) as body:
                    u0 = body * BODY
                    for step in range(STEPS):
                        w = step
                        if w < BODY:
                            act.wait_ge(s["lifted"], u0 + w + 1 + 2)
                            act.wait_ge(s["turned"], u0 + w + 1)
                            nc.scalar.activation(prob[w % DEEP][:, :], low[w % DEEP][:, :], ACT.Exp, bias=nmax[:, w:w + 1],
                                                 scale=-1.0, accum_out=total[:, w:w + 1]).then_inc(s["exped"], 1)
                        w = step - LAG_T
                        if 0 <= w < BODY and w % 2 == 1:
                            act.wait_ge(s["turned"], u0 + w + 1 + DEEP)
                            if w % NT == 1:
                                act.wait_ge(s["pv"], body * 8 + w // NT + 1)
                            nc.scalar.copy(pT[w // NT % 2][:, :, w % NT * P:(w % NT + 1) * P],
                                           ps_t[1][:, :].rearrange("p (k s) -> p k s", k=NT)).then_inc(s["evac_a"], 1)
                        w = step - LAG_N
                        if 0 <= w < BODY and w % NU == NU - 1:
                            par = w // NU
                            act.wait_ge(s["pv"], body * 8 + par * 4 + 4 + 2)
                            act.wait_ge(s["normed"], body * 2 + par + 1)
                            nc.scalar.copy(o_sb[:, :], ps_o[par][:, :]).then_inc(s["o_copied"], 1)


class Router:

    def __init__(self, nc, st, c, experts, top, cap, drop):
        self.nc, self.c, self.E, self.top, self.cap, self.drop = nc, c, experts, top, cap, drop
        self.R = NT * top
        self.nmax, self.sums, self.rsum = st.sb("nmax", [P, NT]), st.sb("sums", [P, NT]), st.sb("rsum", [P, NT])
        self.e = st.sb("e", [P, NT, experts])
        self.best, self.best_at = st.sb("best", [P, NT, 8]), st.sb("best_at", [P, NT, 8], U32)
        self.expert = st.sb("expert", [P, self.R])
        self.hot, self.hot_pos = st.sb("hot", [P, self.R, experts]), st.sb("hot_pos", [P, self.R, experts])
        self.chosen, self.before = st.sb("chosen", [P, NT, experts], BF16), st.sb("before", [P, experts], BF16)
        self.pos, self.fits, self.skip = st.sb("pos", [P, self.R]), st.sb("fits", [P, self.R]), st.sb("skip", [P, self.R])
        self.slot, self.slot_skip = st.sb("slot", [P, self.R]), st.sb("slot_skip", [P, self.R])
        self.slot_read, self.slot_write = st.sb("slot_read", [P, self.R], U32), st.sb("slot_write", [P, self.R], U32)
        self.weight = st.sb("weight", [P, self.R])
        self.tok_f, self.tok = st.sb("tok_f", [P, NT]), st.sb("tok", [P, NT], U32)

    def start(self):
        v = self.nc.vector
        v.memset(self.before[:, :], 0.0)
        v.tensor_copy(self.tok_f[:, :], self.c["token_no"][:, :])

    def tail(self, ap):
        return ap.rearrange("p (r o) -> p r o", o=1)

    def pick(self):
        v = self.nc.vector
        v.reciprocal(self.rsum[:, :], self.sums[:, :])
        for t in range(NT):
            v.max(self.best[:, t, :], self.e[:, t, :])
        v.drain()
        for t in range(NT):
            v.max_index(self.best_at[:, t, :], self.best[:, t, :], self.e[:, t, :])
        v.drain()
        v.tensor_copy(self.expert[:, :].rearrange("p (t j) -> p t j", t=NT), self.best_at[:, :, 0:self.top])
        v.drain()
        full = [P, self.R, self.E]
        v.tensor_tensor(self.hot[:, :, :], self.c["expert_no"][:, 0:self.E].rearrange("p (o e) -> p o e", o=1).to_broadcast(full),
                        self.tail(self.expert[:, :]).to_broadcast(full), ALU.is_equal)
        v.drain()
        if self.top == 1:
            return v.tensor_copy(self.chosen[:, :, :], self.hot[:, :, :])
        with self.nc.allow_low_precision(reason="zeros and ones"):
            return v.tensor_reduce(self.chosen[:, :, :], self.hot[:, :, :].rearrange("p (t j) e -> p t e j", t=NT), AX, ALU.add)

    def place(self, ps_pos):
        v = self.nc.vector
        earlier = ps_pos[:, 0:NT * self.E].rearrange("p (t e) -> p t e", t=NT)
        for t in range(NT):
            rows = slice(t * self.top, (t + 1) * self.top)
            v.tensor_tensor(self.hot_pos[:, rows, :], self.hot[:, rows, :],
                            earlier[:, t:t + 1, :].to_broadcast([P, self.top, self.E]), ALU.mult)
            v.drain()
            v.tensor_tensor(self.before[:, :], self.before[:, :], self.chosen[:, t, :], ALU.add)
        v.drain()
        v.tensor_reduce(self.pos[:, :], self.hot_pos[:, :, :], AX, ALU.add)
        v.drain()
        v.tensor_scalar(self.fits[:, :], self.pos[:, :], float(self.cap), None, ALU.is_lt)
        v.tensor_scalar(self.pos[:, :], self.pos[:, :], float(self.cap - 1), None, ALU.min)
        v.drain()
        v.tensor_scalar(self.skip[:, :], self.fits[:, :], -SKIP, SKIP, ALU.mult, ALU.add)
        v.tensor_scalar(self.slot[:, :], self.expert[:, :], float(self.cap), None, ALU.mult)
        v.tensor_tensor(self.weight[:, :].rearrange("p (t j) -> p t j", t=NT), self.best[:, :, 0:self.top],
                        self.tail(self.rsum[:, :]).to_broadcast([P, NT, self.top]), ALU.mult)
        v.drain()
        v.tensor_tensor(self.slot[:, :], self.slot[:, :], self.pos[:, :], ALU.add)
        if self.drop:
            v.tensor_tensor(self.weight[:, :], self.weight[:, :], self.fits[:, :], ALU.mult)
        v.tensor_copy(self.tok[:, :], self.tok_f[:, :])
        v.drain()
        v.tensor_scalar(self.tok_f[:, :], self.tok_f[:, :], float(S), None, ALU.add)
        return v.tensor_copy(self.slot_read[:, :], self.slot[:, :])

    def exponentials(self, logits):
        for t in range(NT):
            last = self.nc.scalar.activation(self.e[:, t, :], logits[:, t, :], ACT.Exp, bias=self.nmax[:, t:t + 1],
                                             accum_out=self.sums[:, t:t + 1])
        return last

    def count_earlier(self, ps_pos):
        mm = self.nc.tensor.matmul
        for t in range(NT):
            o = ps_pos[:, t * self.E:(t + 1) * self.E]
            mm(o, self.c["ones16"][:, :], self.before[:, :], start=True, stop=False)
            for u in range(t):
                mm(o, self.c["ones16"][:, :], self.chosen[:, u, :], start=False, stop=False)
            last = mm(o, self.c["before"][:, :], self.chosen[:, t, :], start=False, stop=True)
        return last

    def scatter(self, table, done):
        pool = self.nc.gpsimd
        pool.tensor_tensor(self.slot_skip[:, :], self.slot[:, :], self.skip[:, :], ALU.add)
        pool.drain()
        pool.tensor_copy(self.slot_write[:, :], self.slot_skip[:, :])
        pool.drain()
        for r in range(self.R):
            t = r // self.top
            pool.indirect_dma_start(out=table, out_offset=bass.IndirectOffsetOnAxis(ap=self.slot_write[:, r:r + 1], axis=0),
                                    in_=self.tok[:, t:t + 1], in_offset=None, bounds_check=self.E * self.cap - 1,
                                    oob_is_err=False).then_inc(done, 16)


def route0_stage(nc, c, io, d):
    with ExitStack() as ctx:
        st = Store(nc, ctx, "r0")
        s = st.sems("w_in wo_in bo_in zeroed o_in x_in product summed normed turned xT_out logits maxed exped picked counted placed "
                    "scattered x_saved xn_saved slots_saved table_zero")
        wo = st.sb("wo", [P, QUADS, D])
        wr = st.sb("wr", [P, KD, E0])
        bo = st.sb("bo", [P, D])
        o4, x4 = st.sb("o4", [P, QUADS, S]), st.sb("x4", [P, NT, D])
        x1, xn = st.sb("x1", [P, NT, D]), st.sb("xn", [P, NT, D])
        xT = st.sb("xT", [P, KD, S])
        nb = norm_buffers(st)
        r = Router(nc, st, c, E0, TOP0, CAP0, drop=False)
        ps_y = [st.ps(f"y{i}") for i in range(2)]
        ps_x = [st.ps(f"x{i}") for i in range(KD)]
        ps_l, ps_p = st.ps("l"), st.ps("p")
        logits = ps_l[:, 0:NT * E0].rearrange("p (t e) -> p t e", t=NT)

        with nc.Block() as block:
            @block.sync
            def _(sp):
                sp.wait_ge(s["zeroed"], 1)
                for h in range(HEADS):
                    sp.dma_start(wo[h % 4 * PAD0:h % 4 * PAD0 + DH0, h // 4, :],
                                 io["L0_xattn_w_out"][h * DH0:(h + 1) * DH0, :]).then_inc(s["wo_in"], 16)
                sp.dma_start(wr[:, :, :], io["L0_ffn_router_w"].rearrange("(k p) e -> p k e", p=P)).then_inc(s["w_in"], 16)
                sp.dma_start(bo[:, :], io["L0_xattn_b_out"].rearrange("(a f) -> a f", a=1).to_broadcast([P, D])).then_inc(s["bo_in"], 16)
                sp.dma_start(d["table0"].rearrange("(p k) o -> p (k o)", p=P), c["zeros"][:, :].bitcast(U32)).then_inc(s["table_zero"], 16)
                with sp.Fori(0, B) as b:
                    sp.wait_ge(s["product"], 2 * b)
                    sp.dma_start(o4[:, :, :], at(d["o0"].rearrange("(b q) p s -> b q p s", b=B), b).rearrange("q p s -> p q s")).then_inc(s["o_in"], 16)
                    sp.wait_ge(s["summed"], b)
                    sp.dma_start(x4[:, :, :], at(io["x"], b).rearrange("(t p) f -> p t f", p=P)).then_inc(s["x_in"], 16)
                    sp.wait_ge(s["summed"], b + 1)
                    sp.dma_start(at(d["x1"], b).rearrange("(t p) f -> p t f", p=P), x1[:, :, :]).then_inc(s["x_saved"], 16)
                    sp.wait_ge(s["normed"], b + 1)
                    sp.dma_start(at(d["xn1"].rearrange("(b s) f -> b s f", b=B), b).rearrange("(t p) f -> p t f", p=P), xn[:, :, :]).then_inc(s["xn_saved"], 16)
                    sp.wait_ge(s["placed"], b + 1)
                    sp.dma_start(at(d["slots0"], b), r.slot_read[:, :]).then_inc(s["slots_saved"], 16)
                    sp.dma_start(at(d["weights0"], b), r.weight[:, :]).then_inc(s["slots_saved"], 16)
                sp.wait_ge(s["x_saved"], 16 * B)
                sp.wait_ge(s["xn_saved"], 16 * B)
                sp.wait_ge(s["slots_saved"], 32 * B)

            @block.gpsimd
            def _(pool):
                pool.wait_ge(s["table_zero"], 16)
                with pool.Fori(0, B) as b:
                    pool.wait_ge(s["scattered"], 16 * r.R * b)
                    pool.wait_ge(s["placed"], b + 1)
                    r.scatter(d["table0"], s["scattered"])
                pool.wait_ge(s["scattered"], 16 * r.R * B)

            @block.tensor
            def _(pe):
                pe.wait_ge(s["wo_in"], 16 * HEADS)
                pe.wait_ge(s["w_in"], 16)
                with pe.Fori(0, B) as b:
                    pe.wait_ge(s["o_in"], 16 * b + 16)
                    pe.wait_ge(s["summed"], b)
                    for t in range(NT):
                        for q in range(QUADS):
                            last = nc.tensor.matmul(ps_y[t // 2][:, t % 2 * D:(t % 2 + 1) * D], o4[:, q, t * P:(t + 1) * P],
                                                    wo[:, q, :], start=q == 0, stop=q == QUADS - 1)
                        if t % 2:
                            last.then_inc(s["product"], 1)
                    pe.wait_ge(s["normed"], b + 1)
                    pe.wait_ge(s["xT_out"], KD * b)
                    for k in range(KD):
                        for t in range(NT):
                            last = nc.tensor.transpose(ps_x[k][:, t * P:(t + 1) * P], xn[:, t, k * P:(k + 1) * P], c["ident"][:, :])
                    last.then_inc(s["turned"], 1)
                    pe.wait_ge(s["xT_out"], KD * (b + 1))
                    for t in range(NT):
                        for k in range(KD):
                            last = nc.tensor.matmul(ps_l[:, t * E0:(t + 1) * E0], xT[:, k, t * P:(t + 1) * P], wr[:, k, :],
                                                    start=k == 0, stop=k == KD - 1)
                    last.then_inc(s["logits"], 1)
                    pe.wait_ge(s["picked"], b + 1)
                    r.count_earlier(ps_p).then_inc(s["counted"], 1)

            @block.scalar
            def _(act):
                with act.Fori(0, B) as b:
                    act.wait_ge(s["turned"], b + 1)
                    for k in range(KD):
                        nc.scalar.copy(xT[:, k, :], ps_x[k][:, :]).then_inc(s["xT_out"], 1)
                    act.wait_ge(s["maxed"], b + 1)
                    r.exponentials(logits).then_inc(s["exped"], 1)

            @block.vector
            def _(dve):
                nc.vector.memset(wo[:, :, :].rearrange("p q f -> p (q f)"), 0.0).then_inc(s["zeroed"], 1)
                r.start()
                dve.wait_ge(s["bo_in"], 16)
                with dve.Fori(0, B) as b:
                    dve.wait_ge(s["x_in"], 16 * b + 16)
                    dve.wait_ge(s["x_saved"], 16 * b)
                    for t in range(NT):
                        nc.vector.tensor_tensor(x1[:, t, :], x4[:, t, :], bo[:, :], ALU.add)
                    nc.vector.drain()
                    for half in range(2):
                        dve.wait_ge(s["product"], 2 * b + half + 1)
                        last = nc.vector.tensor_tensor(x1[:, 2 * half:2 * half + 2, :], x1[:, 2 * half:2 * half + 2, :],
                                                       ps_y[half][:, :].rearrange("p (t f) -> p t f", t=2), ALU.add)
                    last.then_inc(s["summed"], 1)
                    nc.vector.drain()
                    dve.wait_ge(s["xn_saved"], 16 * b)
                    dve.wait_ge(s["turned"], b)
                    layer_norm(nc, x1, *nb, xn, 1e-5).then_inc(s["normed"], 1)
                    dve.wait_ge(s["logits"], b + 1)
                    nc.vector.tensor_reduce(r.nmax[:, :], logits, AX, ALU.max, negate=True).then_inc(s["maxed"], 1)
                    dve.wait_ge(s["exped"], b + 1)
                    r.pick().then_inc(s["picked"], 1)
                    dve.wait_ge(s["slots_saved"], 32 * b)
                    dve.wait_ge(s["scattered"], 16 * r.R * b)
                    dve.wait_ge(s["counted"], b + 1)
                    r.place(ps_p).then_inc(s["placed"], 1)


def experts0_stage(nc, c, io, d):
    HALVES = CAP0 // P
    BODIES = E0 // DEEP
    with ExitStack() as ctx:
        st = Store(nc, ctx, "e0")
        s = st.sems("table_in table_f table_T idx_made turned xT_out h silu gated y y_out " +
                    " ".join(f"w{i} rows{i} saved{i}" for i in range(DEEP)))
        table, table_f = st.sb("table", [P, P], U32), st.sb("table_f", [P, P])
        idx_all = st.sb("idx_all", [P, P], U32)
        idx = [st.sb(f"idx{i}", [P, HALVES], U32) for i in range(DEEP)]
        carry = st.sb("carry", [P, DEEP])
        rows = [st.sb(f"rows{i}", [P, HALVES, D]) for i in range(DEEP)]
        w1 = [st.sb(f"w1{i}", [P, KD, 2 * I0]) for i in range(DEEP)]
        w2 = [st.sb(f"w2{i}", [P, D]) for i in range(DEEP)]
        y = [st.sb(f"y{i}", [P, HALVES, D]) for i in range(DEEP)]
        xT = [st.sb(f"xT{i}", [P, KD, CAP0]) for i in range(2)]
        sg, g = [st.sb(f"sg{i}", [P, CAP0]) for i in range(2)], [st.sb(f"g{i}", [P, CAP0]) for i in range(2)]
        ps_x, ps_h, ps_y = [[st.ps(f"{n}{i}") for i in range(2)] for n in "xhy"]
        s_w, s_rows, s_saved = ([s[f"{n}{i}"] for i in range(DEEP)] for n in ("w", "rows", "saved"))
        y_out = d["y0"].rearrange("(e h p) f -> e p h f", p=P, h=HALVES)

        with nc.Block() as block:
            @block.sync
            def _(sp):
                sp.dma_start(table[:, :], d["table0"].rearrange("(g p) o -> g (p o)", p=P)).then_inc(s["table_in"], 16)
                with sp.Fori(0, BODIES) as body:
                    for i in range(DEEP):
                        e = body * DEEP + i
                        sp.wait_ge(s["y"], e + 1)
                        sp.dma_start(w1[i][:, :, :], at(io["L0_ffn_w1"], e).rearrange("(k p) f -> p k f", p=P)).then_inc(s_w[i], 16)
                        sp.dma_start(w2[i][:, :], at(io["L0_ffn_w2"], e)).then_inc(s_w[i], 16)

            @block.gpsimd
            def _(pool):
                pool.wait_ge(s["idx_made"], 1)
                with pool.Fori(0, BODIES) as body:
                    for i in range(DEEP):
                        e = body * DEEP + i
                        pool.wait_ge(s["turned"], e + 1)
                        nc.gpsimd.tensor_tensor(carry[:, i:i + 1], c["ones"][:, 0:1], c["ones"][:, 0:1], ALU.mult)
                        nc.gpsimd.tensor_copy(idx[i][:, :], idx_all[:, bass.ds(e * HALVES, HALVES)])
                        nc.gpsimd.drain()
                        for h in range(HALVES):
                            nc.gpsimd.indirect_dma_start(out=rows[i][:, h, :], out_offset=None, in_=d["xn1"],
                                                         in_offset=bass.IndirectOffsetOnAxis(ap=idx[i][:, h:h + 1], axis=0),
                                                         ).then_inc(s_rows[i], 16)

            @block.tensor
            def _(pe):
                pe.sem_inc(s["turned"], DEEP)
                pe.sem_inc(s["y"], DEEP)
                pe.wait_ge(s["table_f"], 1)
                nc.tensor.transpose(ps_x[0][:, 0:P], table_f[:, :], c["ident"][:, :]).then_inc(s["table_T"], 1)
                pe.wait_ge(s["idx_made"], 1)

                def turn(body, i):
                    e = body * DEEP + i
                    pe.wait_ge(s_rows[i], body * (16 * HALVES) + 16 * HALVES)
                    pe.wait_ge(s["xT_out"], e + 1)
                    for k in range(KD):
                        for h in range(HALVES):
                            last = nc.tensor.transpose(ps_x[i % 2][:, k * CAP0 + h * P:k * CAP0 + (h + 1) * P],
                                                       rows[i][:, h, k * P:(k + 1) * P], c["ident"][:, :])
                    last.then_inc(s["turned"], 1)

                def first(body, i):
                    e = body * DEEP + i
                    pe.wait_ge(s_w[i], body * 32 + 32)
                    pe.wait_ge(s["xT_out"], e + 1 + 2)
                    pe.wait_ge(s["gated"], e + 1)
                    for m in range(2):
                        for k in range(KD):
                            last = nc.tensor.matmul(ps_h[i % 2][:, m * CAP0:(m + 1) * CAP0], w1[i][:, k, m * I0:(m + 1) * I0],
                                                    xT[i % 2][:, k, :], start=k == 0, stop=k == KD - 1)
                    last.then_inc(s["h"], 1)

                def second(body, i):
                    e = body * DEEP + i
                    pe.wait_ge(s["gated"], e + 1 + 2)
                    pe.wait_ge(s["y_out"], e + 1)
                    for h in range(HALVES):
                        last = nc.tensor.matmul(ps_y[i % 2][:, h * D:(h + 1) * D], g[i % 2][:, h * P:(h + 1) * P], w2[i][:, :],
                                                start=True, stop=True)
                    last.then_inc(s["y"], 1)

                turn(0, 0)
                for i in range(DEEP):
                    first(0, i)
                    turn((0, 1)[i == DEEP - 1], (i + 1) % DEEP)
                    if i >= 1:
                        second(0, i - 1)
                with pe.Fori(1, BODIES - 1) as body:
                    for i in range(DEEP):
                        first(body, i)
                        turn(body + 1 if i == DEEP - 1 else body, (i + 1) % DEEP)
                        second(body - 1 if i == 0 else body, (i - 1) % DEEP)
                for i in range(DEEP):
                    first(BODIES - 1, i)
                    if i < DEEP - 1:
                        turn(BODIES - 1, i + 1)
                    second(BODIES - 2 if i == 0 else BODIES - 1, (i - 1) % DEEP)
                second(BODIES - 1, DEEP - 1)

            @block.scalar
            def _(act):
                act.sem_inc(s["y_out"], 2)
                for i in range(DEEP):
                    act.sem_inc(s_saved[i], 16)

                def silu(body, i):
                    act.wait_ge(s["h"], body * DEEP + i + 1)
                    act.wait_ge(s["gated"], body * DEEP + i + 1)
                    nc.scalar.activation(sg[i % 2][:, :], ps_h[i % 2][:, 0:CAP0], ACT.Silu).then_inc(s["silu"], 1)

                def leave(body, i):
                    e = body * DEEP + i
                    act.wait_ge(s["y"], e + 1 + DEEP)
                    act.wait_ge(s_saved[i], body * 16 + 16)
                    nc.scalar.copy(y[i][:, :, :], ps_y[i % 2][:, :].rearrange("p (h f) -> p h f", h=HALVES)).then_inc(s["y_out"], 1)
                    act.wait_ge(s["y_out"], e + 1 + 2)
                    act.dma_start(at(y_out, e), y[i][:, :, :]).then_inc(s_saved[i], 16)

                for i in range(DEEP):
                    silu(0, i)
                    if i >= 1:
                        leave(0, i - 1)
                with act.Fori(1, BODIES) as body:
                    for i in range(DEEP):
                        silu(body, i)
                        leave(body - 1 if i == 0 else body, (i - 1) % DEEP)
                leave(BODIES - 1, DEEP - 1)
                for i in range(DEEP):
                    act.wait_ge(s_saved[i], 16 * BODIES + 16)

            @block.vector
            def _(dve):
                dve.sem_inc(s["xT_out"], 2)
                dve.sem_inc(s["gated"], 2)
                dve.wait_ge(s["table_in"], 16)
                nc.vector.tensor_copy(table_f[:, :], table[:, :]).then_inc(s["table_f"], 1)
                dve.wait_ge(s["table_T"], 1)
                nc.vector.tensor_copy(idx_all[:, :], ps_x[0][:, 0:P]).then_inc(s["idx_made"], 1)

                def xT_copy(body, i):
                    e = body * DEEP + i
                    dve.wait_ge(s["turned"], e + 1 + DEEP)
                    if not (isinstance(body, int) and e < 2):
                        dve.wait_ge(s["h"], e - 1)
                    nc.vector.tensor_copy(xT[i % 2][:, :, :], ps_x[i % 2][:, :].rearrange("p (k s) -> p k s", k=KD)).then_inc(s["xT_out"], 1)

                def gate(body, i):
                    e = body * DEEP + i
                    dve.wait_ge(s["silu"], e + 1)
                    dve.wait_ge(s["y"], e + 1 + DEEP - 2)
                    nc.vector.tensor_tensor(g[i % 2][:, :], sg[i % 2][:, :], ps_h[i % 2][:, CAP0:2 * CAP0], ALU.mult).then_inc(s["gated"], 1)

                xT_copy(0, 0)
                for i in range(1, DEEP):
                    xT_copy(0, i)
                    gate(0, i - 1)
                with dve.Fori(1, BODIES) as body:
                    for i in range(DEEP):
                        xT_copy(body, i)
                        gate(body - 1 if i == 0 else body, (i - 1) % DEEP)
                gate(BODIES - 1, DEEP - 1)


def combine0_stage(nc, c, io, d):
    R = NT * TOP0
    with ExitStack() as ctx:
        st = Store(nc, ctx, "c0")
        s = st.sems("x_in slots_in slots_copied rows added normed turned xT_out x_saved xT_saved")
        slots, slots2 = st.sb("slots", [P, R], U32), st.sb("slots2", [P, R], U32)
        weight, weight2 = st.sb("weight", [P, R]), st.sb("weight2", [P, R])
        x4, xn = st.sb("x4", [P, NT, D]), st.sb("xn", [P, NT, D])
        rows = st.sb("rows", [P, R, D])
        xT = st.sb("xT", [P, KD, S])
        nb = norm_buffers(st)
        ps_x = [st.ps(f"x{i}") for i in range(KD)]
        with nc.Block() as block:
            @block.sync
            def _(sp):
                with sp.Fori(0, B) as b:
                    sp.wait_ge(s["slots_copied"], b)
                    sp.dma_start(slots[:, :], at(d["slots0"], b)).then_inc(s["slots_in"], 16)
                    sp.dma_start(weight[:, :], at(d["weights0"], b)).then_inc(s["slots_in"], 16)
                    sp.wait_ge(s["x_saved"], 16 * b)
                    sp.wait_ge(s["normed"], b)
                    sp.dma_start(x4[:, :, :], at(d["x1"], b).rearrange("(t p) f -> p t f", p=P)).then_inc(s["x_in"], 16)
                    sp.wait_ge(s["added"], b + 1)
                    sp.dma_start(at(d["x2"], b).rearrange("(t p) f -> p t f", p=P), x4[:, :, :]).then_inc(s["x_saved"], 16)
                    sp.wait_ge(s["xT_out"], KD * (b + 1))
                    sp.dma_start(at(d["xT2"], b).rearrange("(k p) s -> p k s", p=P), xT[:, :, :]).then_inc(s["xT_saved"], 16)
                sp.wait_ge(s["x_saved"], 16 * B)
                sp.wait_ge(s["xT_saved"], 16 * B)

            @block.gpsimd
            def _(pool):
                with pool.Fori(0, B) as b:
                    pool.wait_ge(s["slots_in"], 32 * b + 32)
                    pool.wait_ge(s["added"], b)
                    nc.gpsimd.tensor_tensor(slots2[:, :], slots[:, :], c["zeros"][:, 0:R].bitcast(U32), ALU.add)
                    nc.gpsimd.tensor_tensor(weight2[:, :], weight[:, :], c["ones"][:, 0:R], ALU.mult).then_inc(s["slots_copied"], 1)
                    nc.gpsimd.drain()
                    for r in range(R):
                        nc.gpsimd.indirect_dma_start(out=rows[:, r, :], out_offset=None, in_=d["y0"],
                                                     in_offset=bass.IndirectOffsetOnAxis(ap=slots2[:, r:r + 1], axis=0),
                                                     ).then_inc(s["rows"], 16)

            @block.tensor
            def _(pe):
                with pe.Fori(0, B) as b:
                    pe.wait_ge(s["normed"], b + 1)
                    pe.wait_ge(s["xT_out"], KD * b)
                    for k in range(KD):
                        for t in range(NT):
                            last = nc.tensor.transpose(ps_x[k][:, t * P:(t + 1) * P], xn[:, t, k * P:(k + 1) * P], c["ident"][:, :])
                    last.then_inc(s["turned"], 1)

            @block.scalar
            def _(act):
                with act.Fori(0, B) as b:
                    act.wait_ge(s["turned"], b + 1)
                    act.wait_ge(s["xT_saved"], 16 * b)
                    for k in range(KD):
                        nc.scalar.copy(xT[:, k, :], ps_x[k][:, :]).then_inc(s["xT_out"], 1)

            @block.vector
            def _(dve):
                with dve.Fori(0, B) as b:
                    dve.wait_ge(s["x_in"], 16 * b + 16)
                    dve.wait_ge(s["slots_copied"], b + 1)
                    dve.wait_ge(s["rows"], 16 * R * (b + 1))
                    for j in range(TOP0):
                        for t in range(NT):
                            r = t * TOP0 + j
                            last = nc.vector.scalar_tensor_tensor(out=x4[:, t, :], in0=rows[:, r, :], scalar=weight2[:, r:r + 1],
                                                                  in1=x4[:, t, :], op0=ALU.mult, op1=ALU.add)
                        nc.vector.drain() if j < TOP0 - 1 else last.then_inc(s["added"], 1)
                    nc.vector.drain()
                    dve.wait_ge(s["turned"], b)
                    layer_norm(nc, x4, *nb, xn, 1e-5).then_inc(s["normed"], 1)


def attention_stage(nc, c, io, d):
    with ExitStack() as ctx:
        st = Store(nc, ctx, "a1")
        s = st.sems("in0 in1 group grouped scores maxed exped turned evac_d evac_a pv o_copied spread "
                    "recip_mm normed saved0 saved1")
        W = 4 * DH1
        x = [st.sb(f"x{i}", [P, KD, S]) for i in range(2)]
        y = [st.sb(f"y{i}", [P, KD, S]) for i in range(2)]
        wq, wk, wv = ([st.sb(f"{n}{i}", [P, KD, W]) for i in range(2)] for n in ("wq", "wk", "wv"))
        qz = st.sb("qz", [P, 4, S])
        kT = st.sb("kT", [P, 2, S])
        v = st.sb("v", [P, NT, W])
        prob = [st.sb(f"prob{i}", [P, S]) for i in range(DEEP)]
        nmax, total = st.sb("nmax", [P, BODY]), st.sb("total", [P, BODY])
        recip, spread = st.sb("recip", [P, NU]), st.sb("spread", [P, 2, NT, 2, DH1])
        pT = [st.sb(f"pT{i}", [P, NT, S]) for i in range(2)]
        o_sb = [st.sb(f"o_sb{i}", [P, S]) for i in range(2)]
        o_n = [st.sb(f"o_n{i}", [P, 2, S]) for i in range(2)]
        ps_s = [st.ps(f"s{i}") for i in range(2)]
        ps_t = [st.ps(f"t{i}") for i in range(2)]
        ps_o = [st.ps(f"o{i}") for i in range(2)]
        ps_r = st.ps("r")
        ps_p = st.ps("p")
        s_in, s_saved = (s["in0"], s["in1"]), (s["saved0"], s["saved1"])
        LOADS = 5
        STEPS1 = NU + LAG_N + 3

        with nc.Block() as block:
            @block.sync
            def _(sp):
                def load(b, quad, par):
                    cols = slice(quad * W, (quad + 1) * W)
                    sp.dma_start(x[par][:, :, :], at(d["xT2"], b).rearrange("(k p) s -> p k s", p=P)).then_inc(s_in[par], 16)
                    sp.dma_start(y[par][:, :, :], at(d["ctxT"], b).rearrange("(k p) s -> p k s", p=P)).then_inc(s_in[par], 16)
                    for dst, src in ((wq, io["L1_xattn_w_q"]), (wk, io["L1_xattn_w_k"]), (wv, io["L1_xattn_w_v"])):
                        sp.dma_start(dst[par][:, :, :], src[:, cols].rearrange("(k p) f -> p k f", p=P)).then_inc(s_in[par], 16)

                def save(b, quad, par):
                    sp.wait_ge(s["normed"], b * (2 * QUADS) + 2 * quad + 2 + 1)
                    sp.dma_start(at(d["o1"], b)[quad].rearrange("(a p) s -> p a s", p=P), o_n[par][:, :, :]).then_inc(s_saved[par], 16)

                sp.sem_inc(s["saved0"], 16)
                sp.sem_inc(s["saved1"], 16)
                with sp.Fori(0, B) as b:
                    for quad in range(QUADS):
                        sp.wait_ge(s["group"], (b * QUADS + quad) * 6 + 6)
                        load(b, quad, quad % 2)
                        if quad >= 1:
                            save(b, quad - 1, (quad - 1) % 2)
                    save(b, QUADS - 1, 1)
                for par in range(2):
                    sp.wait_ge(s_saved[par], 16 * (ITEMS // 2) + 16)

            @block.tensor
            def _(pe):
                pe.sem_inc(s["turned"], DEEP)
                pe.sem_inc(s["pv"], 2)
                pe.sem_inc(s["group"], 12)
                with pe.Fori(0, ITEMS // 2) as body:
                    for par in range(2):
                        i0 = body * 2 + par
                        u0 = body * BODY + par * NU
                        pe.wait_ge(s_in[par], body * (LOADS * 16) + LOADS * 16)
                        for g in range(6):
                            pe.wait_ge(s["grouped"], i0 * 6 + g + 1)
                            if g < 4:
                                wt, src = ((wq, x), (wk, y))[g % 2]
                                for k in range(KD):
                                    last = nc.tensor.matmul(ps_p[:, :], wt[par][:, k, g // 2 * P:(g // 2 + 1) * P], src[par][:, k, :],
                                                            start=k == 0, stop=k == KD - 1)
                            else:
                                for t in range(2):
                                    tile = (g - 4) * 2 + t
                                    for k in range(KD):
                                        last = nc.tensor.matmul(ps_p[:, t * W:(t + 1) * W], y[par][:, k, tile * P:(tile + 1) * P],
                                                                wv[par][:, k, :], start=k == 0, stop=k == KD - 1)
                            last.then_inc(s["group"], 1)
                        for step in range(STEPS1):
                            w = step
                            if w < NU:
                                h, t = w // NT, w % NT
                                if w == 0:
                                    pe.wait_ge(s["grouped"], i0 * 6 + 6 + 1)
                                pe.wait_ge(s["exped"], u0 + w + 1 + DEEP - 2)
                                last = nc.tensor.matmul(ps_s[w % 2][:, :], qz[:, h, t * P:(t + 1) * P], kT[:, h // 2, :],
                                                        start=True, stop=True)
                                last.then_inc(s["scores"], 1)
                            w = step - LAG_T
                            if 0 <= w < NU:
                                pe.wait_ge(s["exped"], u0 + w + 1 + DEEP)
                                pe.wait_ge((s["evac_d"], s["evac_a"])[w % 2], i0 * (NU // 2) + w // 2 + 1)
                                for k in range(NT):
                                    last = nc.tensor.transpose(ps_t[w % 2][:, k * P:(k + 1) * P],
                                                               prob[w % DEEP][:, k * P:(k + 1) * P], c["ident"][:, :])
                                last.then_inc(s["turned"], 1)
                            w = step - LAG_V
                            if 0 <= w < NU and w % NT == NT - 1:
                                h = w // NT
                                pe.wait_ge(s["evac_d"], i0 * (NU // 2) + w // 2 + 1 + 1)
                                pe.wait_ge(s["evac_a"], i0 * (NU // 2) + w // 2 + 1 + 1)
                                if h % 2 == 0:
                                    pe.wait_ge(s["o_copied"], i0 * 2 + h // 2 + 1)
                                for k in range(NT):
                                    last = nc.tensor.matmul(ps_o[h // 2][h % 2 * DH1:(h % 2 + 1) * DH1, :],
                                                            v[:, k, h * DH1:(h + 1) * DH1], pT[h % 2][:, k, :],
                                                            start=k == 0, stop=k == NT - 1)
                                last.then_inc(s["pv"], 1)
                            w = step - LAG_N
                            if 0 <= w < NU and w % (2 * NT) == 2 * NT - 1:
                                a = w // (2 * NT)
                                pe.wait_ge(s["spread"], i0 * 2 + a + 1)
                                pe.wait_ge(s["normed"], i0 * 2 + a + 1)
                                for t in range(NT):
                                    last = nc.tensor.matmul(ps_r[:, t * P:(t + 1) * P],
                                                            spread[:, a, t, :, :].rearrange("p h f -> p (h f)"), c["ident"][:, :],
                                                            start=True, stop=True)
                                last.then_inc(s["recip_mm"], 1)

            @block.vector
            def _(dve):
                dve.sem_inc(s["evac_d"], 1)
                dve.sem_inc(s["normed"], 1)
                dve.sem_inc(s["grouped"], 1)
                nc.vector.memset(qz[:, :, :].rearrange("p h s -> p (h s)"), 0.0)
                nc.vector.drain()
                with dve.Fori(0, ITEMS // 2) as body:
                    for par in range(2):
                        i0 = body * 2 + par
                        u0 = body * BODY + par * NU
                        for g in range(6):
                            dve.wait_ge(s["group"], i0 * 6 + g + 1 + 12)
                            if g < 4 and g % 2 == 0:
                                for h in range(2):
                                    rows = slice(h * DH1, (h + 1) * DH1)
                                    last = nc.vector.tensor_scalar(qz[rows, g + h, :], ps_p[rows, :], DH1 ** -0.5, None, ALU.mult)
                            elif g < 4:
                                last = nc.vector.tensor_copy(kT[:, g // 2, :], ps_p[:, :])
                            else:
                                last = nc.vector.tensor_copy(v[:, (g - 4) * 2:(g - 4) * 2 + 2, :],
                                                             ps_p[:, :].rearrange("p (t f) -> p t f", t=2))
                            last.then_inc(s["grouped"], 1)
                        for step in range(STEPS1):
                            w = step
                            if w < NU:
                                dve.wait_ge(s["scores"], u0 + w + 1)
                                nc.vector.tensor_reduce(nmax[:, par * NU + w:par * NU + w + 1], ps_s[w % 2][:, :], AX, ALU.max,
                                                        negate=True).then_inc(s["maxed"], 1)
                            w = step - LAG_T
                            if 0 <= w < NU and w % 2 == 0:
                                dve.wait_ge(s["turned"], u0 + w + 1 + DEEP)
                                if w % NT == 0:
                                    dve.wait_ge(s["pv"], i0 * 4 + w // NT + 1)
                                nc.vector.tensor_copy(pT[w // NT % 2][:, :, w % NT * P:(w % NT + 1) * P],
                                                      ps_t[0][:, :].rearrange("p (k s) -> p k s", k=NT)).then_inc(s["evac_d"], 1)
                            if 0 <= w < NU and w % (2 * NT) == 2 * NT - 1:
                                a = w // (2 * NT)
                                pair = slice(a * 2 * NT, (a + 1) * 2 * NT)
                                dve.wait_ge(s["exped"], u0 + (a + 1) * 2 * NT + DEEP)
                                dve.wait_ge(s["recip_mm"], i0 * 2 + a - 1 + 1)
                                nc.vector.reciprocal(recip[:, pair], total[:, par * NU + a * 2 * NT:par * NU + (a + 1) * 2 * NT])
                                nc.vector.drain()
                                nc.vector.tensor_copy(spread[:, a, :, :, :],
                                                      recip[:, pair].rearrange("p (h t o) -> p t h o", h=2, o=1)
                                                      .to_broadcast([P, NT, 2, DH1])).then_inc(s["spread"], 1)
                            w = step - LAG_N - 1
                            if 0 <= w < NU and w % (2 * NT) == 2 * NT - 1:
                                a = w // (2 * NT)
                                dve.wait_ge(s["recip_mm"], i0 * 2 + a + 1)
                                dve.wait_ge(s["o_copied"], i0 * 2 + a + 1 + 2)
                                dve.wait_ge(s_saved[par], body * 16 + 16)
                                nc.vector.tensor_tensor(o_n[par][:, a, :], o_sb[a][:, :], ps_r[:, :], ALU.mult).then_inc(s["normed"], 1)

            @block.scalar
            def _(act):
                act.sem_inc(s["exped"], DEEP)
                act.sem_inc(s["evac_a"], 1)
                act.sem_inc(s["o_copied"], 2)
                with act.Fori(0, ITEMS // 2) as body:
                    for par in range(2):
                        i0 = body * 2 + par
                        u0 = body * BODY + par * NU
                        for step in range(STEPS1):
                            w = step
                            if w < NU:
                                act.wait_ge(s["maxed"], u0 + w + 1)
                                act.wait_ge(s["turned"], u0 + w + 1)
                                col = slice(par * NU + w, par * NU + w + 1)
                                nc.scalar.activation(prob[w % DEEP][:, :], ps_s[w % 2][:, :], ACT.Exp, bias=nmax[:, col],
                                                     accum_out=total[:, col]).then_inc(s["exped"], 1)
                            w = step - LAG_T
                            if 0 <= w < NU and w % 2 == 1:
                                act.wait_ge(s["turned"], u0 + w + 1 + DEEP)
                                if w % NT == 1:
                                    act.wait_ge(s["pv"], i0 * 4 + w // NT + 1)
                                nc.scalar.copy(pT[w // NT % 2][:, :, w % NT * P:(w % NT + 1) * P],
                                               ps_t[1][:, :].rearrange("p (k s) -> p k s", k=NT)).then_inc(s["evac_a"], 1)
                            w = step - LAG_N
                            if 0 <= w < NU and w % (2 * NT) == 2 * NT - 1:
                                a = w // (2 * NT)
                                act.wait_ge(s["pv"], i0 * 4 + a * 2 + 2 + 2)
                                act.wait_ge(s["normed"], i0 * 2 + a)
                                nc.scalar.copy(o_sb[a][:, :], ps_o[a][:, :]).then_inc(s["o_copied"], 1)


def route1_stage(nc, c, io, d):
    GC = E1 + 2
    with ExitStack() as ctx:
        st = Store(nc, ctx, "r1")
        s = st.sems("w_in o_in x_in product summed normed affine turned xT_out logits maxed exped picked counted placed "
                    "h h_out m m_out scattered base_saved a_saved slots_saved table_zero")
        KO = HEADS * DH1 // P
        wo = st.sb("wo", [P, KO, D])
        wg = st.sb("wg", [P, KD, GC])
        w1, w2 = st.sb("w1", [P, KD, I1]), st.sb("w2", [P, KI, D])
        b1, b2 = st.sb("b1", [P, KI]), st.sb("b2", [P, D])
        nw, nbias = st.sb("nw", [P, D]), st.sb("nbias", [P, D])
        o4, x4 = st.sb("o4", [P, KO, S]), st.sb("x4", [P, NT, D])
        x3, xn, a = st.sb("x3", [P, NT, D]), st.sb("xn", [P, NT, D]), st.sb("a", [P, NT, D])
        xT = st.sb("xT", [P, KD, S])
        hT = st.sb("hT", [P, KI, S])
        mix, nmix, emix, smix = st.sb("mix", [P, NT, 2]), st.sb("nmix", [P, NT]), st.sb("emix", [P, NT, 2]), st.sb("smix", [P, NT])
        nb = norm_buffers(st)
        r = Router(nc, st, c, E1, TOP1, CAP1, drop=True)
        ps_y = [st.ps(f"y{i}") for i in range(2)]
        ps_x = [st.ps(f"x{i}") for i in range(KD)]
        ps_l, ps_p = st.ps("l"), st.ps("p")
        ps_h = [st.ps(f"h{i}") for i in range(2)]
        both = ps_l[:, 0:NT * GC].rearrange("p (t e) -> p t e", t=NT)
        logits, mixes = both[:, :, 0:E1], both[:, :, E1:GC]

        with nc.Block() as block:
            @block.sync
            def _(sp):
                def load_x(b):
                    sp.dma_start(o4[:, :, :], at(d["o1"].rearrange("b q f s -> b (q f) s"), b).rearrange("(k p) s -> p k s", p=P)).then_inc(s["o_in"], 16)
                    sp.dma_start(x4[:, :, :], at(d["x2"], b).rearrange("(t p) f -> p t f", p=P)).then_inc(s["x_in"], 16)

                for dst, src in ((wo[:, :, :], io["L1_xattn_w_o"].rearrange("(k p) f -> p k f", p=P)),
                                 (w1[:, :, :], io["L1_ffn_res_inter_w"].rearrange("(k p) f -> p k f", p=P)),
                                 (w2[:, :, :], io["L1_ffn_res_output_w"].rearrange("(k p) f -> p k f", p=P)),
                                 (b2[:, :], io["L1_ffn_res_output_b"].rearrange("(a f) -> a f", a=1).to_broadcast([P, D])),
                                 (nw[:, :], io["L1_ffn_attn_nw"].rearrange("(a f) -> a f", a=1).to_broadcast([P, D])),
                                 (nbias[:, :], io["L1_ffn_attn_nb"].rearrange("(a f) -> a f", a=1).to_broadcast([P, D]))):
                    sp.dma_start(dst, src).then_inc(s["w_in"], 16)
                with nc.allow_non_contiguous_dma(reason="small columns"):
                    sp.dma_start(b1[:, :], io["L1_ffn_res_inter_b"].rearrange("(k p) -> p k", p=P)).then_inc(s["w_in"], 16)
                    sp.dma_start(wg[:, :, 0:E1], io["L1_ffn_wg"].rearrange("(k p) e -> p k e", p=P)).then_inc(s["w_in"], 16)
                    sp.dma_start(wg[:, :, E1:GC], io["L1_ffn_res_coef"].rearrange("(k p) e -> p k e", p=P)).then_inc(s["w_in"], 16)
                sp.dma_start(d["table1"].rearrange("(p k) o -> p (k o)", p=P), c["zeros"][:, 0:E1 * CAP1 // P].bitcast(U32)).then_inc(s["table_zero"], 16)
                with sp.Fori(0, B) as b:
                    sp.wait_ge(s["summed"], b)
                    load_x(b)
                    sp.wait_ge(s["affine"], b + 1)
                    sp.dma_start(at(d["a1"].rearrange("(b s) f -> b s f", b=B), b).rearrange("(t p) f -> p t f", p=P), a[:, :, :]).then_inc(s["a_saved"], 16)
                    sp.wait_ge(s["placed"], b + 1)
                    sp.dma_start(at(d["slots1"], b), r.slot_read[:, :]).then_inc(s["slots_saved"], 16)
                    sp.dma_start(at(d["weights1"], b), r.weight[:, :]).then_inc(s["slots_saved"], 16)
                    sp.wait_ge(s["m_out"], 2 * b + 2)
                    sp.dma_start(at(d["base"], b).rearrange("(t p) f -> p t f", p=P), x3[:, :, :]).then_inc(s["base_saved"], 16)
                sp.wait_ge(s["base_saved"], 16 * B)
                sp.wait_ge(s["a_saved"], 16 * B)
                sp.wait_ge(s["slots_saved"], 32 * B)

            @block.gpsimd
            def _(pool):
                pool.wait_ge(s["table_zero"], 16)
                with pool.Fori(0, B) as b:
                    pool.wait_ge(s["scattered"], 16 * r.R * b)
                    pool.wait_ge(s["placed"], b + 1)
                    r.scatter(d["table1"], s["scattered"])
                pool.wait_ge(s["scattered"], 16 * r.R * B)

            @block.tensor
            def _(pe):
                pe.wait_ge(s["w_in"], 16 * 9)
                with pe.Fori(0, B) as b:
                    pe.wait_ge(s["o_in"], 16 * b + 16)
                    pe.wait_ge(s["m_out"], 2 * b)
                    for t in range(NT):
                        for k in range(KO):
                            last = nc.tensor.matmul(ps_y[t // 2][:, t % 2 * D:(t % 2 + 1) * D], o4[:, k, t * P:(t + 1) * P],
                                                    wo[:, k, :], start=k == 0, stop=k == KO - 1)
                        if t % 2:
                            last.then_inc(s["product"], 1)
                    pe.wait_ge(s["affine"], b + 1)
                    for k in range(KD):
                        for t in range(NT):
                            last = nc.tensor.transpose(ps_x[k][:, t * P:(t + 1) * P], a[:, t, k * P:(k + 1) * P], c["ident"][:, :])
                    last.then_inc(s["turned"], 1)
                    pe.wait_ge(s["xT_out"], KD * (b + 1))
                    for t in range(NT):
                        for k in range(KD):
                            last = nc.tensor.matmul(ps_l[:, t * GC:(t + 1) * GC], xT[:, k, t * P:(t + 1) * P], wg[:, k, :],
                                                    start=k == 0, stop=k == KD - 1)
                    last.then_inc(s["logits"], 1)
                    for m in range(KI):
                        pe.wait_ge(s["h_out"], b * KI + m + 1)
                        for k in range(KD):
                            last = nc.tensor.matmul(ps_h[m % 2][:, :], w1[:, k, m * P:(m + 1) * P], xT[:, k, :],
                                                    start=k == 0, stop=k == KD - 1)
                        last.then_inc(s["h"], 1)
                    pe.wait_ge(s["picked"], b + 1)
                    r.count_earlier(ps_p).then_inc(s["counted"], 1)
                    pe.wait_ge(s["h_out"], b * KI + KI + 2)
                    for t in range(NT):
                        for m in range(KI):
                            last = nc.tensor.matmul(ps_y[t // 2][:, t % 2 * D:(t % 2 + 1) * D], hT[:, m, t * P:(t + 1) * P],
                                                    w2[:, m, :], start=m == 0, stop=m == KI - 1)
                        if t % 2:
                            last.then_inc(s["m"], 1)

            @block.scalar
            def _(act):
                act.wait_ge(s["w_in"], 16 * 9)
                act.sem_inc(s["h_out"], 2)
                with act.Fori(0, B) as b:
                    act.wait_ge(s["turned"], b + 1)
                    for k in range(KD):
                        nc.scalar.copy(xT[:, k, :], ps_x[k][:, :]).then_inc(s["xT_out"], 1)
                    act.wait_ge(s["maxed"], b + 1)
                    r.exponentials(logits)
                    for t in range(NT):
                        last = nc.scalar.activation(emix[:, t, :], mixes[:, t, :], ACT.Exp, bias=nmix[:, t:t + 1],
                                                    accum_out=smix[:, t:t + 1])
                    last.then_inc(s["exped"], 1)
                    act.wait_ge(s["m"], 2 * b)
                    for m in range(KI):
                        act.wait_ge(s["h"], b * KI + m + 1)
                        nc.scalar.activation(hT[:, m, :], ps_h[m % 2][:, :], ACT.Gelu_apprx_tanh, bias=b1[:, m:m + 1]).then_inc(s["h_out"], 1)

            @block.vector
            def _(dve):
                r.start()
                dve.wait_ge(s["w_in"], 16 * 9)
                with dve.Fori(0, B) as b:
                    dve.wait_ge(s["x_in"], 16 * b + 16)
                    dve.wait_ge(s["base_saved"], 16 * b)
                    for half in range(2):
                        dve.wait_ge(s["product"], 2 * b + half + 1)
                        last = nc.vector.tensor_tensor(x3[:, 2 * half:2 * half + 2, :], x4[:, 2 * half:2 * half + 2, :],
                                                       ps_y[half][:, :].rearrange("p (t f) -> p t f", t=2), ALU.add)
                    last.then_inc(s["summed"], 1)
                    nc.vector.drain()
                    layer_norm(nc, x3, *nb, xn, 1e-5)
                    nc.vector.drain()
                    for t in range(NT):
                        nc.vector.tensor_tensor(x3[:, t, :], x3[:, t, :], xn[:, t, :], ALU.add)
                    dve.wait_ge(s["turned"], b)
                    dve.wait_ge(s["a_saved"], 16 * b)
                    nc.vector.memset(r.sums[:, :], 0.0)
                    layer_norm(nc, xn, *nb, a, 1e-12)
                    nc.vector.drain()
                    for t in range(NT):
                        nc.vector.tensor_tensor(a[:, t, :], a[:, t, :], nw[:, :], ALU.mult)
                    nc.vector.drain()
                    for t in range(NT):
                        last = nc.vector.tensor_tensor(a[:, t, :], a[:, t, :], nbias[:, :], ALU.add)
                    last.then_inc(s["affine"], 1)
                    dve.wait_ge(s["logits"], b + 1)
                    nc.vector.tensor_reduce(r.nmax[:, :], logits, AX, ALU.max, negate=True)
                    nc.vector.tensor_reduce(nmix[:, :], mixes, AX, ALU.max, negate=True).then_inc(s["maxed"], 1)
                    dve.wait_ge(s["exped"], b + 1)
                    nc.vector.reciprocal(smix[:, :], smix[:, :])
                    r.pick().then_inc(s["picked"], 1)
                    nc.vector.tensor_tensor(mix[:, :, :], emix[:, :, :], r.tail(smix[:, :]).to_broadcast([P, NT, 2]), ALU.mult)
                    dve.wait_ge(s["slots_saved"], 32 * b)
                    dve.wait_ge(s["scattered"], 16 * r.R * b)
                    dve.wait_ge(s["counted"], b + 1)
                    r.place(ps_p)
                    nc.vector.drain()
                    nc.vector.tensor_tensor(r.weight[:, :], r.weight[:, :], mix[:, :, 1], ALU.mult).then_inc(s["placed"], 1)
                    for half in range(2):
                        dve.wait_ge(s["m"], 2 * b + half + 1)
                        rows = slice(2 * half, 2 * half + 2)
                        nc.vector.tensor_tensor(xn[:, rows, :], ps_y[half][:, :].rearrange("p (t f) -> p t f", t=2),
                                                b2[:, :].rearrange("p (o f) -> p o f", o=1).to_broadcast([P, 2, D]), ALU.add)
                        nc.vector.drain()
                        for t in range(2 * half, 2 * half + 2):
                            last = nc.vector.scalar_tensor_tensor(out=x3[:, t, :], in0=xn[:, t, :], scalar=mix[:, t, 0:1],
                                                                  in1=x3[:, t, :], op0=ALU.mult, op1=ALU.add)
                        last.then_inc(s["m_out"], 1)
                    nc.vector.drain()


def experts1_stage(nc, c, io, d):
    HALVES = CAP1 // P
    with ExitStack() as ctx:
        st = Store(nc, ctx, "e1")
        s = st.sems("idx_in w10 w11 w20 w21 b_in rows0 rows1 turned xT_out h h_out y y_out saved0 saved1")
        idx = st.sb("idx", [P, E1, HALVES], U32)
        b1, b2 = st.sb("b1", [P, E1, KI]), st.sb("b2", [P, E1, D])
        rows = [st.sb(f"rows{i}", [P, HALVES, D]) for i in range(2)]
        xT = [st.sb(f"xT{i}", [P, KD, CAP1]) for i in range(2)]
        w1 = [st.sb(f"w1{i}", [P, KD, I1]) for i in range(2)]
        w2 = [st.sb(f"w2{i}", [P, KI, D]) for i in range(2)]
        hT = [st.sb(f"hT{i}", [P, KI, CAP1]) for i in range(2)]
        y = [st.sb(f"y{i}", [P, HALVES, D]) for i in range(2)]
        ps_x = [st.ps(f"x{i}") for i in range(2)]
        ps_h = [st.ps(f"h{i}") for i in range(4)]
        ps_y = [st.ps(f"y{i}") for i in range(2)]
        s_w1, s_w2, s_rows, s_saved = (s["w10"], s["w11"]), (s["w20"], s["w21"]), (s["rows0"], s["rows1"]), (s["saved0"], s["saved1"])
        y_out = d["y1"].rearrange("(e h p) f -> e p h f", p=P, h=HALVES)

        with nc.Block() as block:
            @block.sync
            def _(sp):
                with nc.allow_non_contiguous_dma(reason="token numbers and biases"):
                    sp.dma_start(idx[:, :, :].rearrange("p e h -> p (e h)"), d["table1"].rearrange("(e p) o -> p (e o)", p=P)).then_inc(s["idx_in"], 16)
                    for e in range(E1):
                        sp.dma_start(b1[:, e, :], io["L1_ffn_inter_b"][e].rearrange("(k p) -> p k", p=P)).then_inc(s["b_in"], 16)
                for e in range(E1):
                    sp.dma_start(b2[:, e, :], io["L1_ffn_output_b"][e:e + 1, :].to_broadcast([P, D])).then_inc(s["b_in"], 16)
                for e in range(E1):
                    par = e % 2
                    if e >= 2:
                        sp.wait_ge(s["y"], e - 1)
                    sp.dma_start(w1[par][:, :, :], io["L1_ffn_inter_w"][e].rearrange("(k p) f -> p k f", p=P)).then_inc(s_w1[par], 16)
                    sp.dma_start(w2[par][:, :, :], io["L1_ffn_output_w"][e].rearrange("(k p) f -> p k f", p=P)).then_inc(s_w2[par], 16)

            @block.gpsimd
            def _(pool):
                pool.wait_ge(s["idx_in"], 16)
                for e in range(E1):
                    if e >= 2:
                        pool.wait_ge(s["turned"], e - 1)
                    for h in range(HALVES):
                        nc.gpsimd.indirect_dma_start(out=rows[e % 2][:, h, :], out_offset=None, in_=d["a1"],
                                                     in_offset=bass.IndirectOffsetOnAxis(ap=idx[:, e, h:h + 1], axis=0),
                                                     ).then_inc(s_rows[e % 2], 16)

            @block.tensor
            def _(pe):
                def turn(e):
                    pe.wait_ge(s_rows[e % 2], 16 * HALVES * (e // 2 + 1))
                    if e >= 2:
                        pe.wait_ge(s["xT_out"], e - 1)
                    for k in range(KD):
                        for h in range(HALVES):
                            last = nc.tensor.transpose(ps_x[e % 2][:, k * CAP1 + h * P:k * CAP1 + (h + 1) * P],
                                                       rows[e % 2][:, h, k * P:(k + 1) * P], c["ident"][:, :])
                    last.then_inc(s["turned"], 1)

                turn(0)
                for e in range(E1):
                    par = e % 2
                    pe.wait_ge(s_w1[par], 16 * (e // 2 + 1))
                    pe.wait_ge(s["xT_out"], e + 1)
                    for m in range(KI):
                        if m % 2 == 0 and e >= 1:
                            pe.wait_ge(s["h_out"], (e - 1) * KI + m + 2)
                        for k in range(KD):
                            last = nc.tensor.matmul(ps_h[m // 2][:, m % 2 * CAP1:(m % 2 + 1) * CAP1], w1[par][:, k, m * P:(m + 1) * P],
                                                    xT[par][:, k, :], start=k == 0, stop=k == KD - 1)
                        if m % 2:
                            last.then_inc(s["h"], 1)
                    if e + 1 < E1:
                        turn(e + 1)
                    pe.wait_ge(s_w2[par], 16 * (e // 2 + 1))
                    if e >= 2:
                        pe.wait_ge(s["y_out"], e - 1)
                    pe.wait_ge(s["h_out"], (e + 1) * KI)
                    for h in range(HALVES):
                        for m in range(KI):
                            last = nc.tensor.matmul(ps_y[par][:, h * D:(h + 1) * D], hT[par][:, m, h * P:(h + 1) * P], w2[par][:, m, :],
                                                    start=m == 0, stop=m == KI - 1)
                    last.then_inc(s["y"], 1)

            @block.scalar
            def _(act):
                act.wait_ge(s["b_in"], 16 * 2 * E1)
                for e in range(E1):
                    par = e % 2
                    if e >= 2:
                        act.wait_ge(s["y"], e - 1)
                    for m in range(KI):
                        if m % 2 == 0:
                            act.wait_ge(s["h"], e * (KI // 2) + m // 2 + 1)
                        nc.scalar.activation(hT[par][:, m, :], ps_h[m // 2][:, m % 2 * CAP1:(m % 2 + 1) * CAP1],
                                             ACT.Gelu_apprx_tanh, bias=b1[:, e, m:m + 1]).then_inc(s["h_out"], 1)
                    if e >= 1:
                        act.wait_ge(s["y_out"], e)
                        act.dma_start(y_out[e - 1], y[1 - par][:, :, :]).then_inc(s_saved[1 - par], 16)
                act.wait_ge(s["y_out"], E1)
                act.dma_start(y_out[E1 - 1], y[1][:, :, :]).then_inc(s["saved1"], 16)
                act.wait_ge(s["saved0"], 16 * E1 // 2)
                act.wait_ge(s["saved1"], 16 * E1 // 2)

            @block.vector
            def _(dve):
                dve.wait_ge(s["b_in"], 16 * 2 * E1)

                def xT_copy(e):
                    dve.wait_ge(s["turned"], e + 1)
                    if e >= 2:
                        dve.wait_ge(s["h"], (e - 1) * (KI // 2))
                    nc.vector.tensor_copy(xT[e % 2][:, :, :], ps_x[e % 2][:, :].rearrange("p (k s) -> p k s", k=KD)).then_inc(s["xT_out"], 1)

                xT_copy(0)
                for e in range(E1):
                    if e + 1 < E1:
                        xT_copy(e + 1)
                    dve.wait_ge(s["y"], e + 1)
                    if e >= 2:
                        dve.wait_ge(s_saved[e % 2], 16 * (e // 2))
                    nc.vector.tensor_tensor(y[e % 2][:, :, :], ps_y[e % 2][:, :].rearrange("p (h f) -> p h f", h=HALVES),
                                            b2[:, e:e + 1, :].to_broadcast([P, HALVES, D]), ALU.add).then_inc(s["y_out"], 1)


def combine1_stage(nc, c, io, d, out):
    with ExitStack() as ctx:
        st = Store(nc, ctx, "c1")
        s = st.sems("x_in slots_in rows added saved")
        R = NT * TOP1
        slots, weight = st.sb("slots", [P, B, R], U32), st.sb("weight", [P, B, R])
        x = st.sb("x", [P, B, NT, D])
        rows = st.sb("rows", [P, B, R, D])
        with nc.Block() as block:
            @block.sync
            def _(sp):
                sp.dma_start(slots[:, :, :], d["slots1"].rearrange("b p r -> p b r")).then_inc(s["slots_in"], 16)
                sp.dma_start(weight[:, :, :], d["weights1"].rearrange("b p r -> p b r")).then_inc(s["slots_in"], 16)
                sp.dma_start(x[:, :, :, :].rearrange("p b t f -> p (b t) f"), d["base"].rearrange("b (t p) f -> p (b t) f", p=P)).then_inc(s["x_in"], 16)
                for b in range(B):
                    sp.wait_ge(s["added"], NT * (b + 1))
                    sp.dma_start(out[b].rearrange("(t p) f -> p t f", p=P), x[:, b]).then_inc(s["saved"], 16)
                sp.wait_ge(s["saved"], 16 * B)

            @block.gpsimd
            def _(pool):
                pool.wait_ge(s["slots_in"], 32)
                for b in range(B):
                    for r in range(R):
                        nc.gpsimd.indirect_dma_start(out=rows[:, b, r, :], out_offset=None, in_=d["y1"],
                                                     in_offset=bass.IndirectOffsetOnAxis(ap=slots[:, b, r:r + 1], axis=0),
                                                     ).then_inc(s["rows"], 16)

            @block.vector
            def _(dve):
                dve.wait_ge(s["x_in"], 16)
                dve.wait_ge(s["slots_in"], 32)
                dve.wait_ge(s["rows"], 16 * B * R)
                for b in range(B):
                    for t in range(NT):
                        nc.vector.scalar_tensor_tensor(out=x[:, b, t, :], in0=rows[:, b, t, :], scalar=weight[:, b, t:t + 1],
                                                       in1=x[:, b, t, :], op0=ALU.mult, op1=ALU.add).then_inc(s["added"], 1)


def build(nc, io, out, last_stage=None):
    def scratch(name, shape, dt=F32):
        return nc.dram_tensor(f"scratch_{name}", shape, dt, kind="Internal").ap()

    d = dict(
        ctxT=scratch("ctxT", (B, D, S)),
        qp=scratch("qp", (B, 3, D, S), BF16),
        kp=scratch("kp", (B, 3, D, S), BF16),
        v0=scratch("v0", (B, QUADS, S, 4 * PAD0)),
        o0=scratch("o0", (ITEMS, P, S)),
        x1=scratch("x1", (B, S, D)), xn1=scratch("xn1", (N, D)),
        slots0=scratch("slots0", (B, P, NT * TOP0), U32), weights0=scratch("weights0", (B, P, NT * TOP0)),
        table0=scratch("table0", (E0 * CAP0, 1), U32), y0=scratch("y0", (E0 * CAP0, D)),
        o1=scratch("o1", (B, QUADS, 4 * DH1, S)), a1=scratch("a1", (N, D)), base=scratch("base", (B, S, D)),
        slots1=scratch("slots1", (B, P, NT * TOP1), U32), weights1=scratch("weights1", (B, P, NT * TOP1)),
        table1=scratch("table1", (E1 * CAP1, 1), U32), y1=scratch("y1", (E1 * CAP1, D)),
        x2=scratch("x2", (B, S, D)), xT2=scratch("xT2", (B, D, S)),
    )
    with ExitStack() as ctx:
        st = Store(nc, ctx, "c")
        c = dict(ones=st.sb("ones", [P, P]), zeros=st.sb("zeros", [P, P]), ident=st.sb("ident", [P, P]),
                            ones16=st.sb("ones16", [P, P], BF16), before=st.sb("before", [P, P], BF16),
                            expert_no=st.sb("expert_no", [P, E0]), token_no=st.sb("token_no", [P, NT]))
        build_constants(nc, c)
        stages = [project_stage, masked_attention_stage, route0_stage, experts0_stage, combine0_stage,
                  attention_stage, route1_stage, experts1_stage]
        for stage in stages[:last_stage]:
            stage(nc, c, io, d)
        if last_stage is None:
            combine1_stage(nc, c, io, d, out)


_OUT_SHAPE = (B, S, D)


def kernel(**inputs):
    import numpy as np
    import concourse.bacc as bacc
    from concourse.bass_utils import run_bass_kernel_spmd

    nc = bacc.Bacc("TRN2", target_bir_lowering=False, num_devices=1)
    arrays = {f"in_{name}": np.ascontiguousarray(a) for name, a in inputs.items()}
    io = {
        name: nc.dram_tensor(f"in_{name}", inputs[name].shape, mybir.dt.from_np(arrays[f"in_{name}"].dtype),
                             kind="ExternalInput").ap() for name in inputs}
    out = nc.dram_tensor("out_0", _OUT_SHAPE, F32, kind="ExternalOutput").ap()
    build(nc, io, out)
    return run_bass_kernel_spmd(nc, [arrays], core_ids=[0]).results[0]["out_0"]
```

```python
from contextlib import ExitStack

import concourse.bass as bass
from concourse import mybir

P = 128
B, S, D = 4, 512, 256
N = B * S
NT = S // P
KD = D // P
HEADS = 16
DH0, PAD0 = 16, 32
DH1 = 64
QUADS = HEADS // 4
ITEMS = B * QUADS
E0, TOP0, I0, CAP0 = 64, 4, 128, 256
E1, TOP1, I1, CAP1 = 8, 1, 1024, 256
KI = I1 // P
SKIP = 1.0e6

F32 = mybir.dt.float32
BF16 = mybir.dt.bfloat16
U32 = mybir.dt.uint32
I32 = mybir.dt.int32
ALU = mybir.AluOpType
ACT = mybir.ActivationFunctionType
AX = mybir.AxisListType.X

Q_PARTS = (0, 0, 1, 0, 1, 2)
K_PARTS = (0, 1, 0, 2, 1, 0)
STACK = len(Q_PARTS) * DH0


class Store:

    def __init__(self, nc, ctx, prefix):
        self.nc, self.ctx, self.prefix = nc, ctx, prefix

    def sb(self, name, shape, dt=F32):
        return self.ctx.enter_context(self.nc.sbuf_tensor(f"{self.prefix}_{name}", shape, dt))

    def ps(self, name, shape=(P, 512), dt=F32):
        return self.ctx.enter_context(self.nc.psum_tensor(f"{self.prefix}_ps_{name}", list(shape), dt))

    def sems(self, names):
        return {n: self.nc.alloc_semaphore(f"{self.prefix}_{n}") for n in names.split()}


def build_constants(nc, c):
    filled, made = nc.alloc_semaphore("constants_filled"), nc.alloc_semaphore("constants_made")
    ones16_made = nc.alloc_semaphore("constants_ones16")
    with nc.Block() as block:
        @block.vector
        def _(dve):
            nc.vector.memset(c["ones"][:, :], 1.0)
            nc.vector.memset(c["zeros"][:, :], 0.0).then_inc(filled, 1)
            nc.vector.memset(c["ones16"][:, :], 1.0).then_inc(ones16_made, 1)
            dve.wait_ge(ones16_made, 1)

        @block.gpsimd
        def _(pool):
            pool.wait_ge(filled, 1)
            nc.gpsimd.affine_select(out=c["ident"][:, :], in_=c["ones"][:, :], compare_op=ALU.is_equal, fill=0.0, base=0,
                                    pattern=[[-1, P]], channel_multiplier=1).then_inc(made, 1)
            nc.gpsimd.affine_select(out=c["before"][:, :], in_=c["ones"][:, :], compare_op=ALU.is_gt, fill=0.0, base=0,
                                    pattern=[[1, P]], channel_multiplier=-1).then_inc(made, 1)
            nc.gpsimd.iota(c["expert_no"][:, :], pattern=[[1, E0]], base=0, channel_multiplier=0,
                           allow_small_or_imprecise_dtypes=True).then_inc(made, 1)
            nc.gpsimd.iota(c["token_no"][:, :], pattern=[[P, NT]], base=0, channel_multiplier=1,
                           allow_small_or_imprecise_dtypes=True).then_inc(made, 1)
            pool.wait_ge(made, 4)


def layer_norm(nc, x, stats, mv, var, half, rstd, out, eps):
    for t in range(NT):
        nc.vector.bn_stats(stats[:, t, :], x[:, t, :])
    nc.vector.drain()
    for t in range(NT):
        nc.vector.bn_aggr(mv[:, t, :], stats[:, t, :])
    nc.vector.drain()
    nc.vector.tensor_scalar(var[:, :], mv[:, :, 1], eps, None, ALU.add)
    nc.vector.drain()
    nc.vector.tensor_scalar(rstd[:, :].bitcast(I32), var[:, :].bitcast(I32), -0.5, float(0x5F3759DF), ALU.mult, ALU.add)
    nc.vector.drain()
    for _ in range(3):
        nc.vector.tensor_tensor(half[:, :], rstd[:, :], rstd[:, :], ALU.mult)
        nc.vector.drain()
        nc.vector.tensor_tensor(half[:, :], half[:, :], var[:, :], ALU.mult)
        nc.vector.drain()
        nc.vector.tensor_scalar(half[:, :], half[:, :], -0.5, 1.5, ALU.mult, ALU.add)
        nc.vector.drain()
        nc.vector.tensor_tensor(rstd[:, :], rstd[:, :], half[:, :], ALU.mult)
        nc.vector.drain()
    for t in range(NT):
        last = nc.vector.tensor_scalar(out[:, t, :], x[:, t, :], mv[:, t, 0:1], rstd[:, t:t + 1],
                                       ALU.subtract, ALU.mult)
    return last


def norm_buffers(st, prefix=""):
    return (st.sb(prefix + "stats", [P, NT, 6]), st.sb(prefix + "mv", [P, NT, 2]),
            st.sb(prefix + "var", [P, NT]), st.sb(prefix + "half", [P, NT]), st.sb(prefix + "rstd", [P, NT]))


def at(ap, i):
    v = ap[bass.ds(i, 1)]
    names = " ".join("abcdefg"[:len(ap.shape) - 1])
    first = names.split(" ", 1)
    rest = " " + first[1] if len(first) > 1 else ""
    return v.rearrange(f"z {names} -> (z {first[0]}){rest}")


def project_stage(nc, c, io, d):
    with ExitStack() as ctx:
        st = Store(nc, ctx, "pj")
        s = st.sems("w_in x_in c_in bias normed turned_x turned_c xT_out cT_out mm v_mm out q_split "
                    "k_split v_out cT_saved parts_saved v_saved")
        w = {n: st.sb(n, [P, KD, D]) for n in "qkv"}
        bcol = {n: st.sb("bcol" + n, [P, KD]) for n in "qk"}
        bq4 = st.sb("bq4", [P, KD])
        bv = st.sb("bv", [P, D])
        x4, c4, xn4 = st.sb("x4", [P, NT, D]), st.sb("c4", [P, NT, D]), st.sb("xn4", [P, NT, D])
        xT, cT = st.sb("xT", [P, KD, S]), st.sb("cT", [P, KD, S])
        q1, k1, rest = st.sb("q1", [P, KD, S]), st.sb("k1", [P, KD, S]), [st.sb(f"rest_{n}", [P, KD, S]) for n in "kq"]
        qp, kp = st.sb("qp", [P, 3, KD, S], BF16), st.sb("kp", [P, 3, KD, S], BF16)
        vp = st.sb("vp", [P, NT, HEADS, PAD0])
        nb = norm_buffers(st)
        tx = [st.ps(f"tx{k}") for k in range(KD)]
        tc = [st.ps(f"tc{k}") for k in range(KD)]
        pq = [st.ps(f"pq{k}") for k in range(KD)]
        pk = [st.ps(f"pk{k}") for k in range(KD)]

        with nc.Block() as block:
            @block.sync
            def _(sp):
                def load_x(b):
                    sp.dma_start(x4[:, :, :], at(io["x"], b).rearrange("(t p) f -> p t f", p=P)).then_inc(s["x_in"], 16)

                def load_c(b):
                    sp.dma_start(c4[:, :, :], at(io["ctx_1024"], b).rearrange("(t p) f -> p t f", p=P)).then_inc(s["c_in"], 16)

                def batch(b, next_x=True, next_c=True):
                    if next_c:
                        sp.wait_ge(s["turned_c"], b + 1)
                        load_c(b + 1)
                    sp.wait_ge(s["cT_out"], KD * b + KD)
                    sp.dma_start(at(d["ctxT"], b).rearrange("(k p) s -> p k s", p=P), cT[:, :, :]).then_inc(s["cT_saved"], 16)
                    if next_x:
                        sp.wait_ge(s["normed"], b + 2)
                        load_x(b + 2)
                    sp.wait_ge(s["v_out"], NT * b + NT + NT)
                    for q in range(QUADS):
                        sp.dma_start(at(d["v0"], b)[q].rearrange("(t p) f -> p t f", p=P),
                                     vp[:, :, 4 * q:4 * q + 4, :].rearrange("p t h f -> p t (h f)")).then_inc(s["v_saved"], 16)
                    sp.wait_ge(s["k_split"], b + 1 + 1)
                    sp.dma_start(at(d["kp"], b).rearrange("j (k p) s -> p (j k) s", p=P),
                                 kp[:, :, :, :].rearrange("p j k s -> p (j k) s")).then_inc(s["parts_saved"], 16)
                    sp.wait_ge(s["q_split"], b + 1 + 1)
                    sp.dma_start(at(d["qp"], b).rearrange("j (k p) s -> p (j k) s", p=P),
                                 qp[:, :, :, :].rearrange("p j k s -> p (j k) s")).then_inc(s["parts_saved"], 16)

                sp.sem_inc(s["cT_saved"], 16)
                sp.sem_inc(s["v_saved"], 16 * QUADS)
                sp.sem_inc(s["parts_saved"], 32)
                load_c(0)
                load_x(0)
                for name in "vkq":
                    sp.dma_start(w[name][:, :, :], io[f"L0_xattn_w_{name}"].rearrange("(k p) f -> p k f", p=P)).then_inc(s["w_in"], 16)
                with nc.allow_non_contiguous_dma(reason="256 biases as columns"):
                    for name in "qk":
                        sp.dma_start(bcol[name][:, :], io[f"L0_xattn_b_{name}"].rearrange("(k p) -> p k", p=P)).then_inc(s["bias"], 16)
                sp.dma_start(bv[:, :], io["L0_xattn_b_v"].rearrange("(a f) -> a f", a=1).to_broadcast([P, D])).then_inc(s["bias"], 16)
                sp.wait_ge(s["normed"], 1)
                load_x(1)
                with sp.Fori(0, B - 2) as b:
                    batch(b)
                batch(B - 2, next_x=False)
                batch(B - 1, next_x=False, next_c=False)
                sp.wait_ge(s["cT_saved"], 16 * B + 16)
                sp.wait_ge(s["parts_saved"], 16 * 2 * B + 32)
                sp.wait_ge(s["v_saved"], 16 * QUADS * B + 16 * QUADS)

            @block.tensor
            def _(pe):
                with pe.Fori(0, B) as b:
                    pe.wait_ge(s["c_in"], b * 16 + 16)
                    for k in range(KD):
                        for t in range(NT):
                            last = nc.tensor.transpose(tc[k][:, t * P:(t + 1) * P], c4[:, t, k * P:(k + 1) * P], c["ident"][:, :])
                    last.then_inc(s["turned_c"], 1)
                    pe.wait_ge(s["normed"], b + 1)
                    pe.wait_ge(s["v_out"], NT * b + NT)
                    for k in range(KD):
                        for t in range(NT):
                            last = nc.tensor.transpose(tx[k][:, t * P:(t + 1) * P], xn4[:, t, k * P:(k + 1) * P], c["ident"][:, :])
                    last.then_inc(s["turned_x"], 1)
                    pe.wait_ge(s["w_in"], 48)
                    pe.wait_ge(s["cT_out"], KD * b + KD)
                    for m in range(KD):
                        for k in range(KD):
                            last = nc.tensor.matmul(pk[m][:, :], w["k"][:, k, m * P:(m + 1) * P], cT[:, k, :],
                                                    start=k == 0, stop=k == KD - 1)
                        last.then_inc(s["mm"], 1)
                    pe.wait_ge(s["xT_out"], KD * b + KD)
                    for t in range(NT):
                        for k in range(KD):
                            last = nc.tensor.matmul(tx[t // 2][:, (t % 2) * D:(t % 2 + 1) * D], cT[:, k, t * P:(t + 1) * P],
                                                    w["v"][:, k, :], start=k == 0, stop=k == KD - 1)
                        if t % 2:
                            last.then_inc(s["v_mm"], 1)
                    for m in range(KD):
                        for k in range(KD):
                            last = nc.tensor.matmul(pq[m][:, :], w["q"][:, k, m * P:(m + 1) * P], xT[:, k, :],
                                                    start=k == 0, stop=k == KD - 1)
                        last.then_inc(s["mm"], 1)

            @block.scalar
            def _(act):
                act.wait_ge(s["bias"], 48 + 1)
                with act.Fori(0, B) as b:
                    act.wait_ge(s["turned_c"], b + 1)
                    act.wait_ge(s["cT_saved"], b * 16 + 16)
                    for k in range(KD):
                        nc.scalar.copy(cT[:, k, :], tc[k][:, :]).then_inc(s["cT_out"], 1)
                    act.wait_ge(s["turned_x"], b + 1)
                    for k in range(KD):
                        nc.scalar.copy(xT[:, k, :], tx[k][:, :]).then_inc(s["xT_out"], 1)
                    for m in range(KD):
                        act.wait_ge(s["mm"], 2 * KD * b + m + 1)
                        act.wait_ge(s["k_split"], b + 1)
                        nc.scalar.activation(k1[:, m, :], pk[m][:, :], ACT.Identity, bias=bcol["k"][:, m:m + 1]).then_inc(s["out"], 1)
                        act.wait_ge(s["parts_saved"], b * 32 + 32)
                        nc.scalar.activation(kp[:, 0, m, :], pk[m][:, :], ACT.Identity, bias=bcol["k"][:, m:m + 1]).then_inc(s["out"], 1)
                    for m in range(KD):
                        act.wait_ge(s["mm"], 2 * KD * b + KD + m + 1)
                        act.wait_ge(s["q_split"], b + 1)
                        nc.scalar.activation(q1[:, m, :], pq[m][:, :], ACT.Identity, bias=bq4[:, m:m + 1],
                                             scale=DH0 ** -0.5).then_inc(s["out"], 1)
                        nc.scalar.activation(qp[:, 0, m, :], pq[m][:, :], ACT.Identity, bias=bq4[:, m:m + 1],
                                             scale=DH0 ** -0.5).then_inc(s["out"], 1)

            @block.vector
            def _(dve):
                nc.vector.memset(vp[:, :, :, :].rearrange("p t h f -> p (t h f)"), 0.0)

                def split(src, parts, rest):
                    nc.vector.tensor_tensor(rest[:, :, :], src[:, :, :], parts[:, 0], ALU.subtract)
                    nc.vector.drain()
                    nc.vector.tensor_copy(parts[:, 1], rest[:, :, :])
                    nc.vector.drain()
                    return nc.vector.tensor_tensor(parts[:, 2], rest[:, :, :], parts[:, 1], ALU.subtract)

                def norm(b):
                    dve.wait_ge(s["x_in"], b * 16 + 16)
                    if not (isinstance(b, int) and b == 0):
                        dve.wait_ge(s["turned_x"], b)
                    nc.vector.memset(nb[2][:, :], 0.0)
                    layer_norm(nc, x4, *nb, xn4, 1e-5).then_inc(s["normed"], 1)

                def batch(b, has_next=True):
                    if has_next:
                        norm(b + 1)
                    dve.wait_ge(s["v_saved"], b * (16 * QUADS) + 16 * QUADS)
                    for t in range(NT):
                        if t % 2 == 0:
                            dve.wait_ge(s["v_mm"], NT // 2 * b + t // 2 + 1)
                        nc.vector.tensor_tensor(vp[:, t, :, 0:DH0],
                                                tx[t // 2][:, (t % 2) * D:(t % 2 + 1) * D].rearrange("p (h f) -> p h f", h=HEADS),
                                                bv[:, :].rearrange("p (h f) -> p h f", h=HEADS), ALU.add).then_inc(s["v_out"], 1)
                    dve.wait_ge(s["out"], 4 * KD * b + 2 * KD)
                    dve.wait_ge(s["parts_saved"], b * 32 + 32)
                    split(k1, kp, rest[0]).then_inc(s["k_split"], 1)
                    dve.wait_ge(s["out"], 4 * KD * b + 4 * KD)
                    split(q1, qp, rest[1]).then_inc(s["q_split"], 1)

                dve.sem_inc(s["v_out"], NT)
                dve.sem_inc(s["k_split"], 1)
                dve.sem_inc(s["q_split"], 1)
                norm(0)
                dve.wait_ge(s["bias"], 48)
                nc.vector.tensor_scalar(bq4[:, :], bcol["q"][:, :], DH0 ** -0.5, None, ALU.mult).then_inc(s["bias"], 1)
                with dve.Fori(0, B - 1) as b:
                    batch(b)
                batch(B - 1, has_next=False)


NU = 4 * NT
BODY = 2 * NU
BODIES = ITEMS // 2
DEEP = 4
LAG_T = 3


def lagged(body, step, lag, first, last):
    w = step - lag
    if w >= 0:
        return None if last else (body, w)
    return None if first else (body - 1, w + BODY)


def masked_attention_stage(nc, c, io, d):
    LAG_T = 4
    PROBS = 8
    LAG_V = 6
    STEP_V = 4
    LAG_O = LAG_V + STEP_V * (NT - 1) + 1
    LAG_N = LAG_O + 2
    with ExitStack() as ctx:
        st = Store(nc, ctx, "a0")
        s = st.sems("in0 in1 v_in0 v_in1 mask_in mask_made scores lifted exped turned evac_d evac_a pv o_copied spread recip_mm normed saved0 saved1")
        qs = [st.sb(f"qs{i}", [STACK, 4, S], BF16) for i in range(2)]
        ks = [st.sb(f"ks{i}", [STACK, 4, S], BF16) for i in range(2)]
        v = [st.sb(f"v{i}", [P, NT, 4 * PAD0]) for i in range(2)]
        mask, maskb, pad = st.sb("mask", [P, NT, S]), st.sb("maskb", [P, NT, S]), st.sb("pad", [P, B, S])
        low = [st.sb(f"low{i}", [P, S]) for i in range(DEEP)]
        prob = [st.sb(f"prob{i}", [P, S]) for i in range(PROBS)]
        nmax, total = st.sb("nmax", [P, BODY]), st.sb("total", [P, BODY])
        recip, spread = st.sb("recip", [P, NU]), st.sb("spread", [P, NT, 4, PAD0])
        pT = [st.sb(f"pT{i}", [P, NT, S]) for i in range(8)]
        o_sb = st.sb("o_sb", [P, S])
        o_n = [st.sb(f"o_n{i}", [P, S]) for i in range(2)]
        cells = st.sb("cells", [P, BODY])
        ps_s = [st.ps(f"s{i}") for i in range(2)]
        ps_t = [st.ps(f"t{i}") for i in range(2)]
        ps_o = [st.ps(f"o{i}") for i in range(2)]
        ps_r = st.ps("r")
        s_in, s_v, s_saved = (s["in0"], s["in1"]), (s["v_in0"], s["v_in1"]), (s["saved0"], s["saved1"])
        LOADS = 2 * len(Q_PARTS)

        with nc.Block() as block:
            @block.sync
            def _(sp):
                def load(b, quad):
                    par = quad % 2
                    if not (isinstance(b, int) and quad < 2):
                        sp.wait_ge(s["scores"], (b * QUADS + quad - 1) * NU)
                    for t, (a, b_) in enumerate(zip(Q_PARTS, K_PARTS)):
                        for dst, src in ((qs[par], at(d["qp"], b)[a]), (ks[par], at(d["kp"], b)[b_])):
                            sp.dma_start(dst[t * DH0:(t + 1) * DH0, :, :],
                                         src[quad * 64:quad * 64 + 64, :].rearrange("(h f) s -> f h s", h=4)).then_inc(s_in[par], 16)
                    if not (isinstance(b, int) and quad < 2):
                        sp.wait_ge(s["pv"], b * QUADS + quad + 1)
                    sp.dma_start(v[par][:, :, :], at(d["v0"], b)[quad].rearrange("(t p) f -> p t f", p=P)).then_inc(s_v[par], 16)

                def save(n, par):
                    sp.wait_ge(s["normed"], n + 2)
                    sp.dma_start(at(d["o0"], n), o_n[par][:, :]).then_inc(s_saved[par], 16)

                sp.sem_inc(s["saved0"], 16)
                sp.sem_inc(s["saved1"], 16)
                load(0, 0)
                sp.dma_start(mask[:, :, :], io["mask_1x1xSxS2_fk0"].rearrange("x y (t p) s -> p (x y t) s", p=P)).then_inc(s["mask_in"], 16)
                for b in range(B):
                    sp.dma_start(pad[:, b, :], io["mask_Bx1x1xS2_ff0"][b, 0].to_broadcast([P, S])).then_inc(s["mask_in"], 16)
                load(0, 1)
                for par in range(2):
                    load(0, 2 + par)
                    save(par, par)
                with sp.Fori(1, B) as b:
                    for quad in range(QUADS):
                        load(b, quad)
                        save(b * QUADS + quad - 2, quad % 2)
                save(ITEMS - 2, 0)
                save(ITEMS - 1, 1)
                for par in range(2):
                    sp.wait_ge(s_saved[par], 16 * (ITEMS // 2) + 16)

            @block.gpsimd
            def _(pool):
                pool.wait_ge(s["mask_in"], 16 * (B + 1))
                for b in range(B):
                    for t in range(NT):
                        if b:
                            pool.wait_ge(s["lifted"], 2 * b * BODY - NT + t + 1 + 2)
                        nc.gpsimd.tensor_tensor(maskb[:, t, :], mask[:, t, :], pad[:, b, :], ALU.add).then_inc(s["mask_made"], 1)

            @block.tensor
            def _(pe):
                pe.sem_inc(s["turned"], PROBS)
                pe.sem_inc(s["pv"], 2)

                def run(body, step, first=False, last=False):
                    if lagged(body, step, 0, first, last):
                        par, h, t = step // NU, step % NU // NT, step % NT
                        if step % NU == 0:
                            pe.wait_ge(s_in[par], body * (LOADS * 16) + LOADS * 16)
                        pe.wait_ge(s["lifted"], body * BODY + step + 1)
                        nc.tensor.matmul(ps_s[step % 2][:, :], qs[par][:, h, t * P:(t + 1) * P], ks[par][:, h, :],
                                         start=True, stop=True).then_inc(s["scores"], 1)
                    unit = lagged(body, step, LAG_T, first, last)
                    if unit:
                        ub, w = unit
                        pe.wait_ge(s["exped"], ub * BODY + w + 1 + DEEP)
                        pe.wait_ge((s["evac_d"], s["evac_a"])[w % 2], ub * NU + w // 2 + 1)
                        for k in range(NT):
                            op = nc.tensor.transpose(ps_t[w % 2][:, k * P:(k + 1) * P],
                                                     prob[w % PROBS][:, k * P:(k + 1) * P], c["ident"][:, :])
                        op.then_inc(s["turned"], 1)
                    for k in range(NT):
                        unit = lagged(body, step, LAG_V + STEP_V * k, first, last)
                        if unit and unit[1] % NU == NU - 1:
                            ub, w = unit
                            par = w // NU
                            if k == 0:
                                pe.wait_ge(s_v[par], ub * 16 + 16)
                                pe.wait_ge(s["evac_d"], ub * NU + w // 2 + 1 + 1)
                                pe.wait_ge(s["evac_a"], ub * NU + w // 2 + 1 + 1)
                                pe.wait_ge(s["o_copied"], ub * 2 + par + 1)
                            for h in range(4):
                                op = nc.tensor.matmul(ps_o[par][h * PAD0:(h + 1) * PAD0, :],
                                                      v[par][:, k, h * PAD0:(h + 1) * PAD0], pT[par * 4 + h][:, k, :],
                                                      start=k == 0, stop=k == NT - 1)
                            if k == NT - 1:
                                op.then_inc(s["pv"], 1)
                    unit = lagged(body, step, LAG_V, first, last)
                    if unit and unit[1] % NU == NU - 1:
                        ub, w = unit
                        par = w // NU
                        pe.wait_ge(s["spread"], ub * 2 + par + 1)
                        pe.wait_ge(s["normed"], ub * 2 + par + 1)
                        for t in range(NT):
                            op = nc.tensor.transpose(ps_r[:, t * P:(t + 1) * P],
                                                     spread[:, t, :, :].rearrange("p h f -> p (h f)"), c["ident"][:, :])
                        op.then_inc(s["recip_mm"], 1)

                for step in range(BODY):
                    run(0, step, first=True)
                with pe.Fori(1, BODIES) as body:
                    for step in range(BODY):
                        run(body, step)
                for step in range(LAG_O):
                    run(BODIES, step, last=True)

            @block.vector
            def _(dve):
                dve.sem_inc(s["lifted"], 2)
                dve.sem_inc(s["evac_d"], 1)
                dve.sem_inc(s["normed"], 1)

                def run(b, body, step, first=False, last=False):
                    if lagged(body, step, 0, first, last):
                        dve.wait_ge(s["scores"], body * BODY + step + 1)
                        dve.wait_ge(s["exped"], body * BODY + step + 1)
                        if step < NT:
                            dve.wait_ge(s["mask_made"], b * NT + step + 1)
                        nc.vector.memset(cells[:, step:step + 1], 0.0)
                        nc.vector.tensor_tensor_reduce(out=low[step % DEEP][:, :], in0=ps_s[step % 2][:, :], in1=maskb[:, step % NT, :],
                                                       scale=-1.0, scalar=3.0e38, op0=ALU.add, op1=ALU.min,
                                                       accum_out=nmax[:, step:step + 1]).then_inc(s["lifted"], 1)
                    unit = lagged(body, step, LAG_T, first, last)
                    if unit and unit[1] % 2 == 0:
                        ub, w = unit
                        dve.wait_ge(s["turned"], ub * BODY + w + 1 + PROBS)
                        if w % NU == 0:
                            dve.wait_ge(s["pv"], ub * 2 + w // NU + 1)
                        nc.vector.tensor_copy(pT[w // NT][:, :, w % NT * P:(w % NT + 1) * P],
                                              ps_t[0][:, :].rearrange("p (k s) -> p k s", k=NT)).then_inc(s["evac_d"], 1)
                    if unit and unit[1] % NU == NU - 1:
                        ub, w = unit
                        par = w // NU
                        dve.wait_ge(s["exped"], ub * BODY + w + 1 + DEEP)
                        if not (first and par == 0):
                            dve.wait_ge(s["recip_mm"], ub * 2 + par)
                        nc.vector.reciprocal(recip[:, :], total[:, par * NU:(par + 1) * NU])
                        nc.vector.drain()
                        nc.vector.tensor_copy(spread[:, :, :, :],
                                              recip[:, :].rearrange("p (h t o) -> p t h o", h=4, o=1)
                                              .to_broadcast([P, NT, 4, PAD0])).then_inc(s["spread"], 1)
                    unit = lagged(body, step, LAG_N, first, last)
                    if unit and unit[1] % NU == NU - 1:
                        ub, w = unit
                        par = w // NU
                        dve.wait_ge(s["recip_mm"], ub * 2 + par + 1)
                        dve.wait_ge(s["o_copied"], ub * 2 + par + 1 + 2)
                        dve.wait_ge(s_saved[par], ub * 16 + 16)
                        nc.vector.tensor_tensor(o_n[par][:, :], o_sb[:, :], ps_r[:, :], ALU.mult).then_inc(s["normed"], 1)

                for step in range(BODY):
                    run(0, 0, step, first=True)
                for step in range(BODY):
                    run(0, 1, step)
                with dve.Fori(1, B) as b:
                    with dve.Fori(0, 2) as half:
                        for step in range(BODY):
                            run(b, b * 2 + half, step)
                for step in range(LAG_N):
                    run(B, BODIES, step, last=True)

            @block.scalar
            def _(act):
                act.sem_inc(s["exped"], DEEP)
                act.sem_inc(s["evac_a"], 1)
                act.sem_inc(s["o_copied"], 2)

                def run(body, step, first=False, last=False):
                    unit = lagged(body, step, LAG_T, first, last)
                    if unit and unit[1] % 2 == 1:
                        ub, w = unit
                        act.wait_ge(s["turned"], ub * BODY + w + 1 + PROBS)
                        if w % NU == 1:
                            act.wait_ge(s["pv"], ub * 2 + w // NU + 1)
                        nc.scalar.copy(pT[w // NT][:, :, w % NT * P:(w % NT + 1) * P],
                                       ps_t[1][:, :].rearrange("p (k s) -> p k s", k=NT)).then_inc(s["evac_a"], 1)
                    if lagged(body, step, 0, first, last):
                        act.wait_ge(s["lifted"], body * BODY + step + 1 + 2)
                        act.wait_ge(s["turned"], body * BODY + step + 1)
                        nc.scalar.activation(prob[step % PROBS][:, :], low[step % DEEP][:, :], ACT.Exp, bias=nmax[:, step:step + 1],
                                             scale=-1.0, accum_out=total[:, step:step + 1]).then_inc(s["exped"], 1)
                    unit = lagged(body, step, LAG_O, first, last)
                    if unit and unit[1] % NU == NU - 1:
                        ub, w = unit
                        par = w // NU
                        act.wait_ge(s["pv"], ub * 2 + par + 1 + 2)
                        act.wait_ge(s["normed"], ub * 2 + par + 1)
                        nc.scalar.copy(o_sb[:, :], ps_o[par][:, :]).then_inc(s["o_copied"], 1)

                for step in range(BODY):
                    run(0, step, first=True)
                with act.Fori(1, BODIES) as body:
                    for step in range(BODY):
                        run(body, step)
                for step in range(LAG_O):
                    run(BODIES, step, last=True)


class Router:

    def __init__(self, nc, st, c, experts, top, cap, drop):
        self.nc, self.c, self.E, self.top, self.cap, self.drop = nc, c, experts, top, cap, drop
        self.R = NT * top
        self.nmax, self.sums, self.rsum = st.sb("nmax", [P, NT]), st.sb("sums", [P, NT]), st.sb("rsum", [P, NT])
        self.e = st.sb("e", [P, NT, experts])
        self.best, self.best_at = st.sb("best", [P, NT, 8]), st.sb("best_at", [P, NT, 8], U32)
        self.expert = st.sb("expert", [P, self.R])
        self.hot, self.hot_pos = st.sb("hot", [P, self.R, experts]), st.sb("hot_pos", [P, self.R, experts])
        self.chosen, self.before = st.sb("chosen", [P, NT, experts], BF16), st.sb("before", [P, experts], BF16)
        self.pos, self.fits, self.skip = st.sb("pos", [P, self.R]), st.sb("fits", [P, self.R]), st.sb("skip", [P, self.R])
        self.slot, self.slot_skip = st.sb("slot", [P, self.R]), st.sb("slot_skip", [P, self.R])
        self.slot_read, self.slot_write = st.sb("slot_read", [P, self.R], U32), st.sb("slot_write", [P, self.R], U32)
        self.weight = st.sb("weight", [P, self.R])
        self.tok_f, self.tok = st.sb("tok_f", [P, NT]), st.sb("tok", [P, NT], U32)
        self.tok_write = st.sb("tok_write", [P, NT], U32)

    def start(self):
        v = self.nc.vector
        v.memset(self.before[:, :], 0.0)
        v.tensor_copy(self.tok_f[:, :], self.c["token_no"][:, :])

    def tail(self, ap):
        return ap.rearrange("p (r o) -> p r o", o=1)

    def pick(self):
        v = self.nc.vector
        v.reciprocal(self.rsum[:, :], self.sums[:, :])
        for t in range(NT):
            v.max(self.best[:, t, :], self.e[:, t, :])
        v.drain()
        for t in range(NT):
            v.max_index(self.best_at[:, t, :], self.best[:, t, :], self.e[:, t, :])
        v.drain()
        v.tensor_copy(self.expert[:, :].rearrange("p (t j) -> p t j", t=NT), self.best_at[:, :, 0:self.top])
        v.drain()
        full = [P, self.R, self.E]
        v.tensor_tensor(self.hot[:, :, :], self.c["expert_no"][:, 0:self.E].rearrange("p (o e) -> p o e", o=1).to_broadcast(full),
                        self.tail(self.expert[:, :]).to_broadcast(full), ALU.is_equal)
        v.drain()
        if self.top == 1:
            return v.tensor_copy(self.chosen[:, :, :], self.hot[:, :, :])
        with self.nc.allow_low_precision(reason="zeros and ones"):
            return v.tensor_reduce(self.chosen[:, :, :], self.hot[:, :, :].rearrange("p (t j) e -> p t e j", t=NT), AX, ALU.add)

    def place(self, ps_pos):
        v = self.nc.vector
        earlier = ps_pos[:, 0:NT * self.E].rearrange("p (t e) -> p t e", t=NT)
        for t in range(NT):
            rows = slice(t * self.top, (t + 1) * self.top)
            v.tensor_tensor(self.hot_pos[:, rows, :], self.hot[:, rows, :],
                            earlier[:, t:t + 1, :].to_broadcast([P, self.top, self.E]), ALU.mult)
            v.drain()
            v.tensor_tensor(self.before[:, :], self.before[:, :], self.chosen[:, t, :], ALU.add)
        v.drain()
        v.tensor_reduce(self.pos[:, :], self.hot_pos[:, :, :], AX, ALU.add)
        v.drain()
        v.tensor_scalar(self.fits[:, :], self.pos[:, :], float(self.cap), None, ALU.is_lt)
        v.tensor_scalar(self.pos[:, :], self.pos[:, :], float(self.cap - 1), None, ALU.min)
        v.drain()
        v.tensor_scalar(self.skip[:, :], self.fits[:, :], -SKIP, SKIP, ALU.mult, ALU.add)
        v.tensor_scalar(self.slot[:, :], self.expert[:, :], float(self.cap), None, ALU.mult)
        v.tensor_tensor(self.weight[:, :].rearrange("p (t j) -> p t j", t=NT), self.best[:, :, 0:self.top],
                        self.tail(self.rsum[:, :]).to_broadcast([P, NT, self.top]), ALU.mult)
        v.drain()
        v.tensor_tensor(self.slot[:, :], self.slot[:, :], self.pos[:, :], ALU.add)
        if self.drop:
            v.tensor_tensor(self.weight[:, :], self.weight[:, :], self.fits[:, :], ALU.mult)
        v.tensor_copy(self.tok[:, :], self.tok_f[:, :])
        v.drain()
        v.tensor_scalar(self.tok_f[:, :], self.tok_f[:, :], float(S), None, ALU.add)
        return v.tensor_copy(self.slot_read[:, :], self.slot[:, :])

    def exponentials(self, logits):
        for t in range(NT):
            last = self.nc.scalar.activation(self.e[:, t, :], logits[:, t, :], ACT.Exp, bias=self.nmax[:, t:t + 1],
                                             accum_out=self.sums[:, t:t + 1])
        return last

    def count_earlier(self, ps_pos):
        mm = self.nc.tensor.matmul
        for t in range(NT):
            o = ps_pos[:, t * self.E:(t + 1) * self.E]
            mm(o, self.c["ones16"][:, :], self.before[:, :], start=True, stop=False)
            for u in range(t):
                mm(o, self.c["ones16"][:, :], self.chosen[:, u, :], start=False, stop=False)
            last = mm(o, self.c["before"][:, :], self.chosen[:, t, :], start=False, stop=True)
        return last

    def scatter(self, b, table, done, copied):
        pool = self.nc.gpsimd
        pool.tensor_tensor(self.slot_skip[:, :], self.slot[:, :], self.skip[:, :], ALU.add)
        pool.tensor_copy(self.tok_write[:, :], self.tok[:, :]).then_inc(copied, 1)
        pool.drain()
        pool.tensor_copy(self.slot_write[:, :], self.slot_skip[:, :])
        pool.drain()
        for r in range(self.R):
            t = r // self.top
            pool.indirect_dma_start(out=table, out_offset=bass.IndirectOffsetOnAxis(ap=self.slot_write[:, r:r + 1], axis=0),
                                    in_=self.tok_write[:, t:t + 1], in_offset=None, bounds_check=self.E * self.cap - 1,
                                    oob_is_err=False).then_inc(done, 16)
        pool.wait_ge(done, b * (16 * self.R) + 16 * self.R)


def route0_stage(nc, c, io, d):
    with ExitStack() as ctx:
        st = Store(nc, ctx, "r0")
        s = st.sems("w_in zeroed o_in x_in product summed normed turned xT_out logits maxed exped picked counted placed "
                    "scattered slots_free x_saved xn_saved slots_saved table_zero")
        wo = st.sb("wo", [P, QUADS, D])
        wr = st.sb("wr", [P, KD, E0])
        bo = st.sb("bo", [P, D])
        o4, x4 = st.sb("o4", [P, QUADS, S]), st.sb("x4", [P, NT, D])
        x1, xn = st.sb("x1", [P, NT, D]), st.sb("xn", [P, NT, D])
        xT = st.sb("xT", [P, KD, S])
        nb = norm_buffers(st)
        r = Router(nc, st, c, E0, TOP0, CAP0, drop=False)
        ps_y = [st.ps(f"y{i}") for i in range(2)]
        ps_x = [st.ps(f"x{i}") for i in range(KD)]
        ps_l, ps_p = st.ps("l"), st.ps("p")
        logits = ps_l[:, 0:NT * E0].rearrange("p (t e) -> p t e", t=NT)

        with nc.Block() as block:
            @block.sync
            def _(sp):
                def load(b):
                    sp.dma_start(o4[:, :, :], at(d["o0"].rearrange("(b q) p s -> b q p s", b=B), b).rearrange("q p s -> p q s")).then_inc(s["o_in"], 16)
                    sp.dma_start(x4[:, :, :], at(io["x"], b).rearrange("(t p) f -> p t f", p=P)).then_inc(s["x_in"], 16)

                def save(b):
                    sp.wait_ge(s["summed"], b + 1 + 1)
                    sp.dma_start(at(d["x1"], b).rearrange("(t p) f -> p t f", p=P), x1[:, :, :]).then_inc(s["x_saved"], 16)

                def save_norm(b):
                    sp.wait_ge(s["normed"], b + 1)
                    sp.dma_start(at(d["xn1"].rearrange("(b s) f -> b s f", b=B), b).rearrange("(t p) f -> p t f", p=P), xn[:, :, :]).then_inc(s["xn_saved"], 16)

                def save_choice(b):
                    sp.wait_ge(s["placed"], b + 1)
                    sp.dma_start(at(d["slots0"], b), r.slot_read[:, :]).then_inc(s["slots_saved"], 16)
                    sp.dma_start(at(d["weights0"], b), r.weight[:, :]).then_inc(s["slots_saved"], 16)

                sp.sem_inc(s["slots_saved"], 32)
                load(0)
                sp.dma_start(bo[:, :], io["L0_xattn_b_out"].rearrange("(a f) -> a f", a=1).to_broadcast([P, D])).then_inc(s["w_in"], 16)
                sp.wait_ge(s["zeroed"], 1)
                for h in range(4):
                    sp.dma_start(wo[h * PAD0:h * PAD0 + DH0, :, :],
                                 io["L0_xattn_w_out"].rearrange("(q h f) d -> h f q d", q=QUADS, h=4)[h]).then_inc(s["w_in"], 16)
                sp.dma_start(wr[:, :, :], io["L0_ffn_router_w"].rearrange("(k p) e -> p k e", p=P)).then_inc(s["w_in"], 16)
                sp.dma_start(d["table0"].rearrange("(p k) o -> p (k o)", p=P), c["zeros"][:, :].bitcast(U32)).then_inc(s["table_zero"], 16)
                save(0)
                load(1)
                save_norm(0)
                with sp.Fori(0, B - 2) as b:
                    save(b + 1)
                    load(b + 2)
                    save_norm(b + 1)
                    save_choice(b)
                save(B - 1)
                save_norm(B - 1)
                save_choice(B - 2)
                save_choice(B - 1)
                sp.wait_ge(s["x_saved"], 16 * B)
                sp.wait_ge(s["xn_saved"], 16 * B)
                sp.wait_ge(s["slots_saved"], 32 * B + 32)

            @block.gpsimd
            def _(pool):
                pool.sem_inc(s["slots_free"], 1)
                pool.wait_ge(s["table_zero"], 16)
                with pool.Fori(0, B) as b:
                    pool.wait_ge(s["placed"], b + 1)
                    r.scatter(b, d["table0"], s["scattered"], s["slots_free"])

            @block.tensor
            def _(pe):
                def product(b):
                    pe.wait_ge(s["o_in"], b * 16 + 16)
                    pe.wait_ge(s["summed"], b + 1)
                    for t in range(NT):
                        for q in range(QUADS):
                            last = nc.tensor.matmul(ps_y[t // 2][:, t % 2 * D:(t % 2 + 1) * D], o4[:, q, t * P:(t + 1) * P],
                                                    wo[:, q, :], start=q == 0, stop=q == QUADS - 1)
                        if t % 2:
                            last.then_inc(s["product"], 1)

                def router(b):
                    pe.wait_ge(s["normed"], b + 1)
                    for k in range(KD):
                        for t in range(NT):
                            last = nc.tensor.transpose(ps_x[k][:, t * P:(t + 1) * P], xn[:, t, k * P:(k + 1) * P], c["ident"][:, :])
                    last.then_inc(s["turned"], 1)
                    pe.wait_ge(s["xT_out"], KD * b + KD)
                    pe.wait_ge(s["exped"], b + 1)
                    for t in range(NT):
                        for k in range(KD):
                            last = nc.tensor.matmul(ps_l[:, t * E0:(t + 1) * E0], xT[:, k, t * P:(t + 1) * P], wr[:, k, :],
                                                    start=k == 0, stop=k == KD - 1)
                    last.then_inc(s["logits"], 1)

                def count(b):
                    pe.wait_ge(s["picked"], b + 1)
                    r.count_earlier(ps_p).then_inc(s["counted"], 1)

                pe.wait_ge(s["w_in"], 16 * 6)
                product(0)
                product(1)
                router(0)
                with pe.Fori(0, B - 2) as b:
                    router(b + 1)
                    count(b)
                    product(b + 2)
                router(B - 1)
                count(B - 2)
                count(B - 1)

            @block.scalar
            def _(act):
                act.sem_inc(s["exped"], 1)
                with act.Fori(0, B) as b:
                    act.wait_ge(s["turned"], b + 1)
                    for k in range(KD):
                        nc.scalar.copy(xT[:, k, :], ps_x[k][:, :]).then_inc(s["xT_out"], 1)
                    act.wait_ge(s["maxed"], b + 1)
                    r.exponentials(logits).then_inc(s["exped"], 1)

            @block.vector
            def _(dve):
                def norm(b):
                    dve.wait_ge(s["x_in"], b * 16 + 16)
                    if not (isinstance(b, int) and b == 0):
                        dve.wait_ge(s["x_saved"], 16 * b)
                    for t in range(NT):
                        nc.vector.tensor_tensor(x1[:, t, :], x4[:, t, :], bo[:, :], ALU.add)
                    nc.vector.drain()
                    for half in range(2):
                        dve.wait_ge(s["product"], 2 * b + half + 1)
                        last = nc.vector.tensor_tensor(x1[:, 2 * half:2 * half + 2, :], x1[:, 2 * half:2 * half + 2, :],
                                                       ps_y[half][:, :].rearrange("p (t f) -> p t f", t=2), ALU.add)
                    last.then_inc(s["summed"], 1)
                    nc.vector.drain()
                    if not (isinstance(b, int) and b == 0):
                        dve.wait_ge(s["xn_saved"], 16 * b)
                        dve.wait_ge(s["turned"], b)
                    nc.vector.memset(r.pos[:, :], 0.0)
                    layer_norm(nc, x1, *nb, xn, 1e-5).then_inc(s["normed"], 1)

                def maximum(b):
                    dve.wait_ge(s["logits"], b + 1)
                    nc.vector.tensor_reduce(r.nmax[:, :], logits, AX, ALU.max, negate=True).then_inc(s["maxed"], 1)

                def choose(b):
                    dve.wait_ge(s["exped"], b + 1 + 1)
                    r.pick().then_inc(s["picked"], 1)
                    dve.wait_ge(s["slots_saved"], b * 32 + 32)
                    dve.wait_ge(s["slots_free"], b + 1)
                    dve.wait_ge(s["counted"], b + 1)
                    r.place(ps_p).then_inc(s["placed"], 1)

                dve.sem_inc(s["summed"], 1)
                nc.vector.memset(wo[:, :, :].rearrange("p q f -> p (q f)"), 0.0).then_inc(s["zeroed"], 1)
                r.start()
                dve.wait_ge(s["w_in"], 16 * 6)
                norm(0)
                maximum(0)
                with dve.Fori(0, B - 1) as b:
                    norm(b + 1)
                    choose(b)
                    maximum(b + 1)
                choose(B - 1)


def experts0_stage(nc, c, io, d):
    HALVES = CAP0 // P
    BODIES = E0 // DEEP
    with ExitStack() as ctx:
        st = Store(nc, ctx, "e0")
        s = st.sems("table_in table_f table_T idx_made idx_set turned xT_out h silu gated y y_out " +
                    " ".join(f"w{i} rows{i} saved{i}" for i in range(DEEP)))
        table, table_f = st.sb("table", [P, P], U32), st.sb("table_f", [P, P])
        idx_all = st.sb("idx_all", [P, P], U32)
        idx = [st.sb(f"idx{i}", [P, HALVES], U32) for i in range(DEEP)]
        carry = st.sb("carry", [P, E0])
        rows = [st.sb(f"rows{i}", [P, HALVES, D]) for i in range(DEEP)]
        w1 = [st.sb(f"w1{i}", [P, KD, 2 * I0]) for i in range(DEEP)]
        w2 = [st.sb(f"w2{i}", [P, D]) for i in range(DEEP)]
        y = [st.sb(f"y{i}", [P, HALVES, D]) for i in range(DEEP)]
        xT = [st.sb(f"xT{i}", [P, KD, CAP0]) for i in range(2)]
        sg, g = [st.sb(f"sg{i}", [P, CAP0]) for i in range(2)], [st.sb(f"g{i}", [P, CAP0]) for i in range(2)]
        ps_x, ps_h, ps_y = [[st.ps(f"{n}{i}") for i in range(2)] for n in "xhy"]
        s_w, s_rows, s_saved = ([s[f"{n}{i}"] for i in range(DEEP)] for n in ("w", "rows", "saved"))
        y_out = d["y0"].rearrange("(e h p) f -> e p h f", p=P, h=HALVES)

        with nc.Block() as block:
            @block.sync
            def _(sp):
                sp.dma_start(table[:, :], d["table0"].rearrange("(g p) o -> g (p o)", p=P)).then_inc(s["table_in"], 16)
                with sp.Fori(0, BODIES) as body:
                    for i in range(DEEP):
                        e = body * DEEP + i
                        sp.wait_ge(s["y"], e + 1)
                        sp.dma_start(w1[i][:, :, :], at(io["L0_ffn_w1"], e).rearrange("(k p) f -> p k f", p=P)).then_inc(s_w[i], 16)
                        sp.dma_start(w2[i][:, :], at(io["L0_ffn_w2"], e)).then_inc(s_w[i], 16)

            @block.gpsimd
            def _(pool):
                with pool.Fori(0, BODIES) as body:
                    for i in range(DEEP):
                        e = body * DEEP + i
                        pool.wait_ge(s["idx_set"], e + 1)
                        nc.gpsimd.tensor_tensor(carry[:, bass.ds(e, 1)], c["ones"][:, 0:1], c["ones"][:, 0:1], ALU.mult)
                        for h in range(HALVES):
                            nc.gpsimd.indirect_dma_start(out=rows[i][:, h, :], out_offset=None, in_=d["xn1"],
                                                         in_offset=bass.IndirectOffsetOnAxis(ap=idx[i][:, h:h + 1], axis=0),
                                                         ).then_inc(s_rows[i], 16)

            @block.tensor
            def _(pe):
                pe.sem_inc(s["turned"], DEEP)
                pe.sem_inc(s["y"], DEEP)
                pe.wait_ge(s["table_f"], 1)
                nc.tensor.transpose(ps_x[0][:, 0:P], table_f[:, :], c["ident"][:, :]).then_inc(s["table_T"], 1)
                pe.wait_ge(s["idx_made"], 1)

                def turn(body, i):
                    e = body * DEEP + i
                    pe.wait_ge(s_rows[i], body * (16 * HALVES) + 16 * HALVES)
                    pe.wait_ge(s["xT_out"], e + 1)
                    for k in range(KD):
                        for h in range(HALVES):
                            last = nc.tensor.transpose(ps_x[i % 2][:, k * CAP0 + h * P:k * CAP0 + (h + 1) * P],
                                                       rows[i][:, h, k * P:(k + 1) * P], c["ident"][:, :])
                    last.then_inc(s["turned"], 1)

                def first(body, i):
                    e = body * DEEP + i
                    pe.wait_ge(s_w[i], body * 32 + 32)
                    pe.wait_ge(s["xT_out"], e + 1 + 2)
                    pe.wait_ge(s["gated"], e + 1)
                    for m in range(2):
                        for k in range(KD):
                            last = nc.tensor.matmul(ps_h[i % 2][:, m * CAP0:(m + 1) * CAP0], w1[i][:, k, m * I0:(m + 1) * I0],
                                                    xT[i % 2][:, k, :], start=k == 0, stop=k == KD - 1)
                    last.then_inc(s["h"], 1)

                def second(body, i):
                    e = body * DEEP + i
                    pe.wait_ge(s["gated"], e + 1 + 2)
                    pe.wait_ge(s["y_out"], e + 1)
                    for h in range(HALVES):
                        last = nc.tensor.matmul(ps_y[i % 2][:, h * D:(h + 1) * D], g[i % 2][:, h * P:(h + 1) * P], w2[i][:, :],
                                                start=True, stop=True)
                    last.then_inc(s["y"], 1)

                turn(0, 0)
                for i in range(DEEP):
                    first(0, i)
                    turn((0, 1)[i == DEEP - 1], (i + 1) % DEEP)
                    if i >= 1:
                        second(0, i - 1)
                with pe.Fori(1, BODIES - 1) as body:
                    for i in range(DEEP):
                        first(body, i)
                        turn(body + 1 if i == DEEP - 1 else body, (i + 1) % DEEP)
                        second(body - 1 if i == 0 else body, (i - 1) % DEEP)
                for i in range(DEEP):
                    first(BODIES - 1, i)
                    if i < DEEP - 1:
                        turn(BODIES - 1, i + 1)
                    second(BODIES - 2 if i == 0 else BODIES - 1, (i - 1) % DEEP)
                second(BODIES - 1, DEEP - 1)

            @block.scalar
            def _(act):
                act.sem_inc(s["y_out"], 2)
                for i in range(DEEP):
                    act.sem_inc(s_saved[i], 16)

                def silu(body, i):
                    act.wait_ge(s["h"], body * DEEP + i + 1)
                    act.wait_ge(s["gated"], body * DEEP + i + 1)
                    nc.scalar.activation(sg[i % 2][:, :], ps_h[i % 2][:, 0:CAP0], ACT.Silu).then_inc(s["silu"], 1)

                def leave(body, i):
                    e = body * DEEP + i
                    act.wait_ge(s["y"], e + 1 + DEEP)
                    act.wait_ge(s_saved[i], body * 16 + 16)
                    nc.scalar.copy(y[i][:, :, :], ps_y[i % 2][:, :].rearrange("p (h f) -> p h f", h=HALVES)).then_inc(s["y_out"], 1)
                    act.wait_ge(s["y_out"], e + 1 + 2)
                    act.dma_start(at(y_out, e), y[i][:, :, :]).then_inc(s_saved[i], 16)

                for i in range(DEEP):
                    silu(0, i)
                    if i >= 1:
                        leave(0, i - 1)
                with act.Fori(1, BODIES) as body:
                    for i in range(DEEP):
                        silu(body, i)
                        leave(body - 1 if i == 0 else body, (i - 1) % DEEP)
                leave(BODIES - 1, DEEP - 1)
                for i in range(DEEP):
                    act.wait_ge(s_saved[i], 16 * BODIES + 16)

            @block.vector
            def _(dve):
                dve.sem_inc(s["xT_out"], 2)
                dve.sem_inc(s["gated"], 2)
                dve.wait_ge(s["table_in"], 16)
                nc.vector.tensor_copy(table_f[:, :], table[:, :]).then_inc(s["table_f"], 1)
                dve.wait_ge(s["table_T"], 1)
                nc.vector.tensor_copy(idx_all[:, :], ps_x[0][:, 0:P]).then_inc(s["idx_made"], 1)
                nc.vector.drain()
                for i in range(DEEP):
                    nc.vector.tensor_copy(idx[i][:, :], idx_all[:, i * HALVES:(i + 1) * HALVES]).then_inc(s["idx_set"], 1)

                def xT_copy(body, i):
                    e = body * DEEP + i
                    dve.wait_ge(s["turned"], e + 1 + DEEP)
                    if not (isinstance(body, int) and e < 2):
                        dve.wait_ge(s["h"], e - 1)
                    nc.vector.tensor_copy(xT[i % 2][:, :, :], ps_x[i % 2][:, :].rearrange("p (k s) -> p k s", k=KD)).then_inc(s["xT_out"], 1)

                def idx_next(body, i):
                    e = body * DEEP + i
                    nc.vector.tensor_copy(idx[i][:, :], idx_all[:, bass.ds(e * HALVES + DEEP * HALVES, HALVES)]).then_inc(s["idx_set"], 1)

                def gate(body, i):
                    e = body * DEEP + i
                    dve.wait_ge(s["silu"], e + 1)
                    dve.wait_ge(s["y"], e + 1 + DEEP - 2)
                    nc.vector.tensor_tensor(g[i % 2][:, :], sg[i % 2][:, :], ps_h[i % 2][:, CAP0:2 * CAP0], ALU.mult).then_inc(s["gated"], 1)

                xT_copy(0, 0)
                idx_next(0, 0)
                for i in range(1, DEEP):
                    xT_copy(0, i)
                    idx_next(0, i)
                    gate(0, i - 1)
                with dve.Fori(1, BODIES - 1) as body:
                    for i in range(DEEP):
                        xT_copy(body, i)
                        idx_next(body, i)
                        gate(body - 1 if i == 0 else body, (i - 1) % DEEP)
                for i in range(DEEP):
                    xT_copy(BODIES - 1, i)
                    gate(BODIES - 2 if i == 0 else BODIES - 1, (i - 1) % DEEP)
                gate(BODIES - 1, DEEP - 1)


def combine0_stage(nc, c, io, d):
    R = NT * TOP0
    with ExitStack() as ctx:
        st = Store(nc, ctx, "c0")
        s = st.sems("x_in0 x_in1 slots_in rows0 rows1 added normed turned xT_out x_saved0 x_saved1 xT_saved")
        slots, weight = st.sb("slots", [P, B, R], U32), st.sb("weight", [P, B, R])
        x4, rows = [st.sb(f"x4{i}", [P, NT, D]) for i in range(2)], [st.sb(f"rows{i}", [P, R, D]) for i in range(2)]
        idx, share = [st.sb(f"idx{i}", [P, R], U32) for i in range(2)], [st.sb(f"share{i}", [P, R]) for i in range(2)]
        carry, carry_v = st.sb("carry", [P, 2]), st.sb("carry_v", [P, 2])
        xn = st.sb("xn", [P, NT, D])
        xT = st.sb("xT", [P, KD, S])
        nb = norm_buffers(st)
        ps_x = [st.ps(f"x{i}") for i in range(KD)]
        s_x, s_rows, s_saved = (s["x_in0"], s["x_in1"]), (s["rows0"], s["rows1"]), (s["x_saved0"], s["x_saved1"])
        with nc.Block() as block:
            @block.sync
            def _(sp):
                def load(b, par):
                    sp.dma_start(x4[par][:, :, :], at(d["x1"], b).rearrange("(t p) f -> p t f", p=P)).then_inc(s_x[par], 16)

                def save(b, par):
                    sp.wait_ge(s["added"], b + 1 + 2)
                    sp.dma_start(at(d["x2"], b).rearrange("(t p) f -> p t f", p=P), x4[par][:, :, :]).then_inc(s_saved[par], 16)
                    sp.wait_ge(s["xT_out"], KD * b + 2 * KD)
                    sp.dma_start(at(d["xT2"], b).rearrange("(k p) s -> p k s", p=P), xT[:, :, :]).then_inc(s["xT_saved"], 16)

                sp.sem_inc(s["xT_saved"], 16)
                sp.dma_start(slots[:, :, :], d["slots0"].rearrange("b p r -> p b r")).then_inc(s["slots_in"], 16)
                sp.dma_start(weight[:, :, :], d["weights0"].rearrange("b p r -> p b r")).then_inc(s["slots_in"], 16)
                for par in range(2):
                    load(par, par)
                with sp.Fori(0, B // 2 - 1) as pair:
                    for par in range(2):
                        save(pair * 2 + par, par)
                        sp.wait_ge(s_saved[par], pair * 16 + 16)
                        load(pair * 2 + (par + 2), par)
                for par in range(2):
                    save(B - 2 + par, par)
                for par in range(2):
                    sp.wait_ge(s_saved[par], 16 * B // 2)
                sp.wait_ge(s["xT_saved"], 16 * B + 16)

            @block.gpsimd
            def _(pool):
                pool.wait_ge(s["slots_in"], 32)
                with pool.Fori(0, B // 2) as pair:
                    for par in range(2):
                        b = pair * 2 + par
                        pool.wait_ge(s["added"], b + 1)
                        nc.gpsimd.tensor_tensor(carry[:, par:par + 1], c["ones"][:, 0:1], c["ones"][:, 0:1], ALU.mult)
                        nc.gpsimd.tensor_copy(idx[par][:, :], slots[:, bass.ds(b, 1), :].rearrange("p a r -> p (a r)"))
                        nc.gpsimd.drain()
                        for r in range(R):
                            nc.gpsimd.indirect_dma_start(out=rows[par][:, r, :], out_offset=None, in_=d["y0"],
                                                         in_offset=bass.IndirectOffsetOnAxis(ap=idx[par][:, r:r + 1], axis=0),
                                                         ).then_inc(s_rows[par], 16)

            @block.tensor
            def _(pe):
                with pe.Fori(0, B) as b:
                    pe.wait_ge(s["normed"], b + 1)
                    for k in range(KD):
                        for t in range(NT):
                            last = nc.tensor.transpose(ps_x[k][:, t * P:(t + 1) * P], xn[:, t, k * P:(k + 1) * P], c["ident"][:, :])
                    last.then_inc(s["turned"], 1)

            @block.scalar
            def _(act):
                act.sem_inc(s["xT_out"], KD)
                with act.Fori(0, B) as b:
                    act.wait_ge(s["turned"], b + 1)
                    act.wait_ge(s["xT_saved"], b * 16 + 16)
                    for k in range(KD):
                        nc.scalar.copy(xT[:, k, :], ps_x[k][:, :]).then_inc(s["xT_out"], 1)

            @block.vector
            def _(dve):
                dve.sem_inc(s["added"], 2)
                dve.wait_ge(s["slots_in"], 32)
                with dve.Fori(0, B // 2) as pair:
                    for par in range(2):
                        b = pair * 2 + par
                        nc.vector.tensor_copy(share[par][:, :], weight[:, bass.ds(b, 1), :].rearrange("p a r -> p (a r)"))
                        nc.vector.drain()
                        dve.wait_ge(s_x[par], pair * 16 + 16)
                        dve.wait_ge(s_rows[par], pair * (16 * R) + 16 * R)
                        for j in range(TOP0):
                            for t in range(NT):
                                r = t * TOP0 + j
                                last = nc.vector.scalar_tensor_tensor(out=x4[par][:, t, :], in0=rows[par][:, r, :],
                                                                      scalar=share[par][:, r:r + 1], in1=x4[par][:, t, :],
                                                                      op0=ALU.mult, op1=ALU.add)
                            nc.vector.drain() if j < TOP0 - 1 else last.then_inc(s["added"], 1)
                        nc.vector.drain()
                        dve.wait_ge(s["xT_out"], KD * b + KD)
                        nc.vector.memset(carry_v[:, par:par + 1], 0.0)
                        layer_norm(nc, x4[par], *nb, xn, 1e-5).then_inc(s["normed"], 1)


def attention_stage(nc, c, io, d):
    GROUPS = 6
    LOADS = 5
    LAG_V = 5
    LAG_N = 6
    with ExitStack() as ctx:
        st = Store(nc, ctx, "a1")
        s = st.sems("in0 in1 group grouped scores maxed exped turned evac_d evac_a pv o_copied spread "
                    "recip_mm normed saved0 saved1")
        W = 4 * DH1
        x = [st.sb(f"x{i}", [P, KD, S]) for i in range(2)]
        y = [st.sb(f"y{i}", [P, KD, S]) for i in range(2)]
        wq, wk, wv = ([st.sb(f"{n}{i}", [P, KD, W]) for i in range(2)] for n in ("wq", "wk", "wv"))
        qz = [st.sb(f"qz{i}", [P, 4, S]) for i in range(2)]
        kT = [st.sb(f"kT{i}", [P, 2, S]) for i in range(2)]
        v = [st.sb(f"v{i}", [P, NT, W]) for i in range(2)]
        prob = [st.sb(f"prob{i}", [P, S]) for i in range(DEEP)]
        nmax, total = st.sb("nmax", [P, BODY]), st.sb("total", [P, BODY])
        recip, spread = st.sb("recip", [P, NU]), st.sb("spread", [P, 2, NT, 2, DH1])
        pT = [st.sb(f"pT{i}", [P, NT, S]) for i in range(4)]
        o_sb = [st.sb(f"o_sb{i}", [P, S]) for i in range(2)]
        o_n = [st.sb(f"o_n{i}", [P, 2, S]) for i in range(2)]
        ps_s = [st.ps(f"s{i}") for i in range(2)]
        ps_t = [st.ps(f"t{i}") for i in range(2)]
        ps_o = [st.ps(f"o{i}") for i in range(2)]
        ps_r = st.ps("r")
        ps_p = st.ps("p")
        s_in, s_saved = (s["in0"], s["in1"]), (s["saved0"], s["saved1"])
        PAIR = 2 * NT

        def group_of(step):
            w = step % NU - 3
            return w // 2 if 0 <= w < 2 * GROUPS and w % 2 == 0 else None

        with nc.Block() as block:
            @block.sync
            def _(sp):
                def load(b, quad):
                    par = quad % 2
                    cols = slice(quad * W, (quad + 1) * W)
                    sp.wait_ge(s["group"], (b * QUADS + quad) * GROUPS + GROUPS)
                    sp.dma_start(x[par][:, :, :], at(d["xT2"], b).rearrange("(k p) s -> p k s", p=P)).then_inc(s_in[par], 16)
                    sp.dma_start(y[par][:, :, :], at(d["ctxT"], b).rearrange("(k p) s -> p k s", p=P)).then_inc(s_in[par], 16)
                    for dst, src in ((wq, io["L1_xattn_w_q"]), (wk, io["L1_xattn_w_k"]), (wv, io["L1_xattn_w_v"])):
                        sp.dma_start(dst[par][:, :, :], src[:, cols].rearrange("(k p) f -> p k f", p=P)).then_inc(s_in[par], 16)

                def save(n, par):
                    sp.wait_ge(s["normed"], n * 2 + 2 + 1)
                    sp.dma_start(at(d["o1"].rearrange("b q p s -> (b q) p s"), n).rearrange("(a p) s -> p a s", p=P),
                                 o_n[par][:, :, :]).then_inc(s_saved[par], 16)

                sp.sem_inc(s["saved0"], 16)
                sp.sem_inc(s["saved1"], 16)
                for quad in range(QUADS):
                    load(0, quad)
                    if quad >= 2:
                        save(quad - 2, quad % 2)
                with sp.Fori(1, B) as b:
                    for quad in range(QUADS):
                        load(b, quad)
                        save(b * QUADS + quad - 2, quad % 2)
                save(ITEMS - 2, 0)
                save(ITEMS - 1, 1)
                for par in range(2):
                    sp.wait_ge(s_saved[par], 16 * (ITEMS // 2) + 16)

            @block.tensor
            def _(pe):
                pe.sem_inc(s["turned"], DEEP)
                pe.sem_inc(s["pv"], 2)
                pe.sem_inc(s["group"], 2 * GROUPS)
                pe.sem_inc(s["recip_mm"], 2)

                def project(body, par, g):
                    i0 = body * 2 + par
                    if g == 0:
                        pe.wait_ge(s_in[par], body * (LOADS * 16) + LOADS * 16)
                    pe.wait_ge(s["grouped"], i0 * GROUPS + g + 1)
                    if g < 4:
                        wt, src = ((wq, x), (wk, y))[g % 2]
                        for k in range(KD):
                            last = nc.tensor.matmul(ps_p[:, :], wt[par][:, k, g // 2 * P:(g // 2 + 1) * P], src[par][:, k, :],
                                                    start=k == 0, stop=k == KD - 1)
                    else:
                        for t in range(2):
                            tile = (g - 4) * 2 + t
                            for k in range(KD):
                                last = nc.tensor.matmul(ps_p[:, t * W:(t + 1) * W], y[par][:, k, tile * P:(tile + 1) * P],
                                                        wv[par][:, k, :], start=k == 0, stop=k == KD - 1)
                    last.then_inc(s["group"], 1)

                def run(body, step, first=False, last=False, final=False):
                    now = lagged(body, step, 0, first, last)
                    if now:
                        par, h, t = step // NU, step % NU // NT, step % NT
                        if step % NU == 0:
                            pe.wait_ge(s["grouped"], (body * 2 + par) * GROUPS + GROUPS + 1)
                        pe.wait_ge(s["exped"], body * BODY + step + 1 + DEEP - 2)
                        nc.tensor.matmul(ps_s[step % 2][:, :], qz[par][:, h, t * P:(t + 1) * P], kT[par][:, h // 2, :],
                                         start=True, stop=True).then_inc(s["scores"], 1)
                    unit = lagged(body, step, LAG_T, first, last)
                    if unit:
                        ub, w = unit
                        pe.wait_ge(s["exped"], ub * BODY + w + 1 + DEEP)
                        pe.wait_ge((s["evac_d"], s["evac_a"])[w % 2], ub * NU + w // 2 + 1)
                        for k in range(NT):
                            op = nc.tensor.transpose(ps_t[w % 2][:, k * P:(k + 1) * P],
                                                     prob[w % DEEP][:, k * P:(k + 1) * P], c["ident"][:, :])
                        op.then_inc(s["turned"], 1)
                    if now and group_of(step) is not None and not (final and step >= NU):
                        par = step // NU
                        project(body if par == 0 else body + 1, 1 - par, group_of(step))
                    unit = lagged(body, step, LAG_V, first, last)
                    if unit and unit[1] % PAIR == PAIR - 1:
                        ub, w = unit
                        par, a = w // NU, w // PAIR % 2
                        pe.wait_ge(s["evac_d"], ub * NU + w // 2 + 1 + 1)
                        pe.wait_ge(s["evac_a"], ub * NU + w // 2 + 1 + 1)
                        pe.wait_ge(s["o_copied"], ub * 4 + w // PAIR + 1)
                        for k in range(NT):
                            for h in range(2):
                                head = a * 2 + h
                                op = nc.tensor.matmul(ps_o[a][h * DH1:(h + 1) * DH1, :],
                                                      v[par][:, k, head * DH1:(head + 1) * DH1], pT[head][:, k, :],
                                                      start=k == 0, stop=k == NT - 1)
                        op.then_inc(s["pv"], 1)
                    unit = lagged(body, step, LAG_N, first, last)
                    if unit and unit[1] % PAIR == PAIR - 1:
                        ub, w = unit
                        pe.wait_ge(s["spread"], ub * 4 + w // PAIR + 1)
                        pe.wait_ge(s["normed"], ub * 4 + w // PAIR + 1)
                        for t in range(NT):
                            op = nc.tensor.transpose(ps_r[:, t * P:(t + 1) * P],
                                                     spread[:, w // PAIR % 2, t, :, :].rearrange("p h f -> p (h f)"), c["ident"][:, :])
                        op.then_inc(s["recip_mm"], 1)

                for g in range(GROUPS):
                    project(0, 0, g)
                for step in range(BODY):
                    run(0, step, first=True)
                with pe.Fori(1, BODIES - 1) as body:
                    for step in range(BODY):
                        run(body, step)
                for step in range(BODY):
                    run(BODIES - 1, step, final=True)
                for step in range(LAG_N + 1):
                    run(BODIES, step, last=True)

            @block.vector
            def _(dve):
                dve.sem_inc(s["evac_d"], 1)
                dve.sem_inc(s["normed"], 1)
                dve.sem_inc(s["grouped"], 1)
                for par in range(2):
                    nc.vector.memset(qz[par][:, :, :].rearrange("p h s -> p (h s)"), 0.0)
                nc.vector.drain()

                def group_out(body, par, g):
                    dve.wait_ge(s["group"], (body * 2 + par) * GROUPS + g + 1 + 2 * GROUPS)
                    if g < 4 and g % 2 == 0:
                        for h in range(2):
                            rows = slice(h * DH1, (h + 1) * DH1)
                            op = nc.vector.tensor_scalar(qz[par][rows, g + h, :], ps_p[rows, :], DH1 ** -0.5, None, ALU.mult)
                    elif g < 4:
                        op = nc.vector.tensor_copy(kT[par][:, g // 2, :], ps_p[:, :])
                    else:
                        op = nc.vector.tensor_copy(v[par][:, (g - 4) * 2:(g - 4) * 2 + 2, :],
                                                   ps_p[:, :].rearrange("p (t f) -> p t f", t=2))
                    op.then_inc(s["grouped"], 1)

                def run(body, step, first=False, last=False, final=False):
                    now = lagged(body, step, 0, first, last)
                    if now:
                        dve.wait_ge(s["scores"], body * BODY + step + 1)
                        nc.vector.tensor_reduce(nmax[:, step:step + 1], ps_s[step % 2][:, :], AX, ALU.max,
                                                negate=True).then_inc(s["maxed"], 1)
                    unit = lagged(body, step, LAG_T, first, last)
                    if unit and unit[1] % 2 == 0:
                        ub, w = unit
                        dve.wait_ge(s["turned"], ub * BODY + w + 1 + DEEP)
                        if w % PAIR == 0:
                            dve.wait_ge(s["pv"], ub * 4 + w // PAIR + 1)
                        nc.vector.tensor_copy(pT[w // NT % 4][:, :, w % NT * P:(w % NT + 1) * P],
                                              ps_t[0][:, :].rearrange("p (k s) -> p k s", k=NT)).then_inc(s["evac_d"], 1)
                    if now and group_of(step - 1) is not None and not (final and step >= NU):
                        par = step // NU
                        group_out(body if par == 0 else body + 1, 1 - par, group_of(step - 1))
                    if unit and unit[1] % PAIR == PAIR - 1:
                        ub, w = unit
                        par, a = w // NU, w // PAIR % 2
                        dve.wait_ge(s["exped"], ub * BODY + w + 1 + DEEP)
                        dve.wait_ge(s["recip_mm"], ub * 4 + w // PAIR + 1)
                        nc.vector.reciprocal(recip[:, a * PAIR:(a + 1) * PAIR], total[:, w + 1 - PAIR:w + 1])
                        nc.vector.drain()
                        nc.vector.tensor_copy(spread[:, a, :, :, :],
                                              recip[:, a * PAIR:(a + 1) * PAIR].rearrange("p (h t o) -> p t h o", h=2, o=1)
                                              .to_broadcast([P, NT, 2, DH1])).then_inc(s["spread"], 1)
                    unit = lagged(body, step, LAG_N + 1, first, last)
                    if unit and unit[1] % PAIR == PAIR - 1:
                        ub, w = unit
                        par, a = w // NU, w // PAIR % 2
                        dve.wait_ge(s["recip_mm"], ub * 4 + w // PAIR + 1 + 2)
                        dve.wait_ge(s["o_copied"], ub * 4 + w // PAIR + 1 + 2)
                        dve.wait_ge(s_saved[par], ub * 16 + 16)
                        nc.vector.tensor_tensor(o_n[par][:, a, :], o_sb[a][:, :], ps_r[:, :], ALU.mult).then_inc(s["normed"], 1)

                for g in range(GROUPS):
                    group_out(0, 0, g)
                for step in range(BODY):
                    run(0, step, first=True)
                with dve.Fori(1, BODIES - 1) as body:
                    for step in range(BODY):
                        run(body, step)
                for step in range(BODY):
                    run(BODIES - 1, step, final=True)
                for step in range(LAG_N + 2):
                    run(BODIES, step, last=True)

            @block.scalar
            def _(act):
                act.sem_inc(s["exped"], DEEP)
                act.sem_inc(s["evac_a"], 1)
                act.sem_inc(s["o_copied"], 2)

                def run(body, step, first=False, last=False):
                    if lagged(body, step, 0, first, last):
                        act.wait_ge(s["maxed"], body * BODY + step + 1)
                        act.wait_ge(s["turned"], body * BODY + step + 1)
                        nc.scalar.activation(prob[step % DEEP][:, :], ps_s[step % 2][:, :], ACT.Exp, bias=nmax[:, step:step + 1],
                                             accum_out=total[:, step:step + 1]).then_inc(s["exped"], 1)
                    unit = lagged(body, step, LAG_T, first, last)
                    if unit and unit[1] % 2 == 1:
                        ub, w = unit
                        act.wait_ge(s["turned"], ub * BODY + w + 1 + DEEP)
                        if w % PAIR == 1:
                            act.wait_ge(s["pv"], ub * 4 + w // PAIR + 1)
                        nc.scalar.copy(pT[w // NT % 4][:, :, w % NT * P:(w % NT + 1) * P],
                                       ps_t[1][:, :].rearrange("p (k s) -> p k s", k=NT)).then_inc(s["evac_a"], 1)
                    unit = lagged(body, step, LAG_N, first, last)
                    if unit and unit[1] % PAIR == PAIR - 1:
                        ub, w = unit
                        a = w // PAIR % 2
                        act.wait_ge(s["pv"], ub * 4 + w // PAIR + 1 + 2)
                        if not (first and w < PAIR):
                            act.wait_ge(s["normed"], ub * 4 + w // PAIR)
                        nc.scalar.copy(o_sb[a][:, :], ps_o[a][:, :]).then_inc(s["o_copied"], 1)

                for step in range(BODY):
                    run(0, step, first=True)
                with act.Fori(1, BODIES) as body:
                    for step in range(BODY):
                        run(body, step)
                for step in range(LAG_N + 1):
                    run(BODIES, step, last=True)

def route1_stage(nc, c, io, d):
    GC = E1 + 2
    with ExitStack() as ctx:
        st = Store(nc, ctx, "r1")
        s = st.sems("wo_in norm_in w_in o_in x_in product summed affine turned xT_out logits maxed exped picked counted placed "
                    "h h_out m m_out scattered slots_free base_saved a_saved slots_saved table_zero")
        KO = HEADS * DH1 // P
        wo = st.sb("wo", [P, KO, D])
        wg = st.sb("wg", [P, KD, GC])
        w1, w2 = st.sb("w1", [P, KD, I1]), st.sb("w2", [P, KI, D])
        b1, b2 = st.sb("b1", [P, KI]), st.sb("b2", [P, D])
        nw, nbias = st.sb("nw", [P, D]), st.sb("nbias", [P, D])
        o4, x4 = st.sb("o4", [P, KO, S]), st.sb("x4", [P, NT, D])
        x3, xn, a = st.sb("x3", [P, NT, D]), st.sb("xn", [P, NT, D]), st.sb("a", [P, NT, D])
        base, mlp = st.sb("base", [P, NT, D]), st.sb("mlp", [P, NT, D])
        xT = st.sb("xT", [P, KD, S])
        hT = st.sb("hT", [P, KI, S])
        mix, nmix, emix, smix = st.sb("mix", [P, NT, 2]), st.sb("nmix", [P, NT]), st.sb("emix", [P, NT, 2]), st.sb("smix", [P, NT])
        nb = norm_buffers(st)
        r = Router(nc, st, c, E1, TOP1, CAP1, drop=True)
        ps_y = [st.ps(f"y{i}") for i in range(2)]
        ps_x = [st.ps(f"x{i}") for i in range(KD)]
        ps_l, ps_p = st.ps("l"), st.ps("p")
        ps_h = [st.ps(f"h{i}") for i in range(2)]
        both = ps_l[:, 0:NT * GC].rearrange("p (t e) -> p t e", t=NT)
        logits, mixes = both[:, :, 0:E1], both[:, :, E1:GC]

        with nc.Block() as block:
            @block.sync
            def _(sp):
                def load(b):
                    sp.dma_start(o4[:, :, :], at(d["o1"].rearrange("b q f s -> b (q f) s"), b).rearrange("(k p) s -> p k s", p=P)).then_inc(s["o_in"], 16)
                    sp.dma_start(x4[:, :, :], at(d["x2"], b).rearrange("(t p) f -> p t f", p=P)).then_inc(s["x_in"], 16)

                def save_a(b):
                    sp.wait_ge(s["affine"], b + 1)
                    sp.dma_start(at(d["a1"].rearrange("(b s) f -> b s f", b=B), b).rearrange("(t p) f -> p t f", p=P), a[:, :, :]).then_inc(s["a_saved"], 16)

                def batch(b, load_next=True, save_next=True):
                    sp.wait_ge(s["placed"], b + 1)
                    sp.dma_start(at(d["slots1"], b), r.slot_read[:, :]).then_inc(s["slots_saved"], 16)
                    sp.dma_start(at(d["weights1"], b), r.weight[:, :]).then_inc(s["slots_saved"], 16)
                    if load_next:
                        sp.wait_ge(s["summed"], b + 2 + 1)
                        load(b + 2)
                    if save_next:
                        save_a(b + 1)
                    sp.wait_ge(s["m_out"], 2 * b + 2 + 2)
                    sp.dma_start(at(d["base"], b).rearrange("(t p) f -> p t f", p=P), base[:, :, :]).then_inc(s["base_saved"], 16)

                sp.sem_inc(s["slots_saved"], 32)
                sp.sem_inc(s["base_saved"], 16)
                sp.dma_start(wo[:, :, :], io["L1_xattn_w_o"].rearrange("(k p) f -> p k f", p=P)).then_inc(s["wo_in"], 16)
                load(0)
                for dst, src in ((nw, io["L1_ffn_attn_nw"]), (nbias, io["L1_ffn_attn_nb"])):
                    sp.dma_start(dst[:, :], src.rearrange("(a f) -> a f", a=1).to_broadcast([P, D])).then_inc(s["norm_in"], 16)
                sp.dma_start(w1[:, :, :], io["L1_ffn_res_inter_w"].rearrange("(k p) f -> p k f", p=P)).then_inc(s["w_in"], 16)
                sp.dma_start(w2[:, :, :], io["L1_ffn_res_output_w"].rearrange("(k p) f -> p k f", p=P)).then_inc(s["w_in"], 16)
                sp.dma_start(b2[:, :], io["L1_ffn_res_output_b"].rearrange("(a f) -> a f", a=1).to_broadcast([P, D])).then_inc(s["w_in"], 16)
                with nc.allow_non_contiguous_dma(reason="small columns"):
                    sp.dma_start(b1[:, :], io["L1_ffn_res_inter_b"].rearrange("(k p) -> p k", p=P)).then_inc(s["w_in"], 16)
                    sp.dma_start(wg[:, :, 0:E1], io["L1_ffn_wg"].rearrange("(k p) e -> p k e", p=P)).then_inc(s["w_in"], 16)
                    sp.dma_start(wg[:, :, E1:GC], io["L1_ffn_res_coef"].rearrange("(k p) e -> p k e", p=P)).then_inc(s["w_in"], 16)
                sp.dma_start(d["table1"].rearrange("(p k) o -> p (k o)", p=P), c["zeros"][:, 0:E1 * CAP1 // P].bitcast(U32)).then_inc(s["table_zero"], 16)
                sp.wait_ge(s["summed"], 1 + 1)
                load(1)
                save_a(0)
                with sp.Fori(0, B - 2) as b:
                    batch(b)
                batch(B - 2, load_next=False)
                batch(B - 1, load_next=False, save_next=False)
                sp.wait_ge(s["base_saved"], 16 * B + 16)
                sp.wait_ge(s["a_saved"], 16 * B)
                sp.wait_ge(s["slots_saved"], 32 * B + 32)

            @block.gpsimd
            def _(pool):
                pool.sem_inc(s["slots_free"], 1)
                pool.wait_ge(s["table_zero"], 16)
                with pool.Fori(0, B) as b:
                    pool.wait_ge(s["placed"], b + 1)
                    r.scatter(b, d["table1"], s["scattered"], s["slots_free"])

            @block.tensor
            def _(pe):
                def product(b):
                    pe.wait_ge(s["o_in"], b * 16 + 16)
                    pe.wait_ge(s["summed"], b + 1)
                    for t in range(NT):
                        for k in range(KO):
                            last = nc.tensor.matmul(ps_y[t // 2][:, t % 2 * D:(t % 2 + 1) * D], o4[:, k, t * P:(t + 1) * P],
                                                    wo[:, k, :], start=k == 0, stop=k == KO - 1)
                        if t % 2:
                            last.then_inc(s["product"], 1)

                def batch(b, product_ahead=True):
                    pe.wait_ge(s["affine"], b + 1)
                    pe.wait_ge(s["m_out"], 2 * b + 2)
                    for k in range(KD):
                        for t in range(NT):
                            last = nc.tensor.transpose(ps_x[k][:, t * P:(t + 1) * P], a[:, t, k * P:(k + 1) * P], c["ident"][:, :])
                    last.then_inc(s["turned"], 1)
                    pe.wait_ge(s["xT_out"], KD * b + KD)
                    for t in range(NT):
                        for k in range(KD):
                            last = nc.tensor.matmul(ps_l[:, t * GC:(t + 1) * GC], xT[:, k, t * P:(t + 1) * P], wg[:, k, :],
                                                    start=k == 0, stop=k == KD - 1)
                    last.then_inc(s["logits"], 1)
                    for m in range(KI):
                        pe.wait_ge(s["h_out"], b * KI + m + 1)
                        for k in range(KD):
                            last = nc.tensor.matmul(ps_h[m % 2][:, :], w1[:, k, m * P:(m + 1) * P], xT[:, k, :],
                                                    start=k == 0, stop=k == KD - 1)
                        last.then_inc(s["h"], 1)
                        if m == 0:
                            pe.wait_ge(s["picked"], b + 1)
                            r.count_earlier(ps_p).then_inc(s["counted"], 1)
                    if product_ahead:
                        product(b + 2)
                    pe.wait_ge(s["h_out"], b * KI + KI + 2)
                    for t in range(NT):
                        for m in range(KI):
                            last = nc.tensor.matmul(ps_x[t // 2][:, t % 2 * D:(t % 2 + 1) * D], hT[:, m, t * P:(t + 1) * P],
                                                    w2[:, m, :], start=m == 0, stop=m == KI - 1)
                        if t % 2:
                            last.then_inc(s["m"], 1)

                pe.sem_inc(s["m"], 2)
                pe.wait_ge(s["wo_in"], 16)
                product(0)
                product(1)
                pe.wait_ge(s["w_in"], 16 * 6)
                with pe.Fori(0, B - 2) as b:
                    batch(b)
                batch(B - 2, product_ahead=False)
                batch(B - 1, product_ahead=False)

            @block.scalar
            def _(act):
                act.sem_inc(s["h_out"], 2)
                act.wait_ge(s["w_in"], 16 * 6)
                with act.Fori(0, B) as b:
                    act.wait_ge(s["turned"], b + 1)
                    for k in range(KD):
                        nc.scalar.copy(xT[:, k, :], ps_x[k][:, :]).then_inc(s["xT_out"], 1)
                    act.wait_ge(s["maxed"], b + 1)
                    r.exponentials(logits)
                    for t in range(NT):
                        last = nc.scalar.activation(emix[:, t, :], mixes[:, t, :], ACT.Exp, bias=nmix[:, t:t + 1],
                                                    accum_out=smix[:, t:t + 1])
                    last.then_inc(s["exped"], 1)
                    act.wait_ge(s["m"], 2 * b + 2)
                    for m in range(KI):
                        act.wait_ge(s["h"], b * KI + m + 1)
                        nc.scalar.activation(hT[:, m, :], ps_h[m % 2][:, :], ACT.Gelu_apprx_tanh, bias=b1[:, m:m + 1]).then_inc(s["h_out"], 1)

            @block.vector
            def _(dve):
                def norms(b):
                    dve.wait_ge(s["x_in"], b * 16 + 16)
                    for half in range(2):
                        dve.wait_ge(s["product"], 2 * b + half + 1)
                        last = nc.vector.tensor_tensor(x3[:, 2 * half:2 * half + 2, :], x4[:, 2 * half:2 * half + 2, :],
                                                       ps_y[half][:, :].rearrange("p (t f) -> p t f", t=2), ALU.add)
                    last.then_inc(s["summed"], 1)
                    nc.vector.drain()
                    layer_norm(nc, x3, *nb, xn, 1e-5)
                    nc.vector.drain()
                    nc.vector.memset(r.sums[:, :], 0.0)
                    if not (isinstance(b, int) and b == 0):
                        dve.wait_ge(s["turned"], b)
                        dve.wait_ge(s["a_saved"], 16 * b)
                    nc.vector.memset(r.pos[:, :], 0.0)
                    layer_norm(nc, xn, *nb, a, 1e-12)
                    nc.vector.drain()
                    for t in range(NT):
                        nc.vector.tensor_tensor(a[:, t, :], a[:, t, :], nw[:, :], ALU.mult)
                    nc.vector.drain()
                    for t in range(NT):
                        last = nc.vector.tensor_tensor(a[:, t, :], a[:, t, :], nbias[:, :], ALU.add)
                    last.then_inc(s["affine"], 1)

                def batch(b, has_next=True):
                    dve.wait_ge(s["logits"], b + 1)
                    nc.vector.tensor_reduce(r.nmax[:, :], logits, AX, ALU.max, negate=True)
                    nc.vector.tensor_reduce(nmix[:, :], mixes, AX, ALU.max, negate=True).then_inc(s["maxed"], 1)
                    dve.wait_ge(s["exped"], b + 1)
                    nc.vector.reciprocal(smix[:, :], smix[:, :])
                    r.pick().then_inc(s["picked"], 1)
                    nc.vector.tensor_tensor(mix[:, :, :], emix[:, :, :], r.tail(smix[:, :]).to_broadcast([P, NT, 2]), ALU.mult)
                    dve.wait_ge(s["base_saved"], b * 16 + 16)
                    nc.vector.tensor_tensor(base[:, :, :], x3[:, :, :], xn[:, :, :], ALU.add)
                    dve.wait_ge(s["slots_saved"], b * 32 + 32)
                    dve.wait_ge(s["slots_free"], b + 1)
                    dve.wait_ge(s["counted"], b + 1)
                    r.place(ps_p)
                    nc.vector.drain()
                    nc.vector.tensor_tensor(r.weight[:, :], r.weight[:, :], mix[:, :, 1], ALU.mult).then_inc(s["placed"], 1)
                    if has_next:
                        norms(b + 1)
                    for half in range(2):
                        dve.wait_ge(s["m"], 2 * b + half + 1 + 2)
                        rows = slice(2 * half, 2 * half + 2)
                        nc.vector.tensor_tensor(mlp[:, rows, :], ps_x[half][:, :].rearrange("p (t f) -> p t f", t=2),
                                                b2[:, :].rearrange("p (o f) -> p o f", o=1).to_broadcast([P, 2, D]), ALU.add)
                        nc.vector.drain()
                        for t in range(2 * half, 2 * half + 2):
                            last = nc.vector.scalar_tensor_tensor(out=base[:, t, :], in0=mlp[:, t, :], scalar=mix[:, t, 0:1],
                                                                  in1=base[:, t, :], op0=ALU.mult, op1=ALU.add)
                        last.then_inc(s["m_out"], 1)

                dve.sem_inc(s["summed"], 1)
                dve.sem_inc(s["m_out"], 2)
                r.start()
                dve.wait_ge(s["norm_in"], 32)
                norms(0)
                dve.wait_ge(s["w_in"], 16 * 6)
                with dve.Fori(0, B - 1) as b:
                    batch(b)
                batch(B - 1, has_next=False)


def experts1_stage(nc, c, io, d, out):
    HALVES = CAP1 // P
    with ExitStack() as ctx:
        st = Store(nc, ctx, "e1")
        s = st.sems("idx_in w10 w11 w20 w21 b_in rows0 rows1 turned xT_out h h_out y y_out saved0 saved1 "
                    "stored x_in slots_in added out_saved " + " ".join(f"taken{b}" for b in range(B)))
        R = NT * TOP1
        slots, weight = st.sb("slots", [P, B, R], U32), st.sb("weight", [P, B, R])
        x = st.sb("x", [P, B, NT, D])
        taken = st.sb("taken", [P, B, R, D])
        idx = st.sb("idx", [P, E1, HALVES], U32)
        b1, b2 = st.sb("b1", [P, E1, KI]), st.sb("b2", [P, E1, D])
        rows = [st.sb(f"rows{i}", [P, HALVES, D]) for i in range(2)]
        xT = [st.sb(f"xT{i}", [P, KD, CAP1]) for i in range(2)]
        w1 = [st.sb(f"w1{i}", [P, KD, I1]) for i in range(2)]
        w2 = [st.sb(f"w2{i}", [P, KI, D]) for i in range(2)]
        hT = [st.sb(f"hT{i}", [P, KI, CAP1]) for i in range(2)]
        y = [st.sb(f"y{i}", [P, HALVES, D]) for i in range(2)]
        ps_x = [st.ps(f"x{i}") for i in range(2)]
        ps_h = [st.ps(f"h{i}") for i in range(4)]
        ps_y = [st.ps(f"y{i}") for i in range(2)]
        s_w1, s_w2, s_rows, s_saved = (s["w10"], s["w11"]), (s["w20"], s["w21"]), (s["rows0"], s["rows1"]), (s["saved0"], s["saved1"])
        y_out = d["y1"].rearrange("(e h p) f -> e p h f", p=P, h=HALVES)

        with nc.Block() as block:
            @block.sync
            def _(sp):
                with nc.allow_non_contiguous_dma(reason="token numbers and biases"):
                    sp.dma_start(idx[:, :, :].rearrange("p e h -> p (e h)"), d["table1"].rearrange("(e p) o -> p (e o)", p=P)).then_inc(s["idx_in"], 16)
                    for e in range(E1):
                        sp.dma_start(b1[:, e, :], io["L1_ffn_inter_b"][e].rearrange("(k p) -> p k", p=P)).then_inc(s["b_in"], 16)
                for e in range(E1):
                    sp.dma_start(b2[:, e, :], io["L1_ffn_output_b"][e:e + 1, :].to_broadcast([P, D])).then_inc(s["b_in"], 16)
                for e in range(E1):
                    par = e % 2
                    if e >= 2:
                        sp.wait_ge(s["y"], e - 1)
                    sp.dma_start(w1[par][:, :, :], io["L1_ffn_inter_w"][e].rearrange("(k p) f -> p k f", p=P)).then_inc(s_w1[par], 16)
                    sp.dma_start(w2[par][:, :, :], io["L1_ffn_output_w"][e].rearrange("(k p) f -> p k f", p=P)).then_inc(s_w2[par], 16)
                sp.dma_start(slots[:, :, :], d["slots1"].rearrange("b p r -> p b r")).then_inc(s["slots_in"], 16)
                sp.dma_start(weight[:, :, :], d["weights1"].rearrange("b p r -> p b r")).then_inc(s["slots_in"], 16)
                sp.dma_start(x[:, :, :, :].rearrange("p b t f -> p (b t) f"), d["base"].rearrange("b (t p) f -> p (b t) f", p=P)).then_inc(s["x_in"], 16)
                for b in range(B):
                    sp.wait_ge(s["added"], NT * (b + 1))
                    sp.dma_start(out[b].rearrange("(t p) f -> p t f", p=P), x[:, b]).then_inc(s["out_saved"], 16)
                sp.wait_ge(s["out_saved"], 16 * B)

            @block.gpsimd
            def _(pool):
                pool.wait_ge(s["idx_in"], 16)
                for e in range(E1):
                    if e >= 2:
                        pool.wait_ge(s["turned"], e - 1)
                    for h in range(HALVES):
                        nc.gpsimd.indirect_dma_start(out=rows[e % 2][:, h, :], out_offset=None, in_=d["a1"],
                                                     in_offset=bass.IndirectOffsetOnAxis(ap=idx[:, e, h:h + 1], axis=0),
                                                     ).then_inc(s_rows[e % 2], 16)
                pool.wait_ge(s["slots_in"], 32)
                pool.wait_ge(s["stored"], 1)
                for b in range(B):
                    for r in range(R):
                        nc.gpsimd.indirect_dma_start(out=taken[:, b, r, :], out_offset=None, in_=d["y1"],
                                                     in_offset=bass.IndirectOffsetOnAxis(ap=slots[:, b, r:r + 1], axis=0),
                                                     ).then_inc(s[f"taken{b}"], 16)

            @block.tensor
            def _(pe):
                def turn(e):
                    pe.wait_ge(s_rows[e % 2], 16 * HALVES * (e // 2 + 1))
                    if e >= 2:
                        pe.wait_ge(s["xT_out"], e - 1)
                    for k in range(KD):
                        for h in range(HALVES):
                            last = nc.tensor.transpose(ps_x[e % 2][:, k * CAP1 + h * P:k * CAP1 + (h + 1) * P],
                                                       rows[e % 2][:, h, k * P:(k + 1) * P], c["ident"][:, :])
                    last.then_inc(s["turned"], 1)

                turn(0)
                for e in range(E1):
                    par = e % 2
                    pe.wait_ge(s_w1[par], 16 * (e // 2 + 1))
                    pe.wait_ge(s["xT_out"], e + 1)
                    for m in range(KI):
                        if m % 2 == 0 and e >= 1:
                            pe.wait_ge(s["h_out"], (e - 1) * KI + m + 2)
                        for k in range(KD):
                            last = nc.tensor.matmul(ps_h[m // 2][:, m % 2 * CAP1:(m % 2 + 1) * CAP1], w1[par][:, k, m * P:(m + 1) * P],
                                                    xT[par][:, k, :], start=k == 0, stop=k == KD - 1)
                        if m % 2:
                            last.then_inc(s["h"], 1)
                    if e + 1 < E1:
                        turn(e + 1)
                    pe.wait_ge(s_w2[par], 16 * (e // 2 + 1))
                    if e >= 2:
                        pe.wait_ge(s["y_out"], e - 1)
                    pe.wait_ge(s["h_out"], (e + 1) * KI)
                    for h in range(HALVES):
                        for m in range(KI):
                            last = nc.tensor.matmul(ps_y[par][:, h * D:(h + 1) * D], hT[par][:, m, h * P:(h + 1) * P], w2[par][:, m, :],
                                                    start=m == 0, stop=m == KI - 1)
                    last.then_inc(s["y"], 1)

            @block.scalar
            def _(act):
                act.wait_ge(s["b_in"], 16 * 2 * E1)
                for e in range(E1):
                    par = e % 2
                    if e >= 2:
                        act.wait_ge(s["y"], e - 1)
                    for m in range(KI):
                        if m % 2 == 0:
                            act.wait_ge(s["h"], e * (KI // 2) + m // 2 + 1)
                        nc.scalar.activation(hT[par][:, m, :], ps_h[m // 2][:, m % 2 * CAP1:(m % 2 + 1) * CAP1],
                                             ACT.Gelu_apprx_tanh, bias=b1[:, e, m:m + 1]).then_inc(s["h_out"], 1)
                    if e >= 1:
                        act.wait_ge(s["y_out"], e)
                        act.dma_start(y_out[e - 1], y[1 - par][:, :, :]).then_inc(s_saved[1 - par], 16)
                act.wait_ge(s["y_out"], E1)
                act.dma_start(y_out[E1 - 1], y[1][:, :, :]).then_inc(s["saved1"], 16)
                act.wait_ge(s["saved0"], 16 * E1 // 2)
                act.wait_ge(s["saved1"], 16 * E1 // 2)
                act.sem_inc(s["stored"], 1)

            @block.vector
            def _(dve):
                dve.wait_ge(s["b_in"], 16 * 2 * E1)

                def xT_copy(e):
                    dve.wait_ge(s["turned"], e + 1)
                    if e >= 2:
                        dve.wait_ge(s["h"], (e - 1) * (KI // 2))
                    nc.vector.tensor_copy(xT[e % 2][:, :, :], ps_x[e % 2][:, :].rearrange("p (k s) -> p k s", k=KD)).then_inc(s["xT_out"], 1)

                xT_copy(0)
                for e in range(E1):
                    if e + 1 < E1:
                        xT_copy(e + 1)
                    dve.wait_ge(s["y"], e + 1)
                    if e >= 2:
                        dve.wait_ge(s_saved[e % 2], 16 * (e // 2))
                    nc.vector.tensor_tensor(y[e % 2][:, :, :], ps_y[e % 2][:, :].rearrange("p (h f) -> p h f", h=HALVES),
                                            b2[:, e:e + 1, :].to_broadcast([P, HALVES, D]), ALU.add).then_inc(s["y_out"], 1)
                dve.wait_ge(s["x_in"], 16)
                dve.wait_ge(s["slots_in"], 32)
                for b in range(B):
                    dve.wait_ge(s[f"taken{b}"], 16 * R)
                    for t in range(NT):
                        nc.vector.scalar_tensor_tensor(out=x[:, b, t, :], in0=taken[:, b, t, :], scalar=weight[:, b, t:t + 1],
                                                       in1=x[:, b, t, :], op0=ALU.mult, op1=ALU.add).then_inc(s["added"], 1)


FIRST_LAYER = 5


def build(nc, io, out, last_stage=None):
    def scratch(name, shape, dt=F32):
        return nc.dram_tensor(f"scratch_{name}", shape, dt, kind="Internal").ap()

    d = dict(
        ctxT=scratch("ctxT", (B, D, S)),
        qp=scratch("qp", (B, 3, D, S), BF16),
        kp=scratch("kp", (B, 3, D, S), BF16),
        v0=scratch("v0", (B, QUADS, S, 4 * PAD0)),
        o0=scratch("o0", (ITEMS, P, S)),
        x1=scratch("x1", (B, S, D)), xn1=scratch("xn1", (N, D)),
        slots0=scratch("slots0", (B, P, NT * TOP0), U32), weights0=scratch("weights0", (B, P, NT * TOP0)),
        table0=scratch("table0", (E0 * CAP0, 1), U32), y0=scratch("y0", (E0 * CAP0, D)),
        o1=scratch("o1", (B, QUADS, 4 * DH1, S)), a1=scratch("a1", (N, D)), base=scratch("base", (B, S, D)),
        slots1=scratch("slots1", (B, P, NT * TOP1), U32), weights1=scratch("weights1", (B, P, NT * TOP1)),
        table1=scratch("table1", (E1 * CAP1, 1), U32), y1=scratch("y1", (E1 * CAP1, D)),
        x2=scratch("x2", (B, S, D)), xT2=scratch("xT2", (B, D, S)),
    )
    with ExitStack() as ctx:
        st = Store(nc, ctx, "c")
        c = dict(ones=st.sb("ones", [P, P]), zeros=st.sb("zeros", [P, P]), ident=st.sb("ident", [P, P]),
                            ones16=st.sb("ones16", [P, P], BF16), before=st.sb("before", [P, P], BF16),
                            expert_no=st.sb("expert_no", [P, E0]), token_no=st.sb("token_no", [P, NT]))
        build_constants(nc, c)
        stages = [project_stage, masked_attention_stage, route0_stage, experts0_stage, combine0_stage,
                  attention_stage, route1_stage]
        with nc.cleanup_on_exit():
            for stage in stages[:last_stage][:FIRST_LAYER]:
                stage(nc, c, io, d)
        for stage in stages[:last_stage][FIRST_LAYER:]:
            stage(nc, c, io, d)
        if last_stage is None:
            experts1_stage(nc, c, io, d, out)


_OUT_SHAPE = (B, S, D)


def kernel(**inputs):
    import numpy as np
    import concourse.bacc as bacc
    from concourse.bass_utils import run_bass_kernel_spmd

    nc = bacc.Bacc("TRN2", target_bir_lowering=False, num_devices=1)
    arrays = {f"in_{name}": np.ascontiguousarray(a) for name, a in inputs.items()}
    io = {
        name: nc.dram_tensor(f"in_{name}", inputs[name].shape, mybir.dt.from_np(arrays[f"in_{name}"].dtype),
                             kind="ExternalInput").ap() for name in inputs}
    out = nc.dram_tensor("out_0", _OUT_SHAPE, F32, kind="ExternalOutput").ap()
    build(nc, io, out)
    return run_bass_kernel_spmd(nc, [arrays], core_ids=[0]).results[0]["out_0"]
```

```python
from contextlib import ExitStack

import concourse.bass as bass
from concourse import mybir

P = 128
B, S, D = 4, 512, 256
N = B * S
NT = S // P
KD = D // P
HEADS = 16
DH0, PAD0 = 16, 32
DH1 = 64
QUADS = HEADS // 4
ITEMS = B * QUADS
E0, TOP0, I0, CAP0 = 64, 4, 128, 256
E1, TOP1, I1, CAP1 = 8, 1, 1024, 256
KI = I1 // P
SKIP = 1.0e6

F32 = mybir.dt.float32
BF16 = mybir.dt.bfloat16
U32 = mybir.dt.uint32
I32 = mybir.dt.int32
ALU = mybir.AluOpType
ACT = mybir.ActivationFunctionType
AX = mybir.AxisListType.X

Q_PARTS = (0, 0, 1, 0, 1, 2)
K_PARTS = (0, 1, 0, 2, 1, 0)
STACK = len(Q_PARTS) * DH0


class Store:

    def __init__(self, nc, ctx, prefix):
        self.nc, self.ctx, self.prefix = nc, ctx, prefix

    def sb(self, name, shape, dt=F32):
        return self.ctx.enter_context(self.nc.sbuf_tensor(f"{self.prefix}_{name}", shape, dt))

    def ps(self, name, shape=(P, 512), dt=F32):
        return self.ctx.enter_context(self.nc.psum_tensor(f"{self.prefix}_ps_{name}", list(shape), dt))

    def sems(self, names):
        return {n: self.nc.alloc_semaphore(f"{self.prefix}_{n}") for n in names.split()}


def build_constants(nc, c):
    filled, made = nc.alloc_semaphore("constants_filled"), nc.alloc_semaphore("constants_made")
    ones16_made = nc.alloc_semaphore("constants_ones16")
    with nc.Block() as block:
        @block.vector
        def _(dve):
            nc.vector.memset(c["ones"][:, :], 1.0)
            nc.vector.memset(c["zeros"][:, :], 0.0).then_inc(filled, 1)
            nc.vector.memset(c["ones16"][:, :], 1.0).then_inc(ones16_made, 1)
            dve.wait_ge(ones16_made, 1)

        @block.gpsimd
        def _(pool):
            pool.wait_ge(filled, 1)
            nc.gpsimd.affine_select(out=c["ident"][:, :], in_=c["ones"][:, :], compare_op=ALU.is_equal, fill=0.0, base=0,
                                    pattern=[[-1, P]], channel_multiplier=1).then_inc(made, 1)
            nc.gpsimd.affine_select(out=c["before"][:, :], in_=c["ones"][:, :], compare_op=ALU.is_gt, fill=0.0, base=0,
                                    pattern=[[1, P]], channel_multiplier=-1).then_inc(made, 1)
            nc.gpsimd.iota(c["expert_no"][:, :], pattern=[[1, E0]], base=0, channel_multiplier=0,
                           allow_small_or_imprecise_dtypes=True).then_inc(made, 1)
            nc.gpsimd.iota(c["token_no"][:, :], pattern=[[P, NT]], base=0, channel_multiplier=1,
                           allow_small_or_imprecise_dtypes=True).then_inc(made, 1)
            pool.wait_ge(made, 4)


def layer_norm_part(nc, part, x, stats, mv, var, half, rstd, out, eps):
    v = nc.vector
    if part in (0, 1):
        for t in range(NT)[2 * part:2 * part + 2]:
            last = v.bn_stats(stats[:, t, :], x[:, t, :])
        v.drain()
    elif part == 2:
        for t in range(NT):
            v.bn_aggr(mv[:, t, :], stats[:, t, :])
        v.drain()
        v.tensor_scalar(var[:, :], mv[:, :, 1], eps, None, ALU.add)
        v.drain()
        last = v.tensor_scalar(rstd[:, :].bitcast(I32), var[:, :].bitcast(I32), -0.5, float(0x5F3759DF), ALU.mult, ALU.add)
        v.drain()
    elif part in (3, 4, 5):
        v.tensor_tensor(half[:, :], rstd[:, :], rstd[:, :], ALU.mult)
        v.drain()
        v.tensor_tensor(half[:, :], half[:, :], var[:, :], ALU.mult)
        v.drain()
        v.tensor_scalar(half[:, :], half[:, :], -0.5, 1.5, ALU.mult, ALU.add)
        v.drain()
        last = v.tensor_tensor(rstd[:, :], rstd[:, :], half[:, :], ALU.mult)
        v.drain()
    else:
        for t in range(NT)[2 * (part - 6):2 * (part - 6) + 2]:
            last = v.tensor_scalar(out[:, t, :], x[:, t, :], mv[:, t, 0:1], rstd[:, t:t + 1], ALU.subtract, ALU.mult)
    return last


def layer_norm(nc, x, stats, mv, var, half, rstd, out, eps):
    for part in range(8):
        last = layer_norm_part(nc, part, x, stats, mv, var, half, rstd, out, eps)
    return last


def norm_buffers(st, prefix=""):
    return (st.sb(prefix + "stats", [P, NT, 6]), st.sb(prefix + "mv", [P, NT, 2]),
            st.sb(prefix + "var", [P, NT]), st.sb(prefix + "half", [P, NT]), st.sb(prefix + "rstd", [P, NT]))


def at(ap, i):
    v = ap[bass.ds(i, 1)]
    names = " ".join("abcdefg"[:len(ap.shape) - 1])
    first = names.split(" ", 1)
    rest = " " + first[1] if len(first) > 1 else ""
    return v.rearrange(f"z {names} -> (z {first[0]}){rest}")


def project_stage(nc, c, io, d):
    with ExitStack() as ctx:
        st = Store(nc, ctx, "pj")
        s = st.sems("w_in x_in c_in bias normed turned_x turned_c xT_out cT_out mm v_mm out q_split "
                    "k_split v_out cT_saved parts_saved v_saved mask_in mask_made")
        mask, maskb, pad = c["mask"], c["maskb"], c["pad"]
        w = {n: st.sb(n, [P, KD, D]) for n in "qkv"}
        bcol = {n: st.sb("bcol" + n, [P, KD]) for n in "qk"}
        bq4 = st.sb("bq4", [P, KD])
        bv = st.sb("bv", [P, D])
        x4, c4, xn4 = st.sb("x4", [P, NT, D]), st.sb("c4", [P, NT, D]), st.sb("xn4", [P, NT, D])
        xT, cT = st.sb("xT", [P, KD, S]), st.sb("cT", [P, KD, S])
        q1, k1, rest = st.sb("q1", [P, KD, S]), st.sb("k1", [P, KD, S]), [st.sb(f"rest_{n}", [P, KD, S]) for n in "kq"]
        qp, kp = st.sb("qp", [P, 3, KD, S], BF16), st.sb("kp", [P, 3, KD, S], BF16)
        vp = st.sb("vp", [P, NT, HEADS, PAD0])
        nb = norm_buffers(st)
        tx = [st.ps(f"tx{k}") for k in range(KD)]
        tc = [st.ps(f"tc{k}") for k in range(KD)]
        pq = [st.ps(f"pq{k}") for k in range(KD)]
        pk = [st.ps(f"pk{k}") for k in range(KD)]

        with nc.Block() as block:
            @block.sync
            def _(sp):
                def load_x(b):
                    sp.dma_start(x4[:, :, :], at(io["x"], b).rearrange("(t p) f -> p t f", p=P)).then_inc(s["x_in"], 16)

                def load_c(b):
                    sp.dma_start(c4[:, :, :], at(io["ctx_1024"], b).rearrange("(t p) f -> p t f", p=P)).then_inc(s["c_in"], 16)

                def batch(b, next_x=True, next_c=True):
                    if next_c:
                        sp.wait_ge(s["turned_c"], b + 1)
                        load_c(b + 1)
                    sp.wait_ge(s["cT_out"], KD * b + KD)
                    sp.dma_start(at(d["ctxT"], b).rearrange("(k p) s -> p k s", p=P), cT[:, :, :]).then_inc(s["cT_saved"], 16)
                    if next_x:
                        sp.wait_ge(s["normed"], b + 2)
                        load_x(b + 2)
                    sp.wait_ge(s["v_out"], NT * b + NT + NT)
                    for q in range(QUADS):
                        sp.dma_start(at(d["v0"], b)[q].rearrange("(t p) f -> p t f", p=P),
                                     vp[:, :, 4 * q:4 * q + 4, :].rearrange("p t h f -> p t (h f)")).then_inc(s["v_saved"], 16)
                    sp.wait_ge(s["k_split"], b + 1 + 1)
                    sp.dma_start(at(d["kp"], b).rearrange("j (k p) s -> p (j k) s", p=P),
                                 kp[:, :, :, :].rearrange("p j k s -> p (j k) s")).then_inc(s["parts_saved"], 16)
                    sp.wait_ge(s["q_split"], b + 1 + 1)
                    sp.dma_start(at(d["qp"], b).rearrange("j (k p) s -> p (j k) s", p=P),
                                 qp[:, :, :, :].rearrange("p j k s -> p (j k) s")).then_inc(s["parts_saved"], 16)

                sp.sem_inc(s["cT_saved"], 16)
                sp.sem_inc(s["v_saved"], 16 * QUADS)
                sp.sem_inc(s["parts_saved"], 32)
                load_c(0)
                load_x(0)
                for name in "vkq":
                    sp.dma_start(w[name][:, :, :], io[f"L0_xattn_w_{name}"].rearrange("(k p) f -> p k f", p=P)).then_inc(s["w_in"], 16)
                with nc.allow_non_contiguous_dma(reason="256 biases as columns"):
                    for name in "qk":
                        sp.dma_start(bcol[name][:, :], io[f"L0_xattn_b_{name}"].rearrange("(k p) -> p k", p=P)).then_inc(s["bias"], 16)
                sp.dma_start(bv[:, :], io["L0_xattn_b_v"].rearrange("(a f) -> a f", a=1).to_broadcast([P, D])).then_inc(s["bias"], 16)
                sp.wait_ge(s["normed"], 1)
                load_x(1)
                sp.dma_start(mask[:, :, :], io["mask_1x1xSxS2_fk0"].rearrange("x y (t p) s -> p (x y t) s", p=P)).then_inc(s["mask_in"], 16)
                for b in range(B):
                    sp.dma_start(pad[:, b, :], io["mask_Bx1x1xS2_ff0"][b, 0].to_broadcast([P, S])).then_inc(s["mask_in"], 16)
                with sp.Fori(0, B - 2) as b:
                    batch(b)
                batch(B - 2, next_x=False)
                batch(B - 1, next_x=False, next_c=False)
                sp.wait_ge(s["cT_saved"], 16 * B + 16)
                sp.wait_ge(s["parts_saved"], 16 * 2 * B + 32)
                sp.wait_ge(s["v_saved"], 16 * QUADS * B + 16 * QUADS)

            @block.gpsimd
            def _(pool):
                pool.wait_ge(s["mask_in"], 16 * (B + 1))
                for t in range(NT):
                    nc.gpsimd.tensor_tensor(maskb[:, t, :], mask[:, t, :], pad[:, 0, :], ALU.add).then_inc(s["mask_made"], 1)
                pool.wait_ge(s["mask_made"], NT)

            @block.tensor
            def _(pe):
                with pe.Fori(0, B) as b:
                    pe.wait_ge(s["c_in"], b * 16 + 16)
                    for k in range(KD):
                        for t in range(NT):
                            last = nc.tensor.transpose(tc[k][:, t * P:(t + 1) * P], c4[:, t, k * P:(k + 1) * P], c["ident"][:, :])
                    last.then_inc(s["turned_c"], 1)
                    pe.wait_ge(s["normed"], b + 1)
                    pe.wait_ge(s["v_out"], NT * b + NT)
                    for k in range(KD):
                        for t in range(NT):
                            last = nc.tensor.transpose(tx[k][:, t * P:(t + 1) * P], xn4[:, t, k * P:(k + 1) * P], c["ident"][:, :])
                    last.then_inc(s["turned_x"], 1)
                    pe.wait_ge(s["w_in"], 48)
                    pe.wait_ge(s["cT_out"], KD * b + KD)
                    for m in range(KD):
                        for k in range(KD):
                            last = nc.tensor.matmul(pk[m][:, :], w["k"][:, k, m * P:(m + 1) * P], cT[:, k, :],
                                                    start=k == 0, stop=k == KD - 1)
                        last.then_inc(s["mm"], 1)
                    pe.wait_ge(s["xT_out"], KD * b + KD)
                    for t in range(NT):
                        for k in range(KD):
                            last = nc.tensor.matmul(tx[t // 2][:, (t % 2) * D:(t % 2 + 1) * D], cT[:, k, t * P:(t + 1) * P],
                                                    w["v"][:, k, :], start=k == 0, stop=k == KD - 1)
                        if t % 2:
                            last.then_inc(s["v_mm"], 1)
                    for m in range(KD):
                        for k in range(KD):
                            last = nc.tensor.matmul(pq[m][:, :], w["q"][:, k, m * P:(m + 1) * P], xT[:, k, :],
                                                    start=k == 0, stop=k == KD - 1)
                        last.then_inc(s["mm"], 1)

            @block.scalar
            def _(act):
                act.wait_ge(s["bias"], 48 + 1)
                with act.Fori(0, B) as b:
                    act.wait_ge(s["turned_c"], b + 1)
                    act.wait_ge(s["cT_saved"], b * 16 + 16)
                    for k in range(KD):
                        nc.scalar.copy(cT[:, k, :], tc[k][:, :]).then_inc(s["cT_out"], 1)
                    act.wait_ge(s["turned_x"], b + 1)
                    for k in range(KD):
                        nc.scalar.copy(xT[:, k, :], tx[k][:, :]).then_inc(s["xT_out"], 1)
                    for m in range(KD):
                        act.wait_ge(s["mm"], 2 * KD * b + m + 1)
                        act.wait_ge(s["k_split"], b + 1)
                        nc.scalar.activation(k1[:, m, :], pk[m][:, :], ACT.Identity, bias=bcol["k"][:, m:m + 1]).then_inc(s["out"], 1)
                        act.wait_ge(s["parts_saved"], b * 32 + 32)
                        nc.scalar.activation(kp[:, 0, m, :], pk[m][:, :], ACT.Identity, bias=bcol["k"][:, m:m + 1]).then_inc(s["out"], 1)
                    for m in range(KD):
                        act.wait_ge(s["mm"], 2 * KD * b + KD + m + 1)
                        act.wait_ge(s["q_split"], b + 1)
                        nc.scalar.activation(q1[:, m, :], pq[m][:, :], ACT.Identity, bias=bq4[:, m:m + 1],
                                             scale=DH0 ** -0.5).then_inc(s["out"], 1)
                        nc.scalar.activation(qp[:, 0, m, :], pq[m][:, :], ACT.Identity, bias=bq4[:, m:m + 1],
                                             scale=DH0 ** -0.5).then_inc(s["out"], 1)

            @block.vector
            def _(dve):
                nc.vector.memset(vp[:, :, :, :].rearrange("p t h f -> p (t h f)"), 0.0)
                nc.vector.memset(c["wo0"][:, :, :].rearrange("p q f -> p (q f)"), 0.0)

                def split(src, parts, rest):
                    nc.vector.tensor_tensor(rest[:, :, :], src[:, :, :], parts[:, 0], ALU.subtract)
                    nc.vector.drain()
                    nc.vector.tensor_copy(parts[:, 1], rest[:, :, :])
                    nc.vector.drain()
                    return nc.vector.tensor_tensor(parts[:, 2], rest[:, :, :], parts[:, 1], ALU.subtract)

                def norm(b):
                    dve.wait_ge(s["x_in"], b * 16 + 16)
                    if not (isinstance(b, int) and b == 0):
                        dve.wait_ge(s["turned_x"], b)
                    nc.vector.memset(nb[2][:, :], 0.0)
                    layer_norm(nc, x4, *nb, xn4, 1e-5).then_inc(s["normed"], 1)

                def batch(b, has_next=True):
                    if has_next:
                        norm(b + 1)
                    dve.wait_ge(s["v_saved"], b * (16 * QUADS) + 16 * QUADS)
                    for t in range(NT):
                        if t % 2 == 0:
                            dve.wait_ge(s["v_mm"], NT // 2 * b + t // 2 + 1)
                        nc.vector.tensor_tensor(vp[:, t, :, 0:DH0],
                                                tx[t // 2][:, (t % 2) * D:(t % 2 + 1) * D].rearrange("p (h f) -> p h f", h=HEADS),
                                                bv[:, :].rearrange("p (h f) -> p h f", h=HEADS), ALU.add).then_inc(s["v_out"], 1)
                    dve.wait_ge(s["out"], 4 * KD * b + 2 * KD)
                    dve.wait_ge(s["parts_saved"], b * 32 + 32)
                    split(k1, kp, rest[0]).then_inc(s["k_split"], 1)
                    dve.wait_ge(s["out"], 4 * KD * b + 4 * KD)
                    split(q1, qp, rest[1]).then_inc(s["q_split"], 1)

                dve.sem_inc(s["v_out"], NT)
                dve.sem_inc(s["k_split"], 1)
                dve.sem_inc(s["q_split"], 1)
                norm(0)
                dve.wait_ge(s["bias"], 48)
                nc.vector.tensor_scalar(bq4[:, :], bcol["q"][:, :], DH0 ** -0.5, None, ALU.mult).then_inc(s["bias"], 1)
                with dve.Fori(0, B - 1) as b:
                    batch(b)
                batch(B - 1, has_next=False)


NU = 4 * NT
BODY = 2 * NU
BODIES = ITEMS // 2
DEEP = 4


def lagged(body, step, lag, first, last):
    w = step - lag
    if w >= 0:
        return None if last else (body, w)
    return None if first else (body - 1, w + BODY)


def masked_attention_stage(nc, c, io, d):
    LAG_T = 4
    PROBS = 8
    LAG_V = 6
    STEP_V = 3
    LAG_O = LAG_V + STEP_V * (NT - 1) + 1
    LAG_N = LAG_O + 2
    with ExitStack() as ctx:
        st = Store(nc, ctx, "a0")
        s = st.sems("in0 in1 v_in0 v_in1 next_in mask_made scores lifted exped turned evac_d evac_a pv o_copied spread recip_mm normed saved0 saved1")
        qs = [st.sb(f"qs{i}", [STACK, 4, S], BF16) for i in range(2)]
        ks = [st.sb(f"ks{i}", [STACK, 4, S], BF16) for i in range(2)]
        v = [st.sb(f"v{i}", [P, NT, 4 * PAD0]) for i in range(2)]
        mask, maskb, pad = c["mask"], c["maskb"], c["pad"]
        low = [st.sb(f"low{i}", [P, S]) for i in range(DEEP)]
        prob = [st.sb(f"prob{i}", [P, S]) for i in range(PROBS)]
        nmax, total = st.sb("nmax", [P, BODY]), st.sb("total", [P, BODY])
        recip, spread = st.sb("recip", [P, NU]), st.sb("spread", [P, NT, 4, PAD0])
        pT = [st.sb(f"pT{i}", [P, NT, S]) for i in range(8)]
        o_sb = st.sb("o_sb", [P, S])
        o_n = [st.sb(f"o_n{i}", [P, S]) for i in range(2)]
        cells = st.sb("cells", [P, BODY])
        ps_s = [st.ps(f"s{i}") for i in range(2)]
        ps_t = [st.ps(f"t{i}") for i in range(2)]
        ps_o = [st.ps(f"o{i}") for i in range(2)]
        ps_r = st.ps("r")
        s_in, s_v, s_saved = (s["in0"], s["in1"]), (s["v_in0"], s["v_in1"]), (s["saved0"], s["saved1"])
        LOADS = 2 * len(Q_PARTS)

        with nc.Block() as block:
            @block.sync
            def _(sp):
                def load(b, quad):
                    par = quad % 2
                    if not (isinstance(b, int) and quad < 2):
                        sp.wait_ge(s["scores"], (b * QUADS + quad - 1) * NU)
                    for t, (a, b_) in enumerate(zip(Q_PARTS, K_PARTS)):
                        for dst, src in ((qs[par], at(d["qp"], b)[a]), (ks[par], at(d["kp"], b)[b_])):
                            sp.dma_start(dst[t * DH0:(t + 1) * DH0, :, :],
                                         src[quad * 64:quad * 64 + 64, :].rearrange("(h f) s -> f h s", h=4)).then_inc(s_in[par], 16)
                    if not (isinstance(b, int) and quad < 2):
                        sp.wait_ge(s["pv"], b * QUADS + quad + 1)
                    sp.dma_start(v[par][:, :, :], at(d["v0"], b)[quad].rearrange("(t p) f -> p t f", p=P)).then_inc(s_v[par], 16)

                def save(n, par):
                    sp.wait_ge(s["normed"], n + 2)
                    sp.dma_start(at(d["o0"], n), o_n[par][:, :]).then_inc(s_saved[par], 16)

                sp.sem_inc(s["saved0"], 16)
                sp.sem_inc(s["saved1"], 16)
                load(0, 0)
                for h in range(4):
                    sp.dma_start(c["wo0"][h * PAD0:h * PAD0 + DH0, :, :],
                                 io["L0_xattn_w_out"].rearrange("(q h f) d -> h f q d", q=QUADS, h=4)[h]).then_inc(s["next_in"], 16)
                sp.dma_start(c["wr0"][:, :, :], io["L0_ffn_router_w"].rearrange("(k p) e -> p k e", p=P)).then_inc(s["next_in"], 16)
                sp.dma_start(c["bo0"][:, :], io["L0_xattn_b_out"].rearrange("(a f) -> a f", a=1).to_broadcast([P, D])).then_inc(s["next_in"], 16)
                load(0, 1)
                for par in range(2):
                    load(0, 2 + par)
                    save(par, par)
                with sp.Fori(1, B) as b:
                    for quad in range(QUADS):
                        load(b, quad)
                        save(b * QUADS + quad - 2, quad % 2)
                save(ITEMS - 2, 0)
                save(ITEMS - 1, 1)
                sp.wait_ge(s["next_in"], 16 * 6)
                for par in range(2):
                    sp.wait_ge(s_saved[par], 16 * (ITEMS // 2) + 16)

            @block.gpsimd
            def _(pool):
                pool.sem_inc(s["mask_made"], NT)
                for b in range(1, B):
                    for t in range(NT):
                        pool.wait_ge(s["lifted"], 2 * b * BODY - NT + t + 1 + 2)
                        nc.gpsimd.tensor_tensor(maskb[:, t, :], mask[:, t, :], pad[:, b, :], ALU.add).then_inc(s["mask_made"], 1)

            @block.tensor
            def _(pe):
                pe.sem_inc(s["turned"], PROBS)
                pe.sem_inc(s["pv"], 2)

                def run(body, step, first=False, last=False):
                    if lagged(body, step, 0, first, last):
                        par, h, t = step // NU, step % NU // NT, step % NT
                        if step % NU == 0:
                            pe.wait_ge(s_in[par], body * (LOADS * 16) + LOADS * 16)
                        pe.wait_ge(s["lifted"], body * BODY + step + 1)
                        nc.tensor.matmul(ps_s[step % 2][:, :], qs[par][:, h, t * P:(t + 1) * P], ks[par][:, h, :],
                                         start=True, stop=True).then_inc(s["scores"], 1)
                    unit = lagged(body, step, LAG_T, first, last)
                    if unit:
                        ub, w = unit
                        pe.wait_ge(s["exped"], ub * BODY + w + 1 + DEEP)
                        pe.wait_ge((s["evac_d"], s["evac_a"])[w % 2], ub * NU + w // 2 + 1)
                        for k in range(NT):
                            op = nc.tensor.transpose(ps_t[w % 2][:, k * P:(k + 1) * P],
                                                     prob[w % PROBS][:, k * P:(k + 1) * P], c["ident"][:, :])
                        op.then_inc(s["turned"], 1)
                    for k in range(NT):
                        unit = lagged(body, step, LAG_V + STEP_V * k, first, last)
                        if unit and unit[1] % NU == NU - 1:
                            ub, w = unit
                            par = w // NU
                            if k == 0:
                                pe.wait_ge(s_v[par], ub * 16 + 16)
                                pe.wait_ge(s["evac_d"], ub * NU + w // 2 + 1 + 1)
                                pe.wait_ge(s["evac_a"], ub * NU + w // 2 + 1 + 1)
                                pe.wait_ge(s["o_copied"], ub * 2 + par + 1)
                            for h in range(4):
                                op = nc.tensor.matmul(ps_o[par][h * PAD0:(h + 1) * PAD0, :],
                                                      v[par][:, k, h * PAD0:(h + 1) * PAD0], pT[par * 4 + h][:, k, :],
                                                      start=k == 0, stop=k == NT - 1)
                            if k == NT - 1:
                                op.then_inc(s["pv"], 1)
                    unit = lagged(body, step, LAG_V, first, last)
                    if unit and unit[1] % NU == NU - 1:
                        ub, w = unit
                        par = w // NU
                        pe.wait_ge(s["spread"], ub * 2 + par + 1)
                        pe.wait_ge(s["normed"], ub * 2 + par + 1)
                        for t in range(NT):
                            op = nc.tensor.transpose(ps_r[:, t * P:(t + 1) * P],
                                                     spread[:, t, :, :].rearrange("p h f -> p (h f)"), c["ident"][:, :])
                        op.then_inc(s["recip_mm"], 1)

                for step in range(BODY):
                    run(0, step, first=True)
                with pe.Fori(1, BODIES) as body:
                    for step in range(BODY):
                        run(body, step)
                for step in range(LAG_O):
                    run(BODIES, step, last=True)

            @block.vector
            def _(dve):
                dve.sem_inc(s["lifted"], 2)
                dve.sem_inc(s["evac_d"], 1)
                dve.sem_inc(s["normed"], 1)

                def run(b, body, step, first=False, last=False):
                    if lagged(body, step, 0, first, last):
                        dve.wait_ge(s["scores"], body * BODY + step + 1)
                        dve.wait_ge(s["exped"], body * BODY + step + 1)
                        if step < NT:
                            dve.wait_ge(s["mask_made"], b * NT + step + 1)
                        nc.vector.memset(cells[:, step:step + 1], 0.0)
                        nc.vector.tensor_tensor_reduce(out=low[step % DEEP][:, :], in0=ps_s[step % 2][:, :], in1=maskb[:, step % NT, :],
                                                       scale=-1.0, scalar=3.0e38, op0=ALU.add, op1=ALU.min,
                                                       accum_out=nmax[:, step:step + 1]).then_inc(s["lifted"], 1)
                    unit = lagged(body, step, LAG_T, first, last)
                    if unit and unit[1] % 2 == 0:
                        ub, w = unit
                        dve.wait_ge(s["turned"], ub * BODY + w + 1 + PROBS)
                        if w % NU == 0:
                            dve.wait_ge(s["pv"], ub * 2 + w // NU + 1)
                        nc.vector.tensor_copy(pT[w // NT][:, :, w % NT * P:(w % NT + 1) * P],
                                              ps_t[0][:, :].rearrange("p (k s) -> p k s", k=NT)).then_inc(s["evac_d"], 1)
                    if unit and unit[1] % NU == NU - 1:
                        ub, w = unit
                        par = w // NU
                        dve.wait_ge(s["exped"], ub * BODY + w + 1 + DEEP)
                        if not (first and par == 0):
                            dve.wait_ge(s["recip_mm"], ub * 2 + par)
                        nc.vector.reciprocal(recip[:, :], total[:, par * NU:(par + 1) * NU])
                        nc.vector.drain()
                        nc.vector.tensor_copy(spread[:, :, :, :],
                                              recip[:, :].rearrange("p (h t o) -> p t h o", h=4, o=1)
                                              .to_broadcast([P, NT, 4, PAD0])).then_inc(s["spread"], 1)
                    unit = lagged(body, step, LAG_N, first, last)
                    if unit and unit[1] % NU == NU - 1:
                        ub, w = unit
                        par = w // NU
                        dve.wait_ge(s["recip_mm"], ub * 2 + par + 1)
                        dve.wait_ge(s["o_copied"], ub * 2 + par + 1 + 2)
                        dve.wait_ge(s_saved[par], ub * 16 + 16)
                        nc.vector.tensor_tensor(o_n[par][:, :], o_sb[:, :], ps_r[:, :], ALU.mult).then_inc(s["normed"], 1)

                for step in range(BODY):
                    run(0, 0, step, first=True)
                for step in range(BODY):
                    run(0, 1, step)
                with dve.Fori(1, B) as b:
                    with dve.Fori(0, 2) as half:
                        for step in range(BODY):
                            run(b, b * 2 + half, step)
                for step in range(LAG_N):
                    run(B, BODIES, step, last=True)

            @block.scalar
            def _(act):
                act.sem_inc(s["exped"], DEEP)
                act.sem_inc(s["evac_a"], 1)
                act.sem_inc(s["o_copied"], 2)

                def run(body, step, first=False, last=False):
                    unit = lagged(body, step, LAG_T, first, last)
                    if unit and unit[1] % 2 == 1:
                        ub, w = unit
                        act.wait_ge(s["turned"], ub * BODY + w + 1 + PROBS)
                        if w % NU == 1:
                            act.wait_ge(s["pv"], ub * 2 + w // NU + 1)
                        nc.scalar.copy(pT[w // NT][:, :, w % NT * P:(w % NT + 1) * P],
                                       ps_t[1][:, :].rearrange("p (k s) -> p k s", k=NT)).then_inc(s["evac_a"], 1)
                    if lagged(body, step, 0, first, last):
                        act.wait_ge(s["lifted"], body * BODY + step + 1 + 2)
                        act.wait_ge(s["turned"], body * BODY + step + 1)
                        nc.scalar.activation(prob[step % PROBS][:, :], low[step % DEEP][:, :], ACT.Exp, bias=nmax[:, step:step + 1],
                                             scale=-1.0, accum_out=total[:, step:step + 1]).then_inc(s["exped"], 1)
                    unit = lagged(body, step, LAG_O, first, last)
                    if unit and unit[1] % NU == NU - 1:
                        ub, w = unit
                        par = w // NU
                        act.wait_ge(s["pv"], ub * 2 + par + 1 + 2)
                        act.wait_ge(s["normed"], ub * 2 + par + 1)
                        nc.scalar.copy(o_sb[:, :], ps_o[par][:, :]).then_inc(s["o_copied"], 1)

                for step in range(BODY):
                    run(0, step, first=True)
                with act.Fori(1, BODIES) as body:
                    for step in range(BODY):
                        run(body, step)
                for step in range(LAG_O):
                    run(BODIES, step, last=True)


class Router:

    def __init__(self, nc, st, c, experts, top, cap, drop):
        self.nc, self.c, self.E, self.top, self.cap, self.drop = nc, c, experts, top, cap, drop
        self.R = NT * top
        self.nmax, self.sums, self.rsum = st.sb("nmax", [P, NT]), st.sb("sums", [P, NT]), st.sb("rsum", [P, NT])
        self.e = st.sb("e", [P, NT, experts])
        self.best, self.best_at = st.sb("best", [P, NT, 8]), st.sb("best_at", [P, NT, 8], U32)
        self.expert = st.sb("expert", [P, self.R])
        self.hot, self.hot_pos = st.sb("hot", [P, self.R, experts]), st.sb("hot_pos", [P, self.R, experts])
        self.chosen, self.before = st.sb("chosen", [P, NT, experts], BF16), st.sb("before", [P, experts], BF16)
        self.pos, self.fits, self.skip = st.sb("pos", [P, self.R]), st.sb("fits", [P, self.R]), st.sb("skip", [P, self.R])
        self.slot, self.slot_skip = st.sb("slot", [P, self.R]), st.sb("slot_skip", [P, self.R])
        self.slot_read, self.slot_write = st.sb("slot_read", [P, self.R], U32), st.sb("slot_write", [P, self.R], U32)
        self.weight = st.sb("weight", [P, self.R])
        self.tok_f, self.tok = st.sb("tok_f", [P, NT]), st.sb("tok", [P, NT], U32)
        self.tok_write = st.sb("tok_write", [P, NT], U32)

    def start(self):
        v = self.nc.vector
        v.memset(self.before[:, :], 0.0)
        v.tensor_copy(self.tok_f[:, :], self.c["token_no"][:, :])

    def tail(self, ap):
        return ap.rearrange("p (r o) -> p r o", o=1)

    def pick(self):
        v = self.nc.vector
        v.reciprocal(self.rsum[:, :], self.sums[:, :])
        for t in range(NT):
            v.max(self.best[:, t, :], self.e[:, t, :])
        v.drain()
        for t in range(NT):
            v.max_index(self.best_at[:, t, :], self.best[:, t, :], self.e[:, t, :])
        v.drain()
        v.tensor_copy(self.expert[:, :].rearrange("p (t j) -> p t j", t=NT), self.best_at[:, :, 0:self.top])
        v.drain()
        full = [P, self.R, self.E]
        v.tensor_tensor(self.hot[:, :, :], self.c["expert_no"][:, 0:self.E].rearrange("p (o e) -> p o e", o=1).to_broadcast(full),
                        self.tail(self.expert[:, :]).to_broadcast(full), ALU.is_equal)
        v.drain()
        if self.top == 1:
            return v.tensor_copy(self.chosen[:, :, :], self.hot[:, :, :])
        with self.nc.allow_low_precision(reason="zeros and ones"):
            return v.tensor_reduce(self.chosen[:, :, :], self.hot[:, :, :].rearrange("p (t j) e -> p t e j", t=NT), AX, ALU.add)

    def place(self, ps_pos):
        v = self.nc.vector
        earlier = ps_pos[:, 0:NT * self.E].rearrange("p (t e) -> p t e", t=NT)
        for t in range(NT):
            rows = slice(t * self.top, (t + 1) * self.top)
            v.tensor_tensor(self.hot_pos[:, rows, :], self.hot[:, rows, :],
                            earlier[:, t:t + 1, :].to_broadcast([P, self.top, self.E]), ALU.mult)
            v.drain()
            v.tensor_tensor(self.before[:, :], self.before[:, :], self.chosen[:, t, :], ALU.add)
        v.drain()
        v.tensor_reduce(self.pos[:, :], self.hot_pos[:, :, :], AX, ALU.add)
        v.drain()
        v.tensor_scalar(self.fits[:, :], self.pos[:, :], float(self.cap), None, ALU.is_lt)
        v.tensor_scalar(self.pos[:, :], self.pos[:, :], float(self.cap - 1), None, ALU.min)
        v.drain()
        v.tensor_scalar(self.skip[:, :], self.fits[:, :], -SKIP, SKIP, ALU.mult, ALU.add)
        v.tensor_scalar(self.slot[:, :], self.expert[:, :], float(self.cap), None, ALU.mult)
        v.tensor_tensor(self.weight[:, :].rearrange("p (t j) -> p t j", t=NT), self.best[:, :, 0:self.top],
                        self.tail(self.rsum[:, :]).to_broadcast([P, NT, self.top]), ALU.mult)
        v.drain()
        v.tensor_tensor(self.slot[:, :], self.slot[:, :], self.pos[:, :], ALU.add)
        if self.drop:
            v.tensor_tensor(self.weight[:, :], self.weight[:, :], self.fits[:, :], ALU.mult)
        v.tensor_copy(self.tok[:, :], self.tok_f[:, :])
        v.drain()
        v.tensor_scalar(self.tok_f[:, :], self.tok_f[:, :], float(S), None, ALU.add)
        return v.tensor_copy(self.slot_read[:, :], self.slot[:, :])

    def exponentials(self, logits):
        for t in range(NT):
            last = self.nc.scalar.activation(self.e[:, t, :], logits[:, t, :], ACT.Exp, bias=self.nmax[:, t:t + 1],
                                             accum_out=self.sums[:, t:t + 1])
        return last

    def count_earlier(self, ps_pos):
        mm = self.nc.tensor.matmul
        for t in range(NT):
            o = ps_pos[:, t * self.E:(t + 1) * self.E]
            mm(o, self.c["ones16"][:, :], self.before[:, :], start=True, stop=False)
            for u in range(t):
                mm(o, self.c["ones16"][:, :], self.chosen[:, u, :], start=False, stop=False)
            last = mm(o, self.c["before"][:, :], self.chosen[:, t, :], start=False, stop=True)
        return last

    def scatter(self, b, table, done, copied):
        pool = self.nc.gpsimd
        pool.tensor_tensor(self.slot_skip[:, :], self.slot[:, :], self.skip[:, :], ALU.add)
        pool.tensor_copy(self.tok_write[:, :], self.tok[:, :]).then_inc(copied, 1)
        pool.drain()
        pool.tensor_copy(self.slot_write[:, :], self.slot_skip[:, :])
        pool.drain()
        for r in range(self.R):
            t = r // self.top
            pool.indirect_dma_start(out=table, out_offset=bass.IndirectOffsetOnAxis(ap=self.slot_write[:, r:r + 1], axis=0),
                                    in_=self.tok_write[:, t:t + 1], in_offset=None, bounds_check=self.E * self.cap - 1,
                                    oob_is_err=False).then_inc(done, 16)
        pool.wait_ge(done, b * (16 * self.R) + 16 * self.R)


def route0_stage(nc, c, io, d):
    with ExitStack() as ctx:
        st = Store(nc, ctx, "r0")
        s = st.sems("o_in x_in product summed normed turned xT_out logits maxed exped picked counted placed "
                    "scattered slots_free x_saved xn_saved slots_saved table_zero")
        wo, wr, bo = c["wo0"], c["wr0"], c["bo0"]
        o4, x4 = st.sb("o4", [P, QUADS, S]), st.sb("x4", [P, NT, D])
        x1, xn = st.sb("x1", [P, NT, D]), st.sb("xn", [P, NT, D])
        xT = st.sb("xT", [P, KD, S])
        nb = norm_buffers(st)
        r = Router(nc, st, c, E0, TOP0, CAP0, drop=False)
        ps_y = [st.ps(f"y{i}") for i in range(2)]
        ps_x = [st.ps(f"x{i}") for i in range(KD)]
        ps_l, ps_p = st.ps("l"), st.ps("p")
        logits = ps_l[:, 0:NT * E0].rearrange("p (t e) -> p t e", t=NT)

        with nc.Block() as block:
            @block.sync
            def _(sp):
                def load(b):
                    sp.dma_start(o4[:, :, :], at(d["o0"].rearrange("(b q) p s -> b q p s", b=B), b).rearrange("q p s -> p q s")).then_inc(s["o_in"], 16)
                    sp.dma_start(x4[:, :, :], at(io["x"], b).rearrange("(t p) f -> p t f", p=P)).then_inc(s["x_in"], 16)

                def save(b, load_ahead=True):
                    sp.wait_ge(s["summed"], b + 1 + 1)
                    if load_ahead:
                        load(b + 1)
                    sp.dma_start(at(d["x1"], b).rearrange("(t p) f -> p t f", p=P), x1[:, :, :]).then_inc(s["x_saved"], 16)

                def save_norm(b):
                    sp.wait_ge(s["normed"], b + 1)
                    sp.dma_start(at(d["xn1"].rearrange("(b s) f -> b s f", b=B), b).rearrange("(t p) f -> p t f", p=P), xn[:, :, :]).then_inc(s["xn_saved"], 16)

                def save_choice(b):
                    sp.wait_ge(s["placed"], b + 1)
                    sp.dma_start(at(d["slots0"], b), r.slot_read[:, :]).then_inc(s["slots_saved"], 16)
                    sp.dma_start(at(d["weights0"], b), r.weight[:, :]).then_inc(s["slots_saved"], 16)

                sp.sem_inc(s["slots_saved"], 32)
                load(0)
                sp.dma_start(d["table0"].rearrange("(p k) o -> p (k o)", p=P), c["zeros"][:, :].bitcast(U32)).then_inc(s["table_zero"], 16)
                save(0)
                save_norm(0)
                with sp.Fori(0, B - 2) as b:
                    save(b + 1)
                    save_norm(b + 1)
                    save_choice(b)
                save(B - 1, load_ahead=False)
                save_norm(B - 1)
                save_choice(B - 2)
                save_choice(B - 1)
                sp.wait_ge(s["x_saved"], 16 * B)
                sp.wait_ge(s["xn_saved"], 16 * B)
                sp.wait_ge(s["slots_saved"], 32 * B + 32)

            @block.gpsimd
            def _(pool):
                pool.sem_inc(s["slots_free"], 1)
                pool.wait_ge(s["table_zero"], 16)
                with pool.Fori(0, B) as b:
                    pool.wait_ge(s["placed"], b + 1)
                    r.scatter(b, d["table0"], s["scattered"], s["slots_free"])

            @block.tensor
            def _(pe):
                def product(b):
                    pe.wait_ge(s["o_in"], b * 16 + 16)
                    pe.wait_ge(s["summed"], b + 1)
                    for t in range(NT):
                        for q in range(QUADS):
                            last = nc.tensor.matmul(ps_y[t // 2][:, t % 2 * D:(t % 2 + 1) * D], o4[:, q, t * P:(t + 1) * P],
                                                    wo[:, q, :], start=q == 0, stop=q == QUADS - 1)
                        if t % 2:
                            last.then_inc(s["product"], 1)

                def router(b):
                    pe.wait_ge(s["normed"], b + 1)
                    for k in range(KD):
                        for t in range(NT):
                            last = nc.tensor.transpose(ps_x[k][:, t * P:(t + 1) * P], xn[:, t, k * P:(k + 1) * P], c["ident"][:, :])
                    last.then_inc(s["turned"], 1)
                    pe.wait_ge(s["xT_out"], KD * b + KD)
                    pe.wait_ge(s["exped"], b + 1)
                    for t in range(NT):
                        for k in range(KD):
                            last = nc.tensor.matmul(ps_l[:, t * E0:(t + 1) * E0], xT[:, k, t * P:(t + 1) * P], wr[:, k, :],
                                                    start=k == 0, stop=k == KD - 1)
                    last.then_inc(s["logits"], 1)

                def count(b):
                    pe.wait_ge(s["picked"], b + 1)
                    r.count_earlier(ps_p).then_inc(s["counted"], 1)

                product(0)
                product(1)
                router(0)
                with pe.Fori(0, B - 2) as b:
                    router(b + 1)
                    count(b)
                    product(b + 2)
                router(B - 1)
                count(B - 2)
                count(B - 1)

            @block.scalar
            def _(act):
                act.sem_inc(s["exped"], 1)
                with act.Fori(0, B) as b:
                    act.wait_ge(s["turned"], b + 1)
                    for k in range(KD):
                        nc.scalar.copy(xT[:, k, :], ps_x[k][:, :]).then_inc(s["xT_out"], 1)
                    act.wait_ge(s["maxed"], b + 1)
                    r.exponentials(logits).then_inc(s["exped"], 1)

            @block.vector
            def _(dve):
                def norm(b):
                    dve.wait_ge(s["x_in"], b * 16 + 16)
                    if not (isinstance(b, int) and b == 0):
                        dve.wait_ge(s["x_saved"], 16 * b)
                    for t in range(NT):
                        nc.vector.tensor_tensor(x1[:, t, :], x4[:, t, :], bo[:, :], ALU.add)
                    nc.vector.drain()
                    for half in range(2):
                        dve.wait_ge(s["product"], 2 * b + half + 1)
                        last = nc.vector.tensor_tensor(x1[:, 2 * half:2 * half + 2, :], x1[:, 2 * half:2 * half + 2, :],
                                                       ps_y[half][:, :].rearrange("p (t f) -> p t f", t=2), ALU.add)
                    last.then_inc(s["summed"], 1)
                    nc.vector.drain()
                    if not (isinstance(b, int) and b == 0):
                        dve.wait_ge(s["xn_saved"], 16 * b)
                        dve.wait_ge(s["turned"], b)
                    nc.vector.memset(r.pos[:, :], 0.0)
                    layer_norm(nc, x1, *nb, xn, 1e-5).then_inc(s["normed"], 1)

                def maximum(b):
                    dve.wait_ge(s["logits"], b + 1)
                    nc.vector.tensor_reduce(r.nmax[:, :], logits, AX, ALU.max, negate=True).then_inc(s["maxed"], 1)

                def choose(b):
                    dve.wait_ge(s["exped"], b + 1 + 1)
                    r.pick().then_inc(s["picked"], 1)
                    dve.wait_ge(s["slots_saved"], b * 32 + 32)
                    dve.wait_ge(s["slots_free"], b + 1)
                    dve.wait_ge(s["counted"], b + 1)
                    r.place(ps_p).then_inc(s["placed"], 1)

                dve.sem_inc(s["summed"], 1)
                r.start()
                norm(0)
                maximum(0)
                with dve.Fori(0, B - 1) as b:
                    norm(b + 1)
                    choose(b)
                    maximum(b + 1)
                choose(B - 1)


def experts0_stage(nc, c, io, d):
    HALVES = CAP0 // P
    BODIES = E0 // DEEP
    with ExitStack() as ctx:
        st = Store(nc, ctx, "e0")
        s = st.sems("next_in table_in table_f table_T idx_made idx_set turned xT_out h silu gated y y_out " +
                    " ".join(f"w{i} rows{i} saved{i}" for i in range(DEEP)))
        table, table_f = st.sb("table", [P, P], U32), st.sb("table_f", [P, P])
        idx_all = st.sb("idx_all", [P, P], U32)
        idx = [st.sb(f"idx{i}", [P, HALVES], U32) for i in range(DEEP)]
        carry = st.sb("carry", [P, E0])
        rows = [st.sb(f"rows{i}", [P, HALVES, D]) for i in range(DEEP)]
        w1 = [st.sb(f"w1{i}", [P, KD, 2 * I0]) for i in range(DEEP)]
        w2 = [st.sb(f"w2{i}", [P, D]) for i in range(DEEP)]
        y = [st.sb(f"y{i}", [P, HALVES, D]) for i in range(DEEP)]
        xT = [st.sb(f"xT{i}", [P, KD, CAP0]) for i in range(2)]
        sg, g = [st.sb(f"sg{i}", [P, CAP0]) for i in range(2)], [st.sb(f"g{i}", [P, CAP0]) for i in range(2)]
        ps_x, ps_h, ps_y = [[st.ps(f"{n}{i}") for i in range(2)] for n in "xhy"]
        s_w, s_rows, s_saved = ([s[f"{n}{i}"] for i in range(DEEP)] for n in ("w", "rows", "saved"))
        y_out = d["y0"].rearrange("(e h p) f -> e p h f", p=P, h=HALVES)

        with nc.Block() as block:
            @block.sync
            def _(sp):
                sp.dma_start(table[:, :], d["table0"].rearrange("(g p) o -> g (p o)", p=P)).then_inc(s["table_in"], 16)
                with sp.Fori(0, BODIES) as body:
                    for i in range(DEEP):
                        e = body * DEEP + i
                        sp.wait_ge(s["y"], e + 1)
                        sp.dma_start(w1[i][:, :, :], at(io["L0_ffn_w1"], e).rearrange("(k p) f -> p k f", p=P)).then_inc(s_w[i], 16)
                        sp.dma_start(w2[i][:, :], at(io["L0_ffn_w2"], e)).then_inc(s_w[i], 16)
                sp.dma_start(c["slots0"][:, :, :], d["slots0"].rearrange("b p r -> p b r")).then_inc(s["next_in"], 16)
                sp.dma_start(c["weights0"][:, :, :], d["weights0"].rearrange("b p r -> p b r")).then_inc(s["next_in"], 16)
                sp.wait_ge(s["next_in"], 32)

            @block.gpsimd
            def _(pool):
                with pool.Fori(0, BODIES) as body:
                    for i in range(DEEP):
                        e = body * DEEP + i
                        pool.wait_ge(s["idx_set"], e + 1)
                        nc.gpsimd.tensor_tensor(carry[:, bass.ds(e, 1)], c["ones"][:, 0:1], c["ones"][:, 0:1], ALU.mult)
                        for h in range(HALVES):
                            nc.gpsimd.indirect_dma_start(out=rows[i][:, h, :], out_offset=None, in_=d["xn1"],
                                                         in_offset=bass.IndirectOffsetOnAxis(ap=idx[i][:, h:h + 1], axis=0),
                                                         ).then_inc(s_rows[i], 16)

            @block.tensor
            def _(pe):
                pe.sem_inc(s["turned"], DEEP)
                pe.sem_inc(s["y"], DEEP)
                pe.wait_ge(s["table_f"], 1)
                nc.tensor.transpose(ps_x[0][:, 0:P], table_f[:, :], c["ident"][:, :]).then_inc(s["table_T"], 1)
                pe.wait_ge(s["idx_made"], 1)

                def turn(body, i):
                    e = body * DEEP + i
                    pe.wait_ge(s_rows[i], body * (16 * HALVES) + 16 * HALVES)
                    pe.wait_ge(s["xT_out"], e + 1)
                    for k in range(KD):
                        for h in range(HALVES):
                            last = nc.tensor.transpose(ps_x[i % 2][:, k * CAP0 + h * P:k * CAP0 + (h + 1) * P],
                                                       rows[i][:, h, k * P:(k + 1) * P], c["ident"][:, :])
                    last.then_inc(s["turned"], 1)

                def first(body, i):
                    e = body * DEEP + i
                    pe.wait_ge(s_w[i], body * 32 + 32)
                    pe.wait_ge(s["xT_out"], e + 1 + 2)
                    pe.wait_ge(s["gated"], e + 1)
                    for m in range(2):
                        for k in range(KD):
                            last = nc.tensor.matmul(ps_h[i % 2][:, m * CAP0:(m + 1) * CAP0], w1[i][:, k, m * I0:(m + 1) * I0],
                                                    xT[i % 2][:, k, :], start=k == 0, stop=k == KD - 1)
                    last.then_inc(s["h"], 1)

                def second(body, i):
                    e = body * DEEP + i
                    pe.wait_ge(s["gated"], e + 1 + 2)
                    pe.wait_ge(s["y_out"], e + 1)
                    for h in range(HALVES):
                        last = nc.tensor.matmul(ps_y[i % 2][:, h * D:(h + 1) * D], g[i % 2][:, h * P:(h + 1) * P], w2[i][:, :],
                                                start=True, stop=True)
                    last.then_inc(s["y"], 1)

                turn(0, 0)
                for i in range(DEEP):
                    first(0, i)
                    turn((0, 1)[i == DEEP - 1], (i + 1) % DEEP)
                    if i >= 1:
                        second(0, i - 1)
                with pe.Fori(1, BODIES - 1) as body:
                    for i in range(DEEP):
                        first(body, i)
                        turn(body + 1 if i == DEEP - 1 else body, (i + 1) % DEEP)
                        second(body - 1 if i == 0 else body, (i - 1) % DEEP)
                for i in range(DEEP):
                    first(BODIES - 1, i)
                    if i < DEEP - 1:
                        turn(BODIES - 1, i + 1)
                    second(BODIES - 2 if i == 0 else BODIES - 1, (i - 1) % DEEP)
                second(BODIES - 1, DEEP - 1)

            @block.scalar
            def _(act):
                act.sem_inc(s["y_out"], 2)
                for i in range(DEEP):
                    act.sem_inc(s_saved[i], 16)

                def silu(body, i):
                    act.wait_ge(s["h"], body * DEEP + i + 1)
                    act.wait_ge(s["gated"], body * DEEP + i + 1)
                    nc.scalar.activation(sg[i % 2][:, :], ps_h[i % 2][:, 0:CAP0], ACT.Silu).then_inc(s["silu"], 1)

                def leave(body, i):
                    e = body * DEEP + i
                    act.wait_ge(s["y"], e + 1 + DEEP)
                    act.wait_ge(s_saved[i], body * 16 + 16)
                    nc.scalar.copy(y[i][:, :, :], ps_y[i % 2][:, :].rearrange("p (h f) -> p h f", h=HALVES)).then_inc(s["y_out"], 1)
                    act.wait_ge(s["y_out"], e + 1 + 2)
                    act.dma_start(at(y_out, e), y[i][:, :, :]).then_inc(s_saved[i], 16)

                for i in range(DEEP):
                    silu(0, i)
                    if i >= 1:
                        leave(0, i - 1)
                with act.Fori(1, BODIES) as body:
                    for i in range(DEEP):
                        silu(body, i)
                        leave(body - 1 if i == 0 else body, (i - 1) % DEEP)
                leave(BODIES - 1, DEEP - 1)
                for i in range(DEEP):
                    act.wait_ge(s_saved[i], 16 * BODIES + 16)

            @block.vector
            def _(dve):
                dve.sem_inc(s["xT_out"], 2)
                dve.sem_inc(s["gated"], 2)
                dve.wait_ge(s["table_in"], 16)
                nc.vector.tensor_copy(table_f[:, :], table[:, :]).then_inc(s["table_f"], 1)
                dve.wait_ge(s["table_T"], 1)
                nc.vector.tensor_copy(idx_all[:, :], ps_x[0][:, 0:P]).then_inc(s["idx_made"], 1)
                nc.vector.drain()
                for i in range(DEEP):
                    nc.vector.tensor_copy(idx[i][:, :], idx_all[:, i * HALVES:(i + 1) * HALVES]).then_inc(s["idx_set"], 1)

                def xT_copy(body, i):
                    e = body * DEEP + i
                    dve.wait_ge(s["turned"], e + 1 + DEEP)
                    if not (isinstance(body, int) and e < 2):
                        dve.wait_ge(s["h"], e - 1)
                    nc.vector.tensor_copy(xT[i % 2][:, :, :], ps_x[i % 2][:, :].rearrange("p (k s) -> p k s", k=KD)).then_inc(s["xT_out"], 1)

                def idx_next(body, i):
                    e = body * DEEP + i
                    nc.vector.tensor_copy(idx[i][:, :], idx_all[:, bass.ds(e * HALVES + DEEP * HALVES, HALVES)]).then_inc(s["idx_set"], 1)

                def gate(body, i):
                    e = body * DEEP + i
                    dve.wait_ge(s["silu"], e + 1)
                    dve.wait_ge(s["y"], e + 1 + DEEP - 2)
                    nc.vector.tensor_tensor(g[i % 2][:, :], sg[i % 2][:, :], ps_h[i % 2][:, CAP0:2 * CAP0], ALU.mult).then_inc(s["gated"], 1)

                xT_copy(0, 0)
                idx_next(0, 0)
                for i in range(1, DEEP):
                    xT_copy(0, i)
                    idx_next(0, i)
                    gate(0, i - 1)
                with dve.Fori(1, BODIES - 1) as body:
                    for i in range(DEEP):
                        xT_copy(body, i)
                        idx_next(body, i)
                        gate(body - 1 if i == 0 else body, (i - 1) % DEEP)
                for i in range(DEEP):
                    xT_copy(BODIES - 1, i)
                    gate(BODIES - 2 if i == 0 else BODIES - 1, (i - 1) % DEEP)
                gate(BODIES - 1, DEEP - 1)


def combine0_stage(nc, c, io, d):
    R = NT * TOP0
    with ExitStack() as ctx:
        st = Store(nc, ctx, "c0")
        s = st.sems("x_in rows added normed turned xT_out x_saved xT_saved")
        slots, share = c["slots0"][:, 0, :], c["weights0"][:, 0, :]
        x4, rows = st.sb("x4", [P, NT, D]), st.sb("rows", [P, R, D])
        xn, xT = st.sb("xn", [P, NT, D]), st.sb("xT", [P, KD, S])
        nb = norm_buffers(st)
        ps_x = [st.ps(f"x{i}") for i in range(KD)]
        with nc.Block() as block:
            @block.sync
            def _(sp):
                sp.dma_start(x4[:, :, :], d["x1"][0].rearrange("(t p) f -> p t f", p=P)).then_inc(s["x_in"], 16)
                sp.wait_ge(s["added"], 1)
                sp.dma_start(d["x2"][0].rearrange("(t p) f -> p t f", p=P), x4[:, :, :]).then_inc(s["x_saved"], 16)
                sp.wait_ge(s["xT_out"], KD)
                sp.dma_start(d["xT2"][0].rearrange("(k p) s -> p k s", p=P), xT[:, :, :]).then_inc(s["xT_saved"], 16)
                sp.wait_ge(s["x_saved"], 16)
                sp.wait_ge(s["xT_saved"], 16)

            @block.gpsimd
            def _(pool):
                for r in range(R):
                    nc.gpsimd.indirect_dma_start(out=rows[:, r, :], out_offset=None, in_=d["y0"],
                                                 in_offset=bass.IndirectOffsetOnAxis(ap=slots[:, r:r + 1], axis=0),
                                                 ).then_inc(s["rows"], 16)

            @block.tensor
            def _(pe):
                pe.wait_ge(s["normed"], 1)
                for k in range(KD):
                    for t in range(NT):
                        last = nc.tensor.transpose(ps_x[k][:, t * P:(t + 1) * P], xn[:, t, k * P:(k + 1) * P], c["ident"][:, :])
                last.then_inc(s["turned"], 1)

            @block.scalar
            def _(act):
                act.wait_ge(s["turned"], 1)
                for k in range(KD):
                    nc.scalar.copy(xT[:, k, :], ps_x[k][:, :]).then_inc(s["xT_out"], 1)

            @block.vector
            def _(dve):
                dve.wait_ge(s["x_in"], 16)
                dve.wait_ge(s["rows"], 16 * R)
                for j in range(TOP0):
                    for t in range(NT):
                        r = t * TOP0 + j
                        last = nc.vector.scalar_tensor_tensor(out=x4[:, t, :], in0=rows[:, r, :], scalar=share[:, r:r + 1],
                                                              in1=x4[:, t, :], op0=ALU.mult, op1=ALU.add)
                    nc.vector.drain() if j < TOP0 - 1 else last.then_inc(s["added"], 1)
                nc.vector.drain()
                layer_norm(nc, x4, *nb, xn, 1e-5).then_inc(s["normed"], 1)


def attention_stage(nc, c, io, d):
    GROUPS = 6
    LOADS = 5
    LAG_T = 3
    LAG_V = 5
    LAG_N = 6
    with ExitStack() as ctx:
        st = Store(nc, ctx, "a1")
        s = st.sems("in0 in1 group grouped scores maxed exped turned evac_d evac_a pv o_copied spread "
                    "recip_mm normed saved0 saved1 next_in "
                    "x1_in rows added ln ln_turned ln_out x2_saved xT_saved split stack0 stack1")
        cells = st.sb("cells", [P, 1])
        W = 4 * DH1
        x = [st.sb(f"x{i}", [P, KD, S]) for i in range(2)]
        y = [st.sb(f"y{i}", [P, KD, S]) for i in range(2)]
        wq, wk, wv = ([st.sb(f"{n}{i}", [P, KD, W]) for i in range(2)] for n in ("wq", "wk", "wv"))
        whole, rest = [st.sb(f"whole{i}", [P, S]) for i in range(2)], st.sb("rest", [P, S])
        parts = [st.sb(f"parts{g}", [P, 3, S], BF16) for g in range(4)]
        qs = [st.sb(f"qs{i}", [P, 3, 4, S], BF16) for i in range(2)]
        ks = [st.sb(f"ks{i}", [P, 2, 4, S], BF16) for i in range(2)]
        K_TILE = (0, 1, 0)
        STACKS = 20
        v = [st.sb(f"v{i}", [P, NT, W]) for i in range(2)]
        prob = [st.sb(f"prob{i}", [P, S]) for i in range(DEEP)]
        nmax, total = st.sb("nmax", [P, BODY]), st.sb("total", [P, BODY])
        recip, spread = st.sb("recip", [P, NU]), st.sb("spread", [P, 2, NT, 2, DH1])
        pT = [st.sb(f"pT{i}", [P, NT, S]) for i in range(4)]
        o_sb = [st.sb(f"o_sb{i}", [P, S]) for i in range(2)]
        o_n = [st.sb(f"o_n{i}", [P, 2, S]) for i in range(2)]
        ps_s = [st.ps(f"s{i}") for i in range(2)]
        ps_t = [st.ps(f"t{i}") for i in range(2)]
        ps_o = [st.ps(f"o{i}") for i in range(2)]
        ps_r = st.ps("r")
        ps_p = st.ps("p")
        s_in, s_saved, s_stack = (s["in0"], s["in1"]), (s["saved0"], s["saved1"]), (s["stack0"], s["stack1"])
        PAIR = 2 * NT
        R = NT * TOP0
        rows, idx, share = st.sb("rows", [P, R, D]), st.sb("idx", [P, R], U32), st.sb("share", [P, R])
        x2, xn, xT = c["mask"][:, :, 0:D], c["mask"][:, :, D:2 * D], c["pad"][:, 0:KD, :]
        carry = st.sb("carry", [P, B])
        nb = norm_buffers(st)
        ADD_AT, LN_AT = 9, 18

        def group_of(step):
            w = step % NU - 3
            return w // 2 if 0 <= w < 2 * GROUPS and w % 2 == 0 else None

        with nc.Block() as block:
            @block.sync
            def _(sp):
                def load(b, quad):
                    par = quad % 2
                    cols = slice(quad * W, (quad + 1) * W)
                    sp.wait_ge(s["group"], (b * QUADS + quad) * GROUPS + GROUPS)
                    sp.dma_start(x[par][:, :, :], at(d["xT2"], b).rearrange("(k p) s -> p k s", p=P)).then_inc(s_in[par], 16)
                    sp.dma_start(y[par][:, :, :], at(d["ctxT"], b).rearrange("(k p) s -> p k s", p=P)).then_inc(s_in[par], 16)
                    for dst, src in ((wq, io["L1_xattn_w_q"]), (wk, io["L1_xattn_w_k"]), (wv, io["L1_xattn_w_v"])):
                        sp.dma_start(dst[par][:, :, :], src[:, cols].rearrange("(k p) f -> p k f", p=P)).then_inc(s_in[par], 16)

                def save(n, par):
                    sp.wait_ge(s["normed"], n * 2 + 2 + 1)
                    sp.dma_start(at(d["o1"].rearrange("b q p s -> (b q) p s"), n).rearrange("(a p) s -> p a s", p=P),
                                 o_n[par][:, :, :]).then_inc(s_saved[par], 16)

                def stack(n, par):
                    for g in range(4):
                        sp.wait_ge(s["split"], n * 4 + g + 1)
                        for h in range(2):
                            head, rows_in = g // 2 * 2 + h, slice(h * DH1, (h + 1) * DH1)
                            if g % 2 == 0:
                                moves = ((qs[par][0:DH1, :, head, :], parts[g][rows_in, :, :]),
                                         (qs[par][DH1:P, 0, head, :], parts[g][rows_in, 0, :]),
                                         (qs[par][DH1:P, 1:3, head, :], parts[g][rows_in, 0:2, :]))
                            else:
                                moves = ((ks[par][0:DH1, :, head, :], parts[g][rows_in, 0:1, :].to_broadcast([DH1, 2, S])),
                                         (ks[par][DH1:P, :, head, :], parts[g][rows_in, 1:3, :]))
                            for dst, src in moves:
                                sp.dma_start(dst, src).then_inc(s_stack[par], 16)

                def load_next(b):
                    if not (isinstance(b, int) and b == 0):
                        sp.wait_ge(s["x2_saved"], b * 16)
                        sp.wait_ge(s["xT_saved"], b * 16)
                    sp.dma_start(x2[:, :, :], at(d["x1"], b + 1).rearrange("(t p) f -> p t f", p=P)).then_inc(s["x1_in"], 16)

                def save_next(b):
                    sp.wait_ge(s["added"], b + 1 + 1)
                    sp.dma_start(at(d["x2"], b + 1).rearrange("(t p) f -> p t f", p=P), x2[:, :, :]).then_inc(s["x2_saved"], 16)
                    sp.wait_ge(s["ln_out"], KD * b + KD)
                    sp.dma_start(at(d["xT2"], b + 1).rearrange("(k p) s -> p k s", p=P), xT[:, :, :]).then_inc(s["xT_saved"], 16)

                sp.sem_inc(s["saved0"], 16)
                sp.sem_inc(s["saved1"], 16)
                load_next(0)
                load(0, 0)
                load(0, 1)
                stack(0, 0)
                for quad in range(1, QUADS):
                    if quad >= 2:
                        load(0, quad)
                    if quad == 1:
                        sp.dma_start(c["wo1"][:, :, :], io["L1_xattn_w_o"].rearrange("(k p) f -> p k f", p=P)).then_inc(s["next_in"], 16)
                    if quad >= 2:
                        save(quad - 2, quad % 2)
                    if quad == 3:
                        save_next(0)
                    stack(quad, quad % 2)
                with sp.Fori(1, B - 1) as b:
                    load_next(b)
                    for quad in range(QUADS):
                        load(b, quad)
                        save(b * QUADS + quad - 2, quad % 2)
                        if quad == 3:
                            save_next(b)
                        stack(b * QUADS + quad, quad % 2)
                sp.wait_ge(s["x2_saved"], (B - 1) * 16)
                sp.wait_ge(s["xT_saved"], (B - 1) * 16)
                for quad in range(QUADS):
                    load(B - 1, quad)
                    save((B - 1) * QUADS + quad - 2, quad % 2)
                    stack((B - 1) * QUADS + quad, quad % 2)
                save(ITEMS - 2, 0)
                save(ITEMS - 1, 1)
                sp.wait_ge(s["next_in"], 16)
                for par in range(2):
                    sp.wait_ge(s_saved[par], 16 * (ITEMS // 2) + 16)

            @block.gpsimd
            def _(pool):
                with pool.Fori(0, B - 1) as b:
                    pool.wait_ge(s["added"], b + 1)
                    nc.gpsimd.tensor_tensor(carry[:, bass.ds(b, 1)], c["ones"][:, 0:1], c["ones"][:, 0:1], ALU.mult)
                    nc.gpsimd.tensor_copy(idx[:, :], c["slots0"][:, bass.ds(b + 1, 1), :].rearrange("p a r -> p (a r)"))
                    nc.gpsimd.drain()
                    for r in range(R):
                        nc.gpsimd.indirect_dma_start(out=rows[:, r, :], out_offset=None, in_=d["y0"],
                                                     in_offset=bass.IndirectOffsetOnAxis(ap=idx[:, r:r + 1], axis=0),
                                                     ).then_inc(s["rows"], 16)

            @block.tensor
            def _(pe):
                pe.sem_inc(s["turned"], DEEP)
                pe.sem_inc(s["pv"], 2)
                pe.sem_inc(s["group"], 2 * GROUPS)
                pe.sem_inc(s["recip_mm"], 2)

                def project(body, par, g):
                    i0 = body * 2 + par
                    if g == 0:
                        pe.wait_ge(s_in[par], body * (LOADS * 16) + LOADS * 16)
                    pe.wait_ge(s["grouped"], i0 * GROUPS + g + 1)
                    if g < 4:
                        wt, src = ((wq, x), (wk, y))[g % 2]
                        for k in range(KD):
                            last = nc.tensor.matmul(ps_p[:, :], wt[par][:, k, g // 2 * P:(g // 2 + 1) * P], src[par][:, k, :],
                                                    start=k == 0, stop=k == KD - 1)
                    else:
                        for t in range(2):
                            tile = (g - 4) * 2 + t
                            for k in range(KD):
                                last = nc.tensor.matmul(ps_p[:, t * W:(t + 1) * W], y[par][:, k, tile * P:(tile + 1) * P],
                                                        wv[par][:, k, :], start=k == 0, stop=k == KD - 1)
                    last.then_inc(s["group"], 1)

                def turn_next(b, k):
                    if k == 0:
                        pe.wait_ge(s["ln"], b + 1)
                        pe.wait_ge(s["grouped"], b * (QUADS * GROUPS) + 3 * GROUPS + 1)
                    else:
                        pe.wait_ge(s["ln_out"], KD * b + k)
                    for t in range(NT):
                        op = nc.tensor.transpose(ps_p[:, t * P:(t + 1) * P], xn[:, t, k * P:(k + 1) * P], c["ident"][:, :])
                    op.then_inc(s["ln_turned"], 1)

                def run(body, step, first=False, last=False, final=False, b=None, half=None):
                    now = lagged(body, step, 0, first, last)
                    if now:
                        par, h, t = step // NU, step % NU // NT, step % NT
                        if step % NU == 0:
                            pe.wait_ge(s["grouped"], (body * 2 + par) * GROUPS + GROUPS + 1)
                            pe.wait_ge(s_stack[par], body * (16 * STACKS) + 16 * STACKS)
                        pe.wait_ge(s["exped"], body * BODY + step + 1 + DEEP - 2)
                        for i in range(3):
                            op = nc.tensor.matmul(ps_s[step % 2][:, :], qs[par][:, i, h, t * P:(t + 1) * P], ks[par][:, K_TILE[i], h, :],
                                                  start=i == 0, stop=i == 2)
                        op.then_inc(s["scores"], 1)
                    unit = lagged(body, step, LAG_T, first, last)
                    if unit:
                        ub, w = unit
                        pe.wait_ge(s["exped"], ub * BODY + w + 1 + DEEP)
                        pe.wait_ge((s["evac_d"], s["evac_a"])[w % 2], ub * NU + w // 2 + 1)
                        for k in range(NT):
                            op = nc.tensor.transpose(ps_t[w % 2][:, k * P:(k + 1) * P],
                                                     prob[w % DEEP][:, k * P:(k + 1) * P], c["ident"][:, :])
                        op.then_inc(s["turned"], 1)
                    if (half, step) == (0, BODY - 1):
                        turn_next(b, 0)
                    if (half, step) == (1, 1):
                        turn_next(b, 1)
                    if (half, step) == (1, 3):
                        pe.wait_ge(s["ln_out"], KD * b + KD)
                    if now and group_of(step) is not None and not (final and step >= NU):
                        par = step // NU
                        project(body if par == 0 else body + 1, 1 - par, group_of(step))
                    unit = lagged(body, step, LAG_V, first, last)
                    if unit and unit[1] % PAIR == PAIR - 1:
                        ub, w = unit
                        par, a = w // NU, w // PAIR % 2
                        pe.wait_ge(s["evac_d"], ub * NU + w // 2 + 1 + 1)
                        pe.wait_ge(s["evac_a"], ub * NU + w // 2 + 1 + 1)
                        pe.wait_ge(s["o_copied"], ub * 4 + w // PAIR + 1)
                        for k in range(NT):
                            for h in range(2):
                                head = a * 2 + h
                                op = nc.tensor.matmul(ps_o[a][h * DH1:(h + 1) * DH1, :],
                                                      v[par][:, k, head * DH1:(head + 1) * DH1], pT[head][:, k, :],
                                                      start=k == 0, stop=k == NT - 1)
                        op.then_inc(s["pv"], 1)
                    unit = lagged(body, step, LAG_N, first, last)
                    if unit and unit[1] % PAIR == PAIR - 1:
                        ub, w = unit
                        pe.wait_ge(s["spread"], ub * 4 + w // PAIR + 1)
                        pe.wait_ge(s["normed"], ub * 4 + w // PAIR + 1)
                        for t in range(NT):
                            op = nc.tensor.transpose(ps_r[:, t * P:(t + 1) * P],
                                                     spread[:, w // PAIR % 2, t, :, :].rearrange("p h f -> p (h f)"), c["ident"][:, :])
                        op.then_inc(s["recip_mm"], 1)

                for g in range(GROUPS):
                    project(0, 0, g)
                for step in range(BODY):
                    run(0, step, first=True, b=0, half=0)
                for step in range(BODY):
                    run(1, step, b=0, half=1)
                with pe.Fori(1, B - 1) as b:
                    for half in range(2):
                        for step in range(BODY):
                            run(b * 2 + half, step, b=b, half=half)
                for step in range(BODY):
                    run(BODIES - 2, step)
                for step in range(BODY):
                    run(BODIES - 1, step, final=True)
                for step in range(LAG_N + 1):
                    run(BODIES, step, last=True)

            @block.vector
            def _(dve):
                dve.sem_inc(s["evac_d"], 1)
                dve.sem_inc(s["normed"], 1)
                dve.sem_inc(s["added"], 1)
                def split(body, par, g):
                    dve.wait_ge(s["grouped"], (body * 2 + par) * GROUPS + g + 1 + 1)
                    nc.vector.tensor_tensor(rest[:, :], whole[g % 2][:, :], parts[g][:, 0, :], ALU.subtract)
                    nc.vector.drain()
                    nc.vector.tensor_copy(parts[g][:, 1, :], rest[:, :])
                    nc.vector.drain()
                    nc.vector.tensor_tensor(parts[g][:, 2, :], rest[:, :], parts[g][:, 1, :], ALU.subtract).then_inc(s["split"], 1)
                    nc.vector.drain()

                def next_input(b, step):
                    if step == ADD_AT - 1:
                        dve.wait_ge(s["x1_in"], b * 16 + 16)
                        dve.wait_ge(s["rows"], b * (16 * R) + 16 * R)
                        nc.vector.tensor_copy(share[:, :], c["weights0"][:, bass.ds(b + 1, 1), :].rearrange("p a r -> p (a r)"))
                    elif ADD_AT <= step < ADD_AT + R // 2:
                        if (step - ADD_AT) % 2 == 0:
                            nc.vector.drain()
                        for i in range(2):
                            j, t = divmod((step - ADD_AT) * 2 + i, NT)
                            r = t * TOP0 + j
                            op = nc.vector.scalar_tensor_tensor(out=x2[:, t, :], in0=rows[:, r, :], scalar=share[:, r:r + 1],
                                                                in1=x2[:, t, :], op0=ALU.mult, op1=ALU.add)
                        if step == ADD_AT + R // 2 - 1:
                            op.then_inc(s["added"], 1)
                            nc.vector.drain()
                    elif LN_AT <= step < LN_AT + 8:
                        part = step - LN_AT
                        if part == 6 and not (isinstance(b, int) and b == 0):
                            dve.wait_ge(s["ln_turned"], KD * b)
                            nc.vector.memset(cells[:, 0:1], 0.0)
                        op = layer_norm_part(nc, part, x2, *nb, xn, 1e-5)
                        if part == 7:
                            op.then_inc(s["ln"], 1)

                def next_out(b, k):
                    dve.wait_ge(s["ln_turned"], KD * b + k + 1)
                    if k == 0 and not (isinstance(b, int) and b == 0):
                        dve.wait_ge(s["xT_saved"], 16 * b)
                    nc.vector.tensor_copy(xT[:, k, :], ps_p[:, :]).then_inc(s["ln_out"], 1)

                def run(body, step, first=False, last=False, final=False, b=None, half=None):
                    now = lagged(body, step, 0, first, last)
                    if now:
                        dve.wait_ge(s["scores"], body * BODY + step + 1)
                        nc.vector.tensor_reduce(nmax[:, step:step + 1], ps_s[step % 2][:, :], AX, ALU.max,
                                                negate=True).then_inc(s["maxed"], 1)
                    unit = lagged(body, step, LAG_T, first, last)
                    if unit and unit[1] % 2 == 0:
                        ub, w = unit
                        dve.wait_ge(s["turned"], ub * BODY + w + 1 + DEEP)
                        if w % PAIR == 0:
                            dve.wait_ge(s["pv"], ub * 4 + w // PAIR + 1)
                        nc.vector.tensor_copy(pT[w // NT % 4][:, :, w % NT * P:(w % NT + 1) * P],
                                              ps_t[0][:, :].rearrange("p (k s) -> p k s", k=NT)).then_inc(s["evac_d"], 1)
                    if half == 0:
                        next_input(b, step)
                    if half == 1 and step in (0, 2):
                        next_out(b, step // 2)
                    if now and group_of(step - 3) in (0, 1, 2, 3) and not (final and step >= NU):
                        par = step // NU
                        split(body if par == 0 else body + 1, 1 - par, group_of(step - 3))
                    if unit and unit[1] % PAIR == PAIR - 1:
                        ub, w = unit
                        par, a = w // NU, w // PAIR % 2
                        dve.wait_ge(s["exped"], ub * BODY + w + 1 + DEEP)
                        dve.wait_ge(s["recip_mm"], ub * 4 + w // PAIR + 1)
                        nc.vector.reciprocal(recip[:, a * PAIR:(a + 1) * PAIR], total[:, w + 1 - PAIR:w + 1])
                        nc.vector.drain()
                        nc.vector.tensor_copy(spread[:, a, :, :, :],
                                              recip[:, a * PAIR:(a + 1) * PAIR].rearrange("p (h t o) -> p t h o", h=2, o=1)
                                              .to_broadcast([P, NT, 2, DH1])).then_inc(s["spread"], 1)
                    unit = lagged(body, step, LAG_N + 1, first, last)
                    if unit and unit[1] % PAIR == PAIR - 1:
                        ub, w = unit
                        par, a = w // NU, w // PAIR % 2
                        dve.wait_ge(s["recip_mm"], ub * 4 + w // PAIR + 1 + 2)
                        dve.wait_ge(s["o_copied"], ub * 4 + w // PAIR + 1 + 2)
                        dve.wait_ge(s_saved[par], ub * 16 + 16)
                        nc.vector.tensor_tensor(o_n[par][:, a, :], o_sb[a][:, :], ps_r[:, :], ALU.mult).then_inc(s["normed"], 1)

                for g in range(4):
                    split(0, 0, g)
                for step in range(BODY):
                    run(0, step, first=True, b=0, half=0)
                for step in range(BODY):
                    run(1, step, b=0, half=1)
                with dve.Fori(1, B - 1) as b:
                    for half in range(2):
                        for step in range(BODY):
                            run(b * 2 + half, step, b=b, half=half)
                for step in range(BODY):
                    run(BODIES - 2, step)
                for step in range(BODY):
                    run(BODIES - 1, step, final=True)
                for step in range(LAG_N + 2):
                    run(BODIES, step, last=True)

            @block.scalar
            def _(act):
                act.sem_inc(s["exped"], DEEP)
                act.sem_inc(s["evac_a"], 1)
                act.sem_inc(s["o_copied"], 2)
                act.sem_inc(s["grouped"], 1)

                def group_out(body, par, g):
                    item = body * 2 + par
                    start = isinstance(body, int) and item == 0
                    act.wait_ge(s["group"], item * GROUPS + g + 1 + 2 * GROUPS)
                    if g < 4:
                        if not (start and g < 2):
                            act.wait_ge(s["split"], item * 4 + g - 1)
                        scale = DH1 ** -0.5 if g % 2 == 0 else 1.0
                        nc.scalar.activation(whole[g % 2][:, :], ps_p[:, :], ACT.Copy, scale=scale)
                        if not start:
                            act.wait_ge(s_stack[1 - par], body * (16 * STACKS) + (16 * STACKS if par else 0))
                        op = nc.scalar.activation(parts[g][:, 0, :], ps_p[:, :], ACT.Copy, scale=scale)
                    else:
                        op = nc.scalar.copy(v[par][:, (g - 4) * 2:(g - 4) * 2 + 2, :],
                                            ps_p[:, :].rearrange("p (t f) -> p t f", t=2))
                    op.then_inc(s["grouped"], 1)

                def run(body, step, first=False, last=False, final=False):
                    if lagged(body, step, 0, first, last) and group_of(step - 1) is not None and not (final and step >= NU):
                        par = step // NU
                        group_out(body if par == 0 else body + 1, 1 - par, group_of(step - 1))
                    if lagged(body, step, 0, first, last):
                        act.wait_ge(s["maxed"], body * BODY + step + 1)
                        act.wait_ge(s["turned"], body * BODY + step + 1)
                        nc.scalar.activation(prob[step % DEEP][:, :], ps_s[step % 2][:, :], ACT.Exp, bias=nmax[:, step:step + 1],
                                             accum_out=total[:, step:step + 1]).then_inc(s["exped"], 1)
                    unit = lagged(body, step, LAG_T, first, last)
                    if unit and unit[1] % 2 == 1:
                        ub, w = unit
                        act.wait_ge(s["turned"], ub * BODY + w + 1 + DEEP)
                        if w % PAIR == 1:
                            act.wait_ge(s["pv"], ub * 4 + w // PAIR + 1)
                        nc.scalar.copy(pT[w // NT % 4][:, :, w % NT * P:(w % NT + 1) * P],
                                       ps_t[1][:, :].rearrange("p (k s) -> p k s", k=NT)).then_inc(s["evac_a"], 1)
                    unit = lagged(body, step, LAG_N, first, last)
                    if unit and unit[1] % PAIR == PAIR - 1:
                        ub, w = unit
                        a = w // PAIR % 2
                        act.wait_ge(s["pv"], ub * 4 + w // PAIR + 1 + 2)
                        if not (first and w < PAIR):
                            act.wait_ge(s["normed"], ub * 4 + w // PAIR)
                        nc.scalar.copy(o_sb[a][:, :], ps_o[a][:, :]).then_inc(s["o_copied"], 1)

                for g in range(GROUPS):
                    group_out(0, 0, g)
                for step in range(BODY):
                    run(0, step, first=True)
                with act.Fori(1, BODIES - 1) as body:
                    for step in range(BODY):
                        run(body, step)
                for step in range(BODY):
                    run(BODIES - 1, step, final=True)
                for step in range(LAG_N + 1):
                    run(BODIES, step, last=True)

def route1_stage(nc, c, io, d):
    GC = E1 + 2
    with ExitStack() as ctx:
        st = Store(nc, ctx, "r1")
        s = st.sems("norm_in w_in o_in x_in product summed affine turned xT_out logits maxed exped picked counted placed "
                    "h h_out m m_out scattered slots_free base_saved a_saved slots_saved table_zero")
        KO = HEADS * DH1 // P
        wo = c["wo1"]
        wg = st.sb("wg", [P, KD, GC])
        w1, w2 = st.sb("w1", [P, KD, I1]), st.sb("w2", [P, KI, D])
        b1, b2 = st.sb("b1", [P, KI]), st.sb("b2", [P, D])
        nw, nbias = st.sb("nw", [P, D]), st.sb("nbias", [P, D])
        o4, x4 = st.sb("o4", [P, KO, S]), st.sb("x4", [P, NT, D])
        x3, xn, a = st.sb("x3", [P, NT, D]), st.sb("xn", [P, NT, D]), st.sb("a", [P, NT, D])
        base, mlp = st.sb("base", [P, NT, D]), st.sb("mlp", [P, NT, D])
        xT = st.sb("xT", [P, KD, S])
        hT = st.sb("hT", [P, KI, S])
        mix, nmix, emix, smix = st.sb("mix", [P, NT, 2]), st.sb("nmix", [P, NT]), st.sb("emix", [P, NT, 2]), st.sb("smix", [P, NT])
        nb = norm_buffers(st)
        r = Router(nc, st, c, E1, TOP1, CAP1, drop=True)
        ps_y = [st.ps(f"y{i}") for i in range(2)]
        ps_x = [st.ps(f"x{i}") for i in range(KD)]
        ps_l, ps_p = st.ps("l"), st.ps("p")
        ps_h = [st.ps(f"h{i}") for i in range(2)]
        both = ps_l[:, 0:NT * GC].rearrange("p (t e) -> p t e", t=NT)
        logits, mixes = both[:, :, 0:E1], both[:, :, E1:GC]

        with nc.Block() as block:
            @block.sync
            def _(sp):
                def load(b):
                    sp.dma_start(o4[:, :, :], at(d["o1"].rearrange("b q f s -> b (q f) s"), b).rearrange("(k p) s -> p k s", p=P)).then_inc(s["o_in"], 16)
                    sp.dma_start(x4[:, :, :], at(d["x2"], b).rearrange("(t p) f -> p t f", p=P)).then_inc(s["x_in"], 16)

                def save_a(b):
                    sp.wait_ge(s["affine"], b + 1)
                    sp.dma_start(at(d["a1"].rearrange("(b s) f -> b s f", b=B), b).rearrange("(t p) f -> p t f", p=P), a[:, :, :]).then_inc(s["a_saved"], 16)

                def batch(b, load_next=True, save_next=True):
                    sp.wait_ge(s["placed"], b + 1)
                    sp.dma_start(at(d["slots1"], b), r.slot_read[:, :]).then_inc(s["slots_saved"], 16)
                    sp.dma_start(at(d["weights1"], b), r.weight[:, :]).then_inc(s["slots_saved"], 16)
                    if load_next:
                        sp.wait_ge(s["summed"], b + 2 + 1)
                        load(b + 2)
                    if save_next:
                        save_a(b + 1)
                    sp.wait_ge(s["m_out"], 2 * b + 2 + 2)
                    sp.dma_start(at(d["base"], b).rearrange("(t p) f -> p t f", p=P), base[:, :, :]).then_inc(s["base_saved"], 16)

                sp.sem_inc(s["slots_saved"], 32)
                sp.sem_inc(s["base_saved"], 16)
                load(0)
                for dst, src in ((nw, io["L1_ffn_attn_nw"]), (nbias, io["L1_ffn_attn_nb"])):
                    sp.dma_start(dst[:, :], src.rearrange("(a f) -> a f", a=1).to_broadcast([P, D])).then_inc(s["norm_in"], 16)
                sp.dma_start(w1[:, :, :], io["L1_ffn_res_inter_w"].rearrange("(k p) f -> p k f", p=P)).then_inc(s["w_in"], 16)
                sp.dma_start(w2[:, :, :], io["L1_ffn_res_output_w"].rearrange("(k p) f -> p k f", p=P)).then_inc(s["w_in"], 16)
                sp.dma_start(b2[:, :], io["L1_ffn_res_output_b"].rearrange("(a f) -> a f", a=1).to_broadcast([P, D])).then_inc(s["w_in"], 16)
                with nc.allow_non_contiguous_dma(reason="small columns"):
                    sp.dma_start(b1[:, :], io["L1_ffn_res_inter_b"].rearrange("(k p) -> p k", p=P)).then_inc(s["w_in"], 16)
                    sp.dma_start(wg[:, :, 0:E1], io["L1_ffn_wg"].rearrange("(k p) e -> p k e", p=P)).then_inc(s["w_in"], 16)
                    sp.dma_start(wg[:, :, E1:GC], io["L1_ffn_res_coef"].rearrange("(k p) e -> p k e", p=P)).then_inc(s["w_in"], 16)
                sp.dma_start(d["table1"].rearrange("(p k) o -> p (k o)", p=P), c["zeros"][:, 0:E1 * CAP1 // P].bitcast(U32)).then_inc(s["table_zero"], 16)
                sp.wait_ge(s["summed"], 1 + 1)
                load(1)
                save_a(0)
                with sp.Fori(0, B - 2) as b:
                    batch(b)
                batch(B - 2, load_next=False)
                batch(B - 1, load_next=False, save_next=False)
                sp.wait_ge(s["base_saved"], 16 * B + 16)
                sp.wait_ge(s["a_saved"], 16 * B)
                sp.wait_ge(s["slots_saved"], 32 * B + 32)

            @block.gpsimd
            def _(pool):
                pool.sem_inc(s["slots_free"], 1)
                pool.wait_ge(s["table_zero"], 16)
                with pool.Fori(0, B) as b:
                    pool.wait_ge(s["placed"], b + 1)
                    r.scatter(b, d["table1"], s["scattered"], s["slots_free"])

            @block.tensor
            def _(pe):
                def product(b):
                    pe.wait_ge(s["o_in"], b * 16 + 16)
                    pe.wait_ge(s["summed"], b + 1)
                    for t in range(NT):
                        for k in range(KO):
                            last = nc.tensor.matmul(ps_y[t // 2][:, t % 2 * D:(t % 2 + 1) * D], o4[:, k, t * P:(t + 1) * P],
                                                    wo[:, k, :], start=k == 0, stop=k == KO - 1)
                        if t % 2:
                            last.then_inc(s["product"], 1)

                def batch(b, product_ahead=True):
                    pe.wait_ge(s["affine"], b + 1)
                    pe.wait_ge(s["m_out"], 2 * b + 2)
                    for k in range(KD):
                        for t in range(NT):
                            last = nc.tensor.transpose(ps_x[k][:, t * P:(t + 1) * P], a[:, t, k * P:(k + 1) * P], c["ident"][:, :])
                    last.then_inc(s["turned"], 1)
                    pe.wait_ge(s["xT_out"], KD * b + KD)
                    for t in range(NT):
                        for k in range(KD):
                            last = nc.tensor.matmul(ps_l[:, t * GC:(t + 1) * GC], xT[:, k, t * P:(t + 1) * P], wg[:, k, :],
                                                    start=k == 0, stop=k == KD - 1)
                    last.then_inc(s["logits"], 1)
                    for m in range(KI):
                        pe.wait_ge(s["h_out"], b * KI + m + 1)
                        for k in range(KD):
                            last = nc.tensor.matmul(ps_h[m % 2][:, :], w1[:, k, m * P:(m + 1) * P], xT[:, k, :],
                                                    start=k == 0, stop=k == KD - 1)
                        last.then_inc(s["h"], 1)
                        if m == 0:
                            pe.wait_ge(s["picked"], b + 1)
                            r.count_earlier(ps_p).then_inc(s["counted"], 1)
                    if product_ahead:
                        product(b + 2)
                    pe.wait_ge(s["h_out"], b * KI + KI + 2)
                    for t in range(NT):
                        for m in range(KI):
                            last = nc.tensor.matmul(ps_x[t // 2][:, t % 2 * D:(t % 2 + 1) * D], hT[:, m, t * P:(t + 1) * P],
                                                    w2[:, m, :], start=m == 0, stop=m == KI - 1)
                        if t % 2:
                            last.then_inc(s["m"], 1)

                pe.sem_inc(s["m"], 2)
                product(0)
                product(1)
                pe.wait_ge(s["w_in"], 16 * 6)
                with pe.Fori(0, B - 2) as b:
                    batch(b)
                batch(B - 2, product_ahead=False)
                batch(B - 1, product_ahead=False)

            @block.scalar
            def _(act):
                act.sem_inc(s["h_out"], 2)
                act.wait_ge(s["w_in"], 16 * 6)
                with act.Fori(0, B) as b:
                    act.wait_ge(s["turned"], b + 1)
                    for k in range(KD):
                        nc.scalar.copy(xT[:, k, :], ps_x[k][:, :]).then_inc(s["xT_out"], 1)
                    act.wait_ge(s["maxed"], b + 1)
                    r.exponentials(logits)
                    for t in range(NT):
                        last = nc.scalar.activation(emix[:, t, :], mixes[:, t, :], ACT.Exp, bias=nmix[:, t:t + 1],
                                                    accum_out=smix[:, t:t + 1])
                    last.then_inc(s["exped"], 1)
                    act.wait_ge(s["m"], 2 * b + 2)
                    for m in range(KI):
                        act.wait_ge(s["h"], b * KI + m + 1)
                        nc.scalar.activation(hT[:, m, :], ps_h[m % 2][:, :], ACT.Gelu_apprx_tanh, bias=b1[:, m:m + 1]).then_inc(s["h_out"], 1)

            @block.vector
            def _(dve):
                def norms(b):
                    dve.wait_ge(s["x_in"], b * 16 + 16)
                    for half in range(2):
                        dve.wait_ge(s["product"], 2 * b + half + 1)
                        last = nc.vector.tensor_tensor(x3[:, 2 * half:2 * half + 2, :], x4[:, 2 * half:2 * half + 2, :],
                                                       ps_y[half][:, :].rearrange("p (t f) -> p t f", t=2), ALU.add)
                    last.then_inc(s["summed"], 1)
                    nc.vector.drain()
                    layer_norm(nc, x3, *nb, xn, 1e-5)
                    nc.vector.drain()
                    nc.vector.memset(r.sums[:, :], 0.0)
                    if not (isinstance(b, int) and b == 0):
                        dve.wait_ge(s["turned"], b)
                        dve.wait_ge(s["a_saved"], 16 * b)
                    nc.vector.memset(r.pos[:, :], 0.0)
                    layer_norm(nc, xn, *nb, a, 1e-12)
                    nc.vector.drain()
                    for t in range(NT):
                        nc.vector.tensor_tensor(a[:, t, :], a[:, t, :], nw[:, :], ALU.mult)
                    nc.vector.drain()
                    for t in range(NT):
                        last = nc.vector.tensor_tensor(a[:, t, :], a[:, t, :], nbias[:, :], ALU.add)
                    last.then_inc(s["affine"], 1)

                def batch(b, has_next=True):
                    dve.wait_ge(s["logits"], b + 1)
                    nc.vector.tensor_reduce(r.nmax[:, :], logits, AX, ALU.max, negate=True)
                    nc.vector.tensor_reduce(nmix[:, :], mixes, AX, ALU.max, negate=True).then_inc(s["maxed"], 1)
                    dve.wait_ge(s["exped"], b + 1)
                    nc.vector.reciprocal(smix[:, :], smix[:, :])
                    r.pick().then_inc(s["picked"], 1)
                    nc.vector.tensor_tensor(mix[:, :, :], emix[:, :, :], r.tail(smix[:, :]).to_broadcast([P, NT, 2]), ALU.mult)
                    dve.wait_ge(s["base_saved"], b * 16 + 16)
                    nc.vector.tensor_tensor(base[:, :, :], x3[:, :, :], xn[:, :, :], ALU.add)
                    dve.wait_ge(s["slots_saved"], b * 32 + 32)
                    dve.wait_ge(s["slots_free"], b + 1)
                    dve.wait_ge(s["counted"], b + 1)
                    r.place(ps_p)
                    nc.vector.drain()
                    nc.vector.tensor_tensor(r.weight[:, :], r.weight[:, :], mix[:, :, 1], ALU.mult).then_inc(s["placed"], 1)
                    if has_next:
                        norms(b + 1)
                    for half in range(2):
                        dve.wait_ge(s["m"], 2 * b + half + 1 + 2)
                        rows = slice(2 * half, 2 * half + 2)
                        nc.vector.tensor_tensor(mlp[:, rows, :], ps_x[half][:, :].rearrange("p (t f) -> p t f", t=2),
                                                b2[:, :].rearrange("p (o f) -> p o f", o=1).to_broadcast([P, 2, D]), ALU.add)
                        nc.vector.drain()
                        for t in range(2 * half, 2 * half + 2):
                            last = nc.vector.scalar_tensor_tensor(out=base[:, t, :], in0=mlp[:, t, :], scalar=mix[:, t, 0:1],
                                                                  in1=base[:, t, :], op0=ALU.mult, op1=ALU.add)
                        last.then_inc(s["m_out"], 1)

                dve.sem_inc(s["summed"], 1)
                dve.sem_inc(s["m_out"], 2)
                r.start()
                dve.wait_ge(s["norm_in"], 32)
                norms(0)
                dve.wait_ge(s["w_in"], 16 * 6)
                with dve.Fori(0, B - 1) as b:
                    batch(b)
                batch(B - 1, has_next=False)


def experts1_stage(nc, c, io, d, out):
    HALVES = CAP1 // P
    with ExitStack() as ctx:
        st = Store(nc, ctx, "e1")
        s = st.sems("idx_in w10 w11 w20 w21 b_in rows0 rows1 turned xT_out h h_out y y_out saved0 saved1 "
                    "stored x_in slots_in added out_saved " + " ".join(f"taken{b}" for b in range(B)))
        R = NT * TOP1
        slots, weight = st.sb("slots", [P, B, R], U32), st.sb("weight", [P, B, R])
        x = st.sb("x", [P, B, NT, D])
        taken = st.sb("taken", [P, B, R, D])
        idx = st.sb("idx", [P, E1, HALVES], U32)
        b1, b2 = st.sb("b1", [P, E1, KI]), st.sb("b2", [P, E1, D])
        rows = [st.sb(f"rows{i}", [P, HALVES, D]) for i in range(2)]
        xT = [st.sb(f"xT{i}", [P, KD, CAP1]) for i in range(2)]
        w1 = [st.sb(f"w1{i}", [P, KD, I1]) for i in range(2)]
        w2 = [st.sb(f"w2{i}", [P, KI, D]) for i in range(2)]
        hT = [st.sb(f"hT{i}", [P, KI, CAP1]) for i in range(2)]
        y = [st.sb(f"y{i}", [P, HALVES, D]) for i in range(2)]
        ps_x = [st.ps(f"x{i}") for i in range(2)]
        ps_h = [st.ps(f"h{i}") for i in range(4)]
        ps_y = [st.ps(f"y{i}") for i in range(2)]
        s_w1, s_w2, s_rows, s_saved = (s["w10"], s["w11"]), (s["w20"], s["w21"]), (s["rows0"], s["rows1"]), (s["saved0"], s["saved1"])
        y_out = d["y1"].rearrange("(e h p) f -> e p h f", p=P, h=HALVES)

        with nc.Block() as block:
            @block.sync
            def _(sp):
                with nc.allow_non_contiguous_dma(reason="token numbers and biases"):
                    sp.dma_start(idx[:, :, :].rearrange("p e h -> p (e h)"), d["table1"].rearrange("(e p) o -> p (e o)", p=P)).then_inc(s["idx_in"], 16)
                    for e in range(E1):
                        sp.dma_start(b1[:, e, :], io["L1_ffn_inter_b"][e].rearrange("(k p) -> p k", p=P)).then_inc(s["b_in"], 16)
                for e in range(E1):
                    sp.dma_start(b2[:, e, :], io["L1_ffn_output_b"][e:e + 1, :].to_broadcast([P, D])).then_inc(s["b_in"], 16)
                for e in range(E1):
                    par = e % 2
                    if e >= 2:
                        sp.wait_ge(s["y"], e - 1)
                    sp.dma_start(w1[par][:, :, :], io["L1_ffn_inter_w"][e].rearrange("(k p) f -> p k f", p=P)).then_inc(s_w1[par], 16)
                    sp.dma_start(w2[par][:, :, :], io["L1_ffn_output_w"][e].rearrange("(k p) f -> p k f", p=P)).then_inc(s_w2[par], 16)
                sp.dma_start(slots[:, :, :], d["slots1"].rearrange("b p r -> p b r")).then_inc(s["slots_in"], 16)
                sp.dma_start(weight[:, :, :], d["weights1"].rearrange("b p r -> p b r")).then_inc(s["slots_in"], 16)
                sp.dma_start(x[:, :, :, :].rearrange("p b t f -> p (b t) f"), d["base"].rearrange("b (t p) f -> p (b t) f", p=P)).then_inc(s["x_in"], 16)
                for b in range(B):
                    sp.wait_ge(s["added"], NT * (b + 1))
                    sp.dma_start(out[b].rearrange("(t p) f -> p t f", p=P), x[:, b]).then_inc(s["out_saved"], 16)
                sp.wait_ge(s["out_saved"], 16 * B)

            @block.gpsimd
            def _(pool):
                pool.wait_ge(s["idx_in"], 16)
                for e in range(E1):
                    if e >= 2:
                        pool.wait_ge(s["turned"], e - 1)
                    for h in range(HALVES):
                        nc.gpsimd.indirect_dma_start(out=rows[e % 2][:, h, :], out_offset=None, in_=d["a1"],
                                                     in_offset=bass.IndirectOffsetOnAxis(ap=idx[:, e, h:h + 1], axis=0),
                                                     ).then_inc(s_rows[e % 2], 16)
                pool.wait_ge(s["slots_in"], 32)
                pool.wait_ge(s["stored"], 1)
                for b in range(B):
                    for r in range(R):
                        nc.gpsimd.indirect_dma_start(out=taken[:, b, r, :], out_offset=None, in_=d["y1"],
                                                     in_offset=bass.IndirectOffsetOnAxis(ap=slots[:, b, r:r + 1], axis=0),
                                                     ).then_inc(s[f"taken{b}"], 16)

            @block.tensor
            def _(pe):
                def turn(e):
                    pe.wait_ge(s_rows[e % 2], 16 * HALVES * (e // 2 + 1))
                    if e >= 2:
                        pe.wait_ge(s["xT_out"], e - 1)
                    for k in range(KD):
                        for h in range(HALVES):
                            last = nc.tensor.transpose(ps_x[e % 2][:, k * CAP1 + h * P:k * CAP1 + (h + 1) * P],
                                                       rows[e % 2][:, h, k * P:(k + 1) * P], c["ident"][:, :])
                    last.then_inc(s["turned"], 1)

                turn(0)
                for e in range(E1):
                    par = e % 2
                    pe.wait_ge(s_w1[par], 16 * (e // 2 + 1))
                    pe.wait_ge(s["xT_out"], e + 1)
                    for m in range(KI):
                        if m % 2 == 0 and e >= 1:
                            pe.wait_ge(s["h_out"], (e - 1) * KI + m + 2)
                        for k in range(KD):
                            last = nc.tensor.matmul(ps_h[m // 2][:, m % 2 * CAP1:(m % 2 + 1) * CAP1], w1[par][:, k, m * P:(m + 1) * P],
                                                    xT[par][:, k, :], start=k == 0, stop=k == KD - 1)
                        if m % 2:
                            last.then_inc(s["h"], 1)
                    if e + 1 < E1:
                        turn(e + 1)
                    pe.wait_ge(s_w2[par], 16 * (e // 2 + 1))
                    if e >= 2:
                        pe.wait_ge(s["y_out"], e - 1)
                    pe.wait_ge(s["h_out"], (e + 1) * KI)
                    for h in range(HALVES):
                        for m in range(KI):
                            last = nc.tensor.matmul(ps_y[par][:, h * D:(h + 1) * D], hT[par][:, m, h * P:(h + 1) * P], w2[par][:, m, :],
                                                    start=m == 0, stop=m == KI - 1)
                    last.then_inc(s["y"], 1)

            @block.scalar
            def _(act):
                act.wait_ge(s["b_in"], 16 * 2 * E1)
                for e in range(E1):
                    par = e % 2
                    if e >= 2:
                        act.wait_ge(s["y"], e - 1)
                    for m in range(KI):
                        if m % 2 == 0:
                            act.wait_ge(s["h"], e * (KI // 2) + m // 2 + 1)
                        nc.scalar.activation(hT[par][:, m, :], ps_h[m // 2][:, m % 2 * CAP1:(m % 2 + 1) * CAP1],
                                             ACT.Gelu_apprx_tanh, bias=b1[:, e, m:m + 1]).then_inc(s["h_out"], 1)
                    if e >= 1:
                        act.wait_ge(s["y_out"], e)
                        act.dma_start(y_out[e - 1], y[1 - par][:, :, :]).then_inc(s_saved[1 - par], 16)
                act.wait_ge(s["y_out"], E1)
                act.dma_start(y_out[E1 - 1], y[1][:, :, :]).then_inc(s["saved1"], 16)
                act.wait_ge(s["saved0"], 16 * E1 // 2)
                act.wait_ge(s["saved1"], 16 * E1 // 2)
                act.sem_inc(s["stored"], 1)

            @block.vector
            def _(dve):
                dve.wait_ge(s["b_in"], 16 * 2 * E1)

                def xT_copy(e):
                    dve.wait_ge(s["turned"], e + 1)
                    if e >= 2:
                        dve.wait_ge(s["h"], (e - 1) * (KI // 2))
                    nc.vector.tensor_copy(xT[e % 2][:, :, :], ps_x[e % 2][:, :].rearrange("p (k s) -> p k s", k=KD)).then_inc(s["xT_out"], 1)

                xT_copy(0)
                for e in range(E1):
                    if e + 1 < E1:
                        xT_copy(e + 1)
                    dve.wait_ge(s["y"], e + 1)
                    if e >= 2:
                        dve.wait_ge(s_saved[e % 2], 16 * (e // 2))
                    nc.vector.tensor_tensor(y[e % 2][:, :, :], ps_y[e % 2][:, :].rearrange("p (h f) -> p h f", h=HALVES),
                                            b2[:, e:e + 1, :].to_broadcast([P, HALVES, D]), ALU.add).then_inc(s["y_out"], 1)
                dve.wait_ge(s["x_in"], 16)
                dve.wait_ge(s["slots_in"], 32)
                for b in range(B):
                    dve.wait_ge(s[f"taken{b}"], 16 * R)
                    for t in range(NT):
                        nc.vector.scalar_tensor_tensor(out=x[:, b, t, :], in0=taken[:, b, t, :], scalar=weight[:, b, t:t + 1],
                                                       in1=x[:, b, t, :], op0=ALU.mult, op1=ALU.add).then_inc(s["added"], 1)


def build(nc, io, out):
    def scratch(name, shape, dt=F32):
        return nc.dram_tensor(f"scratch_{name}", shape, dt, kind="Internal").ap()

    d = dict(
        ctxT=scratch("ctxT", (B, D, S)),
        qp=scratch("qp", (B, 3, D, S), BF16),
        kp=scratch("kp", (B, 3, D, S), BF16),
        v0=scratch("v0", (B, QUADS, S, 4 * PAD0)),
        o0=scratch("o0", (ITEMS, P, S)),
        x1=scratch("x1", (B, S, D)), xn1=scratch("xn1", (N, D)),
        slots0=scratch("slots0", (B, P, NT * TOP0), U32), weights0=scratch("weights0", (B, P, NT * TOP0)),
        table0=scratch("table0", (E0 * CAP0, 1), U32), y0=scratch("y0", (E0 * CAP0, D)),
        o1=scratch("o1", (B, QUADS, 4 * DH1, S)), a1=scratch("a1", (N, D)), base=scratch("base", (B, S, D)),
        slots1=scratch("slots1", (B, P, NT * TOP1), U32), weights1=scratch("weights1", (B, P, NT * TOP1)),
        table1=scratch("table1", (E1 * CAP1, 1), U32), y1=scratch("y1", (E1 * CAP1, D)),
        x2=scratch("x2", (B, S, D)), xT2=scratch("xT2", (B, D, S)),
    )
    with ExitStack() as ctx:
        st = Store(nc, ctx, "c")
        c = dict(
            ones=st.sb("ones", [P, P]), zeros=st.sb("zeros", [P, P]), ident=st.sb("ident", [P, P]),
            ones16=st.sb("ones16", [P, P], BF16), before=st.sb("before", [P, P], BF16),
            mask=st.sb("mask", [P, NT, S]), maskb=st.sb("maskb", [P, NT, S]), pad=st.sb("pad", [P, B, S]),
            wo0=st.sb("wo0", [P, QUADS, D]), wr0=st.sb("wr0", [P, KD, E0]), bo0=st.sb("bo0", [P, D]),
            slots0=st.sb("slots0", [P, B, NT * TOP0], U32), weights0=st.sb("weights0", [P, B, NT * TOP0]),
            wo1=st.sb("wo1", [P, HEADS * DH1 // P, D]),
            expert_no=st.sb("expert_no", [P, E0]), token_no=st.sb("token_no", [P, NT]))
        build_constants(nc, c)
        with nc.cleanup_on_exit():
            for stage in (project_stage, masked_attention_stage, route0_stage, experts0_stage, combine0_stage):
                stage(nc, c, io, d)
        attention_stage(nc, c, io, d)
        route1_stage(nc, c, io, d)
        experts1_stage(nc, c, io, d, out)


_OUT_SHAPE = (B, S, D)


def kernel(**inputs):
    import numpy as np
    import concourse.bacc as bacc
    from concourse.bass_utils import run_bass_kernel_spmd

    nc = bacc.Bacc("TRN2", target_bir_lowering=False, num_devices=1)
    arrays = {f"in_{name}": np.ascontiguousarray(a) for name, a in inputs.items()}
    io = {
        name: nc.dram_tensor(f"in_{name}", inputs[name].shape, mybir.dt.from_np(arrays[f"in_{name}"].dtype),
                             kind="ExternalInput").ap() for name in inputs}
    out = nc.dram_tensor("out_0", _OUT_SHAPE, F32, kind="ExternalOutput").ap()
    build(nc, io, out)
    return run_bass_kernel_spmd(nc, [arrays], core_ids=[0]).results[0]["out_0"]
```
